# Optimizing a Trainium2 kernel written in Bass

```python
import numpy as np
import jax
import jax.numpy as jnp

def _softmax(x, axis=-1):
    return jax.nn.softmax(x, axis=axis)

def _gelu(x):
    return jax.nn.gelu(x, approximate=True)

def _silu(x):
    return jax.nn.silu(x)

def _sigmoid(x):
    return jax.nn.sigmoid(x)

def _layernorm(x, axis=-1, eps=1e-05):
    m = jnp.mean(x, axis=axis, keepdims=True)
    v = jnp.var(x, axis=axis, keepdims=True)
    return (x - m) / jnp.sqrt(v + eps)

def _scatter_add(tgt, idx, src, axis=0):
    return tgt.at[idx].add(src)

def _segment_sum(src, seg, n):
    return jax.ops.segment_sum(src, seg, n)
kernel_name = 'mk_sandwich_d2_jaxref_r8_afba7b'

def setup_inputs(seed: int=0):
    np.random.seed(seed)
    _w = jnp.asarray

    def _L0_attn_setup():
        import jax, jax.numpy as jnp
        import numpy as np
        MAX_DIST = 8
        GUIDANCE_WEIGHT = 0.4
        EPS_MAG = 1e-06
        EPS_COS = 1e-08
        EPS_WSUM = 1e-08
        key = jax.random.key(seed)
        k1, k2 = jax.random.split(key)
        embeddings = jax.random.normal(k1, (4, 256, 128), dtype=jnp.float32)
        guidance_trajectories = jax.random.normal(k2, (64, 128), dtype=jnp.float32)
        return {'embeddings': embeddings, 'guidance_trajectories': guidance_trajectories}
    _L0_attn_in = _L0_attn_setup()

    def _L0_ffn_setup():
        import jax, jax.numpy as jnp
        import numpy as np
        TOP_K = 2
        key = jax.random.key(seed)
        ks = jax.random.split(key, 5)
        B, S, D, E = (4, 256, 128, 8)
        H = 4 * D
        scale = 0.02
        return {'x': jax.random.normal(ks[0], (B, S, D), dtype=jnp.float32), 'gate_w': jax.random.normal(ks[1], (E, D), dtype=jnp.float32) * scale, 'gate_b': jnp.zeros((E,), dtype=jnp.float32), 'w1': jax.random.normal(ks[2], (E, H, D), dtype=jnp.float32) * scale, 'b1': jnp.zeros((E, H), dtype=jnp.float32), 'w2': jax.random.normal(ks[3], (E, D, H), dtype=jnp.float32) * scale, 'b2': jnp.zeros((E, D), dtype=jnp.float32)}
    _L0_ffn_in = _L0_ffn_setup()

    def _L1_attn_setup():
        import jax, jax.numpy as jnp
        import numpy as np
        import math
        DIM = 128
        DIM_HEAD = 64
        HEADS = 16
        B, N = (2, 256)

        def _layernorm(x, g, b, eps=1e-05):
            x32 = x.astype(jnp.float32)
            mu = jnp.mean(x32, axis=-1, keepdims=True)
            var = jnp.var(x32, axis=-1, keepdims=True)
            return ((x32 - mu) * jax.lax.rsqrt(var + eps) * g + b).astype(x.dtype)
        key = jax.random.key(seed)
        ks = jax.random.split(key, 8)
        inner = DIM_HEAD * HEADS
        return {'x': jax.random.normal(ks[0], (B, N, DIM), dtype=jnp.float32), 'w_q': jax.random.normal(ks[1], (inner, DIM), dtype=jnp.float32) * 0.02, 'w_kv': jax.random.normal(ks[2], (2 * DIM_HEAD, DIM), dtype=jnp.float32) * 0.02, 'w_out': jax.random.normal(ks[3], (DIM, inner), dtype=jnp.float32) * 0.02, 'ln_g': jnp.ones((DIM,), dtype=jnp.float32), 'ln_b': jnp.zeros((DIM,), dtype=jnp.float32), 'lno_g': jnp.ones((DIM,), dtype=jnp.float32), 'lno_b': jnp.zeros((DIM,), dtype=jnp.float32)}
    _L1_attn_in = _L1_attn_setup()

    def _L1_ffn_setup():
        import jax, jax.numpy as jnp
        import numpy as np
        D_IN, D_HID = (128, 512)

        def _ternary(key, shape):
            return jax.random.randint(key, shape, -1, 2).astype(jnp.float32)

        def _tlin(x, w, s):
            return jnp.einsum('bsi,oi->bso', x, w) * s
        key = jax.random.key(seed)
        ks = jax.random.split(key, 12)
        inv = lambda fan: 1.0 / np.sqrt(fan).astype(np.float32)
        return {'x': jax.random.normal(ks[0], (4, 256, D_IN), dtype=jnp.float32), 'w1_w': _ternary(ks[1], (D_HID, D_IN)), 'w1_s': jax.random.uniform(ks[2], (D_HID,), dtype=jnp.float32) * inv(D_IN), 'w2_w': _ternary(ks[3], (D_HID, D_IN)), 'w2_s': jax.random.uniform(ks[4], (D_HID,), dtype=jnp.float32) * inv(D_IN), 'h1_w': _ternary(ks[5], (D_HID, D_HID)), 'h1_s': jax.random.uniform(ks[6], (D_HID,), dtype=jnp.float32) * inv(D_HID), 'h2_w': _ternary(ks[7], (D_HID, D_HID)), 'h2_s': jax.random.uniform(ks[8], (D_HID,), dtype=jnp.float32) * inv(D_HID), 'w3_w': _ternary(ks[9], (D_IN, D_HID)), 'w3_s': jax.random.uniform(ks[10], (D_IN,), dtype=jnp.float32) * inv(D_HID)}
    _L1_ffn_in = _L1_ffn_setup()
    _d = {'L0_attn_embeddings': _L0_attn_in['embeddings'], 'L0_attn_guidance_trajectories': _L0_attn_in['guidance_trajectories'], 'L0_ffn_gate_w': _L0_ffn_in['gate_w'], 'L0_ffn_gate_b': _L0_ffn_in['gate_b'], 'L0_ffn_w1': _L0_ffn_in['w1'], 'L0_ffn_b1': _L0_ffn_in['b1'], 'L0_ffn_w2': _L0_ffn_in['w2'], 'L0_ffn_b2': _L0_ffn_in['b2'], 'L1_attn_w_q': _L1_attn_in['w_q'], 'L1_attn_w_kv': _L1_attn_in['w_kv'], 'L1_attn_w_out': _L1_attn_in['w_out'], 'L1_attn_ln_g': _L1_attn_in['ln_g'], 'L1_attn_ln_b': _L1_attn_in['ln_b'], 'L1_attn_lno_g': _L1_attn_in['lno_g'], 'L1_attn_lno_b': _L1_attn_in['lno_b'], 'L1_ffn_w1_w': _L1_ffn_in['w1_w'], 'L1_ffn_w1_s': _L1_ffn_in['w1_s'], 'L1_ffn_w2_w': _L1_ffn_in['w2_w'], 'L1_ffn_w2_s': _L1_ffn_in['w2_s'], 'L1_ffn_h1_w': _L1_ffn_in['h1_w'], 'L1_ffn_h1_s': _L1_ffn_in['h1_s'], 'L1_ffn_h2_w': _L1_ffn_in['h2_w'], 'L1_ffn_h2_s': _L1_ffn_in['h2_s'], 'L1_ffn_w3_w': _L1_ffn_in['w3_w'], 'L1_ffn_w3_s': _L1_ffn_in['w3_s']}
    _x0 = _d['L0_attn_embeddings']
    _d['L0_attn_embeddings'] = jax.random.normal(jax.random.fold_in(jax.random.key(seed), 1), (16, 256, 128), dtype=_x0.dtype)
    del _x0
    return _d

def reference(L0_attn_embeddings, L0_attn_guidance_trajectories, L0_ffn_gate_w, L0_ffn_gate_b, L0_ffn_w1, L0_ffn_b1, L0_ffn_w2, L0_ffn_b2, L1_attn_w_q, L1_attn_w_kv, L1_attn_w_out, L1_attn_ln_g, L1_attn_ln_b, L1_attn_lno_g, L1_attn_lno_b, L1_ffn_w1_w, L1_ffn_w1_s, L1_ffn_w2_w, L1_ffn_w2_s, L1_ffn_h1_w, L1_ffn_h1_s, L1_ffn_h2_w, L1_ffn_h2_s, L1_ffn_w3_w, L1_ffn_w3_s):

    def _L0_attn_ref(embeddings, guidance_trajectories):
        import jax, jax.numpy as jnp
        import numpy as np
        MAX_DIST = 8
        GUIDANCE_WEIGHT = 0.4
        EPS_MAG = 1e-06
        EPS_COS = 1e-08
        EPS_WSUM = 1e-08
        B, S, D = embeddings.shape
        W = min(MAX_DIST, S - 1)
        diffs = embeddings[:, 1:, :] - embeddings[:, :-1, :]
        pos = jnp.arange(S)[:, None]
        k = jnp.arange(W)[None, :]
        idx = pos - W + k
        valid = (idx >= 0) & (pos >= 1)
        windows = diffs[:, jnp.clip(idx, 0, S - 2), :]
        w = jnp.minimum(pos, W)
        j = k - (W - w)
        lin = jnp.where(w > 1, 0.1 + 0.9 * j / jnp.maximum(w - 1, 1), 0.1)
        pos_weights = jnp.where(valid, lin, 0.0).astype(embeddings.dtype)
        mag = jnp.linalg.norm(windows, axis=-1, keepdims=True)
        is_valid_mag = mag > EPS_MAG
        normed = jnp.where(is_valid_mag, windows / jnp.where(is_valid_mag, mag, 1.0), 0.0)
        mag_weights = jnp.tanh(mag * 2.0)
        combined = pos_weights[None, :, :, None] * mag_weights
        g_norm = jnp.linalg.norm(guidance_trajectories, axis=-1)
        a_norm = jnp.linalg.norm(normed, axis=-1)
        dots = jnp.einsum('bswd,gd->bswg', normed, guidance_trajectories)
        sims = dots / (jnp.maximum(a_norm, EPS_COS)[..., None] * jnp.maximum(g_norm, EPS_COS))
        g_weights = jax.nn.softmax(sims * 2.0, axis=-1)
        influence = jnp.einsum('bswg,gd->bswd', g_weights, guidance_trajectories)
        blended = (1.0 - GUIDANCE_WEIGHT) * normed + GUIDANCE_WEIGHT * influence
        weight_sum = jnp.maximum(combined.sum(axis=2), EPS_WSUM)
        trajectories = (blended * combined).sum(axis=2) / weight_sum
        return trajectories

    def _L0_ffn_ref(x, gate_w, gate_b, w1, b1, w2, b2):
        import jax, jax.numpy as jnp
        import numpy as np
        TOP_K = 2
        B, S, D = x.shape
        E = gate_w.shape[0]
        logits = jnp.einsum('bsd,ed->bse', x, gate_w) + gate_b
        scores = jax.nn.softmax(logits, axis=-1)
        topk_scores, topk_idx = jax.lax.top_k(scores, TOP_K)
        onehot = jax.nn.one_hot(topk_idx, E, dtype=scores.dtype)
        dispatch = jnp.einsum('bsk,bske->bse', topk_scores, onehot)
        x_flat = x.reshape(B * S, D)
        w_flat = dispatch.reshape(B * S, E)
        out = jnp.zeros_like(x_flat)
        for i in range(E):
            wi = w_flat[:, i:i + 1]
            h = jax.nn.relu(jnp.einsum('nd,hd->nh', x_flat * wi, w1[i]) + b1[i])
            y = jnp.einsum('nh,dh->nd', h, w2[i]) + b2[i]
            out = jnp.where(wi > 0, y, out)
        return out.reshape(B, S, D)

    def _L1_attn_ref(x, w_q, w_kv, w_out, ln_g, ln_b, lno_g, lno_b):
        import jax, jax.numpy as jnp
        import numpy as np
        import math
        DIM = 128
        DIM_HEAD = 64
        HEADS = 16
        B, N = (2, 256)

        def _layernorm(x, g, b, eps=1e-05):
            x32 = x.astype(jnp.float32)
            mu = jnp.mean(x32, axis=-1, keepdims=True)
            var = jnp.var(x32, axis=-1, keepdims=True)
            return ((x32 - mu) * jax.lax.rsqrt(var + eps) * g + b).astype(x.dtype)
        b, n, _ = x.shape
        scale = DIM_HEAD ** (-0.5)
        xn = _layernorm(x, ln_g, ln_b)
        q = jnp.einsum('bnc,ec->bne', xn, w_q)
        kv = jnp.einsum('bnc,ec->bne', xn, w_kv)
        k, v = jnp.split(kv, 2, axis=-1)
        q = q.reshape(b, n, HEADS, DIM_HEAD).transpose(0, 2, 1, 3)
        sqs = math.sqrt(scale)
        q = q * (scale * sqs)
        k = k * sqs
        sim = jnp.einsum('bhid,bjd->bhij', q, k)
        max_neg = -jnp.finfo(sim.dtype).max
        causal_mask = jnp.triu(jnp.ones((n, n), dtype=bool), k=1)
        sim = jnp.where(causal_mask, max_neg, sim)
        attn = jax.nn.softmax(sim.astype(jnp.float32), axis=-1).astype(sim.dtype)
        out = jnp.einsum('bhij,bjd->bhid', attn, v)
        out = out.transpose(0, 2, 1, 3).reshape(b, n, HEADS * DIM_HEAD)
        out = jnp.einsum('bne,ce->bnc', out, w_out)
        return _layernorm(out, lno_g, lno_b)

    def _L1_ffn_ref(x, w1_w, w1_s, w2_w, w2_s, h1_w, h1_s, h2_w, h2_s, w3_w, w3_s):
        import jax, jax.numpy as jnp
        import numpy as np
        D_IN, D_HID = (128, 512)

        def _ternary(key, shape):
            return jax.random.randint(key, shape, -1, 2).astype(jnp.float32)

        def _tlin(x, w, s):
            return jnp.einsum('bsi,oi->bso', x, w) * s
        h = jax.nn.silu(_tlin(x, w1_w, w1_s)) * _tlin(x, w2_w, w2_s)
        h = jax.nn.gelu(_tlin(h, h1_w, h1_s), approximate=False)
        h = jax.nn.gelu(_tlin(h, h2_w, h2_s), approximate=False)
        return _tlin(h, w3_w, w3_s)
    x = L0_attn_embeddings
    x = x + _layernorm(_L0_attn_ref(_layernorm(x, axis=-1), L0_attn_guidance_trajectories), axis=-1)
    x = x + _layernorm(_L0_ffn_ref(_layernorm(x, axis=-1), L0_ffn_gate_w, L0_ffn_gate_b, L0_ffn_w1, L0_ffn_b1, L0_ffn_w2, L0_ffn_b2), axis=-1)
    x = x + _layernorm(_L1_attn_ref(_layernorm(x, axis=-1), L1_attn_w_q, L1_attn_w_kv, L1_attn_w_out, L1_attn_ln_g, L1_attn_ln_b, L1_attn_lno_g, L1_attn_lno_b), axis=-1)
    x = x + _layernorm(_L1_ffn_ref(_layernorm(x, axis=-1), L1_ffn_w1_w, L1_ffn_w1_s, L1_ffn_w2_w, L1_ffn_w2_s, L1_ffn_h1_w, L1_ffn_h1_s, L1_ffn_h2_w, L1_ffn_h2_s, L1_ffn_w3_w, L1_ffn_w3_s), axis=-1)
    return x

_drawn_inputs = setup_inputs


def setup_inputs(seed=0):
    import zlib

    import numpy as np

    out = dict(_drawn_inputs(seed))
    spreads = {'L0_ffn_gate_b': (0.0, 0.1),
     'L0_ffn_b1': (0.0, 0.1),
     'L0_ffn_b2': (0.0, 0.1),
     'L1_attn_ln_g': (1.0, 0.2),
     'L1_attn_ln_b': (0.0, 0.1),
     'L1_attn_lno_g': (1.0, 0.2),
     'L1_attn_lno_b': (0.0, 0.1)}
    factors = {'L1_attn_w_q': 52.045}
    for name, (base, spread) in spreads.items():
        noise = np.random.default_rng([zlib.crc32(name.encode()), seed]).standard_normal(out[name].shape)
        drawn = base * np.exp(spread * noise) if base else spread * noise
        out[name] = jnp.asarray(drawn.astype(out[name].dtype))
    for name, factor in factors.items():
        out[name] = (out[name] * factor).astype(out[name].dtype)
    return out
```

```python
from contextlib import ExitStack

import concourse.bass as bass
from concourse import mybir

F32 = mybir.dt.float32
F32R = mybir.dt.float32r
I32 = mybir.dt.int32
U32 = mybir.dt.uint32
ALU = mybir.AluOpType
ACT = mybir.ActivationFunctionType
AX = mybir.AxisListType
PE_ENGINE = [mybir.EngineType.PE]
DVE_ENGINE = [mybir.EngineType.DVE]

P = 128
B, S, D = 16, 256, 128
HALVES = S // P
NT = B * HALVES
GT = 4
NG = NT // GT
GW = GT * D
GUIDES = 64
ZW = D + 1
EXPERTS = 8
HID = 4 * D
HC = HID // P
NS = NT + EXPERTS - 1
HEADS, DH = 16, 64
PAIRS = HEADS // 2
QG = 4
NQ = HEADS // QG
EPS = 1e-5
GUIDE_W = 0.4
EPS_MAG = 1e-6
EPS_COS = 1e-8
EPS_WSUM = 1e-8
SCALE = DH ** -0.5
MASKED = -1e30
CONSTS = ["diff", "cross", "band00", "band10", "band11", "causal", "before", "lower_e", "tile_no"]


def ds(start, size):
    return bass.ds(start, size)


def skewed(eng, n, unroll, *stages):
    reach = max(lag for lag, _ in stages)
    first = -(-(reach + unroll) // unroll) * unroll
    for s in range(first):
        for lag, f in stages:
            if s >= lag:
                f(s - lag, (s - lag) % unroll)
    with eng.Fori(first // unroll, n // unroll) as i:
        for u in range(unroll):
            for lag, f in stages:
                f(i * unroll + (u - lag), (u - lag) % unroll)
    for s in range(n, n + reach):
        for lag, f in stages:
            if s - lag < n:
                f(s - lag, (s - lag) % unroll)


def later(g, n):
    return not isinstance(g, int) or g >= n


def groups(eng, step):
    step(0, 0)
    step(1, 1)
    with eng.Fori(1, NG // 2 - 1) as i:
        step(i * 2, 0)
        step(i * 2 + 1, 1)
    step(NG - 2, 0)
    step(NG - 1, 1, False)


def tiles(eng, f, unroll=4):
    with eng.Fori(0, NT // unroll) as i:
        for u in range(unroll):
            f(i * unroll + u)


class Chain:

    def __init__(self, eng, sem):
        self.eng, self.sem, self.n = eng, sem, 0

    def add(self, ins, n=1):
        ins.then_inc(self.sem, 1)
        self.n += n

    def wait(self):
        self.eng.wait_ge(self.sem, self.n)

    def link(self, ins):
        self.add(ins)
        self.wait()


def layer_stats(dve, ch, src, width, st):
    tiles(dve, lambda t: dve.bn_stats(st["raw"][:, ds(t * 6, 6)], src[:, ds(t * width, D)]).then_inc(ch.sem, 1))
    ch.n += NT
    ch.wait()
    combine_stats(ch, st)


def combine_stats(ch, st):
    dve = ch.eng
    raw = st["raw"][:].rearrange("p (t k) -> p t k", k=6)
    dve.tensor_tensor(st["mean"][:], raw[:, :, 1], raw[:, :, 4], ALU.add).then_inc(ch.sem, 1)
    dve.tensor_tensor(st["diff"][:], raw[:, :, 1], raw[:, :, 4], ALU.subtract).then_inc(ch.sem, 1)
    dve.tensor_tensor(st["var"][:], raw[:, :, 2], raw[:, :, 5], ALU.add).then_inc(ch.sem, 1)
    ch.n += 3
    ch.wait()
    dve.tensor_scalar(st["mean"][:], st["mean"][:], 0.5, None, ALU.mult).then_inc(ch.sem, 1)
    dve.scalar_tensor_tensor(out=st["diff"][:], in0=st["diff"][:], scalar=0.25, in1=st["diff"][:], op0=ALU.mult,
                             op1=ALU.mult).then_inc(ch.sem, 1)
    ch.n += 2
    ch.wait()
    ch.link(dve.scalar_tensor_tensor(out=st["var"][:], in0=st["var"][:], scalar=1.0 / D, in1=st["diff"][:], op0=ALU.mult,
                                     op1=ALU.add))


def program(nc, x, guides, gate_wt, gate_b, w1t, b1, w2t, b2, wqt, wkt2, wvt, wot, ln_g, ln_b, lno_g, lno_b,
            f1t, f1s, f2t, f2s, h1t, h1s, h2t, h2s, f3t, f3s, consts, out):
    sorted_x = nc.dram_tensor("sorted_x", (NS * P, D), F32).ap()
    sorted_y = nc.dram_tensor("sorted_y", (NS * P, D), F32).ap()
    with ExitStack() as whole:
        def sem(name, stack=whole):
            return stack.enter_context(nc.semaphore(name))

        def sb(name, cols, dt=F32, stack=whole):
            return stack.enter_context(nc.sbuf_tensor(name, [P, cols], dt))

        def psum(name, banks, stack):
            return stack.enter_context(nc.psum_tensor(name, [P, banks * 512], F32))

        xs = sb("xs", NT * D)
        ident = sb("ident", P)
        neg_half = sb("neg_half", NT)
        half = sb("half", NT)
        st = {"raw": sb("stats_raw", NT * 6), "mean": sb("stats_mean", NT), "var": sb("stats_var", NT),
              "diff": sb("stats_diff", NT)}

        def mean(t):
            return st["mean"][:, ds(t, 1)]

        small = {n: sb("small_" + n, NT) for n in
                 ["ve", "rstd", "mag2", "mag", "inv", "ra", "an", "mw", "c6", "wsum", "rs", "t1", "t2"]}
        cb = sb("consts_sb", len(CONSTS) * P)
        const = {n: cb[:, i * P:(i + 1) * P] for i, n in enumerate(CONSTS)}
        ones = sb("ones", P)
        x_loaded, consts_loaded, setup_done = sem("x_loaded"), sem("consts_loaded"), sem("setup_done")
        moe_loaded, attn_loaded, ffn_loaded = sem("moe_loaded"), sem("attn_loaded"), sem("ffn_loaded")
        sorted_zeroed = sem("sorted_zeroed")
        all_stored = sem("all_stored")

        wq = sb("wq", HEADS * DH)
        wk2 = sb("wk2", P)
        wv = sb("wv", DH)
        wo = sb("wo", PAIRS * D)
        lng, lnb = sb("lng", 1), sb("lnb", 1)
        lnog, lnob = sb("lnog", D), sb("lnob", D)

        def broadcast(ap, n):
            return ap.rearrange("(a n) -> a n", a=1).to_broadcast((P, n))

        moe = ExitStack()
        w1 = sb("w1", EXPERTS * HID, stack=moe)
        w2 = sb("w2", EXPERTS * HID, stack=moe)
        b1s = sb("b1s", EXPERTS * HID, stack=moe)
        b2s = sb("b2s", EXPERTS * D, stack=moe)
        gw = sb("gw", EXPERTS, stack=moe)
        gb = sb("gb", EXPERTS, stack=moe)
        rows = sb("rows", NS * D, stack=moe)
        MOE_LOADS = 6

        with ExitStack() as ph:
            y = sb("y", NT * D, stack=ph)
            dif = sb("dif", NT * D, stack=ph)
            sq = [sb(f"sq{i}", GW, stack=ph) for i in range(2)]
            z = sb("z", NT * ZW, stack=ph)
            zt = z[:].rearrange("p (t k) -> p t k", k=ZW)
            nh = [sb(f"nh{i}", GW, stack=ph) for i in range(2)]
            nht = [sb(f"nht{i}", GW, stack=ph) for i in range(2)]
            et = [sb(f"et{i}", GW, stack=ph) for i in range(2)]
            guide = sb("guide", ZW, stack=ph)
            guide_n = sb("guide_n", D, stack=ph)
            guide_sq = sb("guide_sq", D, stack=ph)
            gt = sb("gt", GUIDES, stack=ph)
            gs = sb("gs", 4, stack=ph)
            c4 = [sb(f"c4{i}", GT, stack=ph) for i in range(2)]
            u = sb("u", NT * ZW, stack=ph)
            ut = u[:].rearrange("p (t k) -> p t k", k=ZW)
            ps_a = [psum(f"ps_a{i}", 1, ph) for i in range(2)]
            ps_s = [psum(f"ps_s{i}", 1, ph) for i in range(2)]
            ps_i = [psum(f"ps_i{i}", 2, ph) for i in range(2)]
            names = ["dve_done", "guide_loaded", "guide_mag2", "guide_mag", "guide_scaled", "guide_t", "guide_ready",
                     "var_ready", "rstd_ready", "y_ready", "diff_made", "diff_copied", "sq_free", 
                     "mag_ready", "mag_for_tanh", "tanh_ready", "nh_ready", "nht_made", "nht_ready", "sims_made",
                     "exp_ready", "infl_made", "infl_free", "z_ready", "u_made", "u_ready", "var2_ready",
                     "rs_ready", "et_zero", "sq_ready"]
            q = {n: sem("a_" + n, ph) for n in names}
            with nc.Block() as block:
                @block.sync
                def _(sp):
                    for c in range(4):
                        sp.dma_start(xs[:, c * 8 * D:(c + 1) * 8 * D].rearrange("p (t d) -> p t d", d=D),
                                     x.rearrange("b (h p) d -> p (b h) d", p=P)[:, c * 8:(c + 1) * 8, :]).then_inc(x_loaded, 16)
                    sp.dma_start(cb[:], consts).then_inc(consts_loaded, 16)
                    sp.dma_start(guide[0:GUIDES, 0:D], guides).then_inc(q["guide_loaded"], 16)
                    sp.wait_ge(setup_done, 6)
                    sp.dma_start(sorted_x.rearrange("(k p) d -> p k d", p=P),
                                 rows[:].rearrange("p (k d) -> p k d", d=D)).then_inc(sorted_zeroed, 16)
                    for dst, src in ((w1[:], w1t), (w2[:], w2t), (b1s[:], broadcast(b1, EXPERTS * HID)),
                                     (b2s[:], broadcast(b2, EXPERTS * D)), (gw[:], gate_wt),
                                     (gb[:], broadcast(gate_b, EXPERTS))):
                        sp.dma_start(dst, src).then_inc(moe_loaded, 16)
                    for dst, src in ((wq[:], wqt), (wk2[:], wkt2), (wv[:], wvt), (wo[:], wot), (lng[:], ln_g), (lnb[:], ln_b),
                                     (lnog[:], broadcast(lno_g, D)), (lnob[:], broadcast(lno_b, D))):
                        sp.dma_start(dst, src).then_inc(attn_loaded, 16)
                    sp.wait_ge(consts_loaded, 16)
                    sp.wait_ge(sorted_zeroed, 16)

                @block.gpsimd
                def _(pool):
                    pool.memset(neg_half[:], -0.5).then_inc(setup_done, 1)
                    pool.memset(half[:], 0.5).then_inc(setup_done, 1)
                    pool.memset(ident[:], 0.0).then_inc(setup_done, 1)
                    pool.memset(ones[:], 1.0).then_inc(setup_done, 1)
                    pool.wait_ge(setup_done, 4)
                    pool.affine_select(out=ident[:], in_=ident[:], compare_op=ALU.not_equal, fill=1.0, base=0,
                                       pattern=[[-1, P]], channel_multiplier=1).then_inc(setup_done, 1)
                    pool.memset(rows[:], 0.0).then_inc(setup_done, 1)
                    pool.wait_ge(q["guide_mag2"], 1)
                    pool.tensor_tensor(gs[0:GUIDES, 1:2], gs[0:GUIDES, 0:1], half[0:GUIDES, 0:1], ALU.pow).then_inc(q["guide_mag"], 1)
                    pool.wait_ge(q["var_ready"], 1)
                    pool.tensor_tensor(small["rstd"][:], small["ve"][:], neg_half[:], ALU.pow).then_inc(q["rstd_ready"], 1)
                    pool.wait_ge(q["sq_free"], NG)
                    pool.tensor_tensor(small["mag"][:], small["mag2"][:], half[:], ALU.pow).then_inc(q["mag_ready"], 1)
                    pool.wait_ge(q["var2_ready"], 1)
                    pool.tensor_tensor(small["rs"][:], small["ve"][:], neg_half[:], ALU.pow).then_inc(q["rs_ready"], 1)

                @block.vector
                def _(dve):
                    ch = Chain(dve, q["dve_done"])
                    dve.memset(guide[GUIDES:P, :], 0.0).then_inc(q["et_zero"], 1)
                    for i in range(2):
                        dve.memset(et[i][GUIDES:P, :], 0.0).then_inc(q["et_zero"], 1)
                    dve.wait_ge(q["guide_loaded"], 16)
                    ch.link(dve.tensor_tensor(guide_sq[0:GUIDES, :], guide[0:GUIDES, 0:D], guide[0:GUIDES, 0:D], ALU.mult))
                    ch.link(dve.memset(guide[0:GUIDES, D:ZW], 1.0))
                    dve.reduce_sum(gs[0:GUIDES, 0:1], guide_sq[0:GUIDES, :], AX.X).then_inc(q["guide_mag2"], 1)
                    dve.wait_ge(x_loaded, 64)
                    layer_stats(dve, ch, xs, D, st)
                    dve.tensor_scalar(small["ve"][:], st["var"][:], EPS, None, ALU.add).then_inc(q["var_ready"], 1)
                    dve.wait_ge(q["guide_mag"], 1)
                    ch.link(dve.tensor_scalar(gs[0:GUIDES, 2:3], gs[0:GUIDES, 1:2], EPS_COS, None, ALU.max))
                    ch.link(dve.reciprocal(gs[0:GUIDES, 3:4], gs[0:GUIDES, 2:3]))
                    dve.tensor_scalar(guide_n[0:GUIDES, :], guide[0:GUIDES, 0:D], gs[0:GUIDES, 3:4], None,
                                      ALU.mult).then_inc(q["guide_scaled"], 1)
                    dve.wait_ge(q["rstd_ready"], 1)
                    tiles(dve, lambda t: dve.tensor_scalar(y[:, ds(t * D, D)], xs[:, ds(t * D, D)], mean(t),
                                                           small["rstd"][:, ds(t, 1)], ALU.subtract,
                                                           ALU.mult).then_inc(q["y_ready"], 1))

                    def mag2(g, slot):
                        dve.wait_ge(q["sq_ready"], g + 1)
                        dve.reduce_sum(small["mag2"][:, ds(g * GT, GT)], sq[slot][:].rearrange("p (t d) -> p t d", d=D),
                                       AX.X).then_inc(q["sq_free"], 1)
                    skewed(dve, NG, 2, (0, mag2))
                    dve.wait_ge(q["mag_ready"], 1)
                    w = small
                    ch.link(dve.tensor_scalar(w["t1"][:], w["mag"][:], EPS_MAG, None, ALU.is_gt))
                    ch.link(dve.tensor_scalar(w["t2"][:], w["mag"][:], EPS_MAG, None, ALU.max))
                    ch.link(dve.reciprocal(w["inv"][:], w["t2"][:]))
                    ch.link(dve.tensor_tensor(w["inv"][:], w["inv"][:], w["t1"][:], ALU.mult))
                    ch.link(dve.tensor_tensor(w["an"][:], w["mag"][:], w["inv"][:], ALU.mult))
                    ch.link(dve.tensor_scalar(w["an"][:], w["an"][:], EPS_COS, None, ALU.max))
                    ch.link(dve.reciprocal(w["ra"][:], w["an"][:]))
                    ch.link(dve.tensor_tensor(w["ra"][:], w["ra"][:], w["inv"][:], ALU.mult))
                    dve.wait_ge(q["tanh_ready"], 1)
                    ch.link(dve.scalar_tensor_tensor(out=w["c6"][:], in0=w["inv"][:], scalar=1.0 - GUIDE_W, in1=w["mw"][:],
                                                     op0=ALU.mult, op1=ALU.mult))
                    ch.link(dve.tensor_copy(zt[:, :, D], w["mw"][:]))

                    def scale_dirs(g, slot):
                        def one(j):
                            return dve.tensor_scalar(nh[slot][:, j * D:(j + 1) * D], dif[:, ds((g * GT + j) * D, D)],
                                                     w["ra"][:, ds(g * GT + j, 1)], None, ALU.mult)
                        if later(g, 2):
                            dve.wait_ge(q["nht_made"], g - 1)
                        for j in range(GT):
                            one(j).then_inc(q["nh_ready"], 1)

                    base = ch.n
                    PER = 2 + GT

                    def blend(g, slot):
                        pi = ps_i[slot][:].rearrange("p (k c) -> p k c", k=2)[:, :, 0:2 * ZW].rearrange("p k (j c) -> p k j c", c=ZW)
                        dve.wait_ge(q["infl_made"], g + 1)
                        c = c4[slot][:].rearrange("p (k j) -> p k j", k=2)
                        dve.reciprocal(c, pi[:, :, :, D]).then_inc(ch.sem, 1)
                        dve.wait_ge(ch.sem, g * PER + (base + 1))
                        dve.scalar_tensor_tensor(out=c4[slot][:], in0=c4[slot][:], scalar=GUIDE_W,
                                                 in1=w["mw"][:, ds(g * GT, GT)], op0=ALU.mult, op1=ALU.mult).then_inc(ch.sem, 1)
                        dve.wait_ge(ch.sem, g * PER + (base + 2))
                        for j in range(GT):
                            dve.tensor_scalar(z[:, ds((g * GT + j) * ZW, D)], pi[:, j // 2, j % 2, 0:D], c4[slot][:, j:j + 1], None,
                                              ALU.mult).then_inc(ch.sem, 1)
                        dve.wait_ge(ch.sem, g * PER + (base + 2 + GT))
                        for j in range(GT):
                            dve.scalar_tensor_tensor(out=z[:, ds((g * GT + j) * ZW, D)], in0=dif[:, ds((g * GT + j) * D, D)],
                                                     scalar=w["c6"][:, ds(g * GT + j, 1)], in1=z[:, ds((g * GT + j) * ZW, D)],
                                                     op0=ALU.mult, op1=ALU.add).then_inc(q["z_ready"], 1)
                    skewed(dve, NG, 2, (0, scale_dirs), (2, blend))
                    ch.n += NG * PER
                    dve.wait_ge(q["u_ready"], 2 * NG)
                    layer_stats(dve, ch, u, ZW, st)
                    ch.link(dve.tensor_scalar(w["wsum"][:], ut[:, :, D], EPS_WSUM, None, ALU.max))
                    ch.link(dve.reciprocal(w["t1"][:], w["wsum"][:]))
                    ch.link(dve.tensor_tensor(w["t2"][:], w["t1"][:], w["t1"][:], ALU.mult))
                    ch.link(dve.tensor_tensor(w["ve"][:], st["var"][:], w["t2"][:], ALU.mult))
                    dve.tensor_scalar(w["ve"][:], w["ve"][:], EPS, None, ALU.add).then_inc(q["var2_ready"], 1)
                    dve.wait_ge(q["rs_ready"], 1)
                    ch.link(dve.tensor_tensor(w["rs"][:], w["rs"][:], w["t1"][:], ALU.mult))
                    tiles(dve, lambda t: dve.tensor_scalar(u[:, ds(t * ZW, D)], u[:, ds(t * ZW, D)], mean(t),
                                                           w["rs"][:, ds(t, 1)], ALU.subtract, ALU.mult).then_inc(ch.sem, 1))
                    ch.n += NT
                    ch.wait()
                    xst = xs[:].rearrange("p (t d) -> p t d", d=D)
                    ch.link(dve.tensor_tensor(xst, xst, ut[:, :, 0:D], ALU.add))

                @block.scalar
                def _(act):
                    act.wait_ge(q["guide_t"], 1)
                    act.activation(gt[:], ps_s[0][:, 0:GUIDES], ACT.Copy).then_inc(q["guide_ready"], 1)

                    def square(g, slot):
                        act.wait_ge(q["diff_made"], g + 1)
                        act.activation(dif[:, ds(g * GW, GW)], ps_a[slot][:], ACT.Copy).then_inc(q["diff_copied"], 1)
                        if later(g, 2):
                            act.wait_ge(q["sq_free"], g - 1)
                        act.activation(sq[slot][:], ps_a[slot][:], ACT.Square).then_inc(q["sq_ready"], 1)
                    skewed(act, NG, 2, (0, square))
                    act.wait_ge(q["mag_ready"], 1)
                    act.activation(small["mw"][:], small["mag"][:], ACT.Tanh, scale=2.0).then_inc(q["tanh_ready"], 1)

                    def turn(g, slot):
                        act.wait_ge(q["nht_made"], g + 1)
                        act.activation(nht[slot][:], ps_a[slot][:], ACT.Copy).then_inc(q["nht_ready"], 1)

                    def weigh(g, slot):
                        act.wait_ge(q["sims_made"], g + 1)
                        act.activation(et[slot][0:GUIDES, :], ps_s[slot][0:GUIDES, :], ACT.Exp, scale=2.0).then_inc(q["exp_ready"], 1)
                    skewed(act, NG, 2, (0, turn), (1, weigh))

                    def copy_u(g, slot):
                        act.wait_ge(q["u_made"], g + 1)
                        uv = u[:, ds(g * GT * ZW, GT * ZW)].rearrange("p (b h c) -> p b h c", b=2, h=2)
                        for h in range(2):
                            act.activation(uv[:, :, h, :], ps_i[slot][:, h * 512:h * 512 + 2 * ZW].rearrange("p (b c) -> p b c", b=2),
                                           ACT.Copy).then_inc(q["u_ready"], 1)
                    skewed(act, NG, 2, (0, copy_u))

                @block.tensor
                def _(pe):
                    pe.wait_ge(setup_done, 6)
                    pe.wait_ge(q["guide_scaled"], 1)
                    pe.transpose(ps_s[0][:, 0:GUIDES], guide_n[0:GUIDES, :], ident[0:GUIDES, 0:GUIDES]).then_inc(q["guide_t"], 1)
                    pe.wait_ge(consts_loaded, 16)

                    def differences(g, slot):
                        pe.wait_ge(q["y_ready"], g * GT + GT)
                        if later(g, 2):
                            pe.wait_ge(q["sq_ready"], g - 1)
                        yg = y[:, ds(g * GW, GW)]
                        pe.matmul(ps_a[slot][:], const["diff"], yg, start=True, stop=False)
                        pe.matmul(ps_a[slot][:].rearrange("p (b h d) -> p b h d", b=2, h=2)[:, :, 0, :], const["cross"],
                                  yg.rearrange("p (b h d) -> p b h d", b=2, h=2)[:, :, 1, :],
                                  start=False, stop=True).then_inc(q["diff_made"], 1)
                    skewed(pe, NG, 2, (0, differences))
                    pe.wait_ge(q["sq_ready"], NG)
                    pe.wait_ge(q["guide_ready"], 1)
                    pe.wait_ge(q["et_zero"], 3)

                    def turn(g, slot):
                        pe.wait_ge(q["nh_ready"], g * GT + GT)
                        if later(g, 2):
                            pe.wait_ge(q["nht_ready"], g - 1)
                        for j in range(GT):
                            last = pe.transpose(ps_a[slot][:, j * D:(j + 1) * D], nh[slot][:, j * D:(j + 1) * D], ident[:])
                        last.then_inc(q["nht_made"], 1)

                    def sims(g, slot):
                        pe.wait_ge(q["nht_ready"], g + 1)
                        if later(g, 2):
                            pe.wait_ge(q["exp_ready"], g - 1)
                        pe.matmul(ps_s[slot][0:GUIDES, :], gt[:], nht[slot][:], start=True, stop=True).then_inc(q["sims_made"], 1)

                    def influence(g, slot):
                        pe.wait_ge(q["exp_ready"], g + 1)
                        if later(g, 2):
                            pe.wait_ge(q["z_ready"], (g - 1) * GT)
                        for j in range(GT):
                            last = pe.matmul(ps_i[slot][:, (j // 2) * 512 + (j % 2) * ZW:][:, 0:ZW], et[slot][:, j * D:(j + 1) * D],
                                             guide[:], start=(j % 2 == 0), stop=True, skip_group_check=True)
                        last.then_inc(q["infl_made"], 1)
                    skewed(pe, NG, 2, (0, turn), (1, sims), (2, influence))

                    def window(g, slot):
                        pe.wait_ge(q["z_ready"], NT)
                        if later(g, 2):
                            pe.wait_ge(q["u_ready"], 2 * g - 2)
                        zg = z[:, ds(g * GT * ZW, GT * ZW)].rearrange("p (b h c) -> p b h c", b=2, h=2)
                        o = [ps_i[slot][:, h * 512:h * 512 + 2 * ZW].rearrange("p (b c) -> p b c", b=2) for h in range(2)]
                        pe.matmul(o[0], const["band00"], zg[:, :, 0, :], start=True, stop=True)
                        pe.matmul(o[1], const["band10"], zg[:, :, 0, :], start=True, stop=False)
                        pe.matmul(o[1], const["band11"], zg[:, :, 1, :], start=False, stop=True).then_inc(q["u_made"], 1)
                    skewed(pe, NG, 2, (0, window))



        with ExitStack() as ph:
            yn = [sb(f"yn{i}", GW, stack=ph) for i in range(2)]
            yt = [sb(f"yt{i}", GW, stack=ph) for i in range(2)]
            ys = sb("ys", NT * D, stack=ph)
            TE = NT * EXPERTS
            r = {n: sb("r_" + n, TE, stack=ph) for n in ["score", "rank", "chosen", "key", "onehot", "tot", "acc0", "acc1", "slot"]}
            cmp_a = sb("cmp_a", TE * EXPERTS, stack=ph)
            cmp_b = sb("cmp_b", TE * EXPERTS, stack=ph)
            e8 = {n: sb("e8_" + n, EXPERTS, stack=ph) for n in ["tiles", "acc0", "acc1", "first"]}
            t32 = {n: sb("t32_" + n, NT, stack=ph) for n in ["max", "sum", "w", "slot"]}
            slot_i = sb("slot_i", NT, I32, stack=ph)
            expert_f = sb("expert_f", NS, stack=ph)
            expert_i = sb("expert_i", NS, I32, stack=ph)
            xin = [sb(f"xin{i}", D, stack=ph) for i in range(3)]
            xt = [sb(f"xt{i}", P, stack=ph) for i in range(3)]
            hp = [sb(f"hp{i}", HID, stack=ph) for i in range(3)]
            ht = [sb(f"ht{i}", HID, stack=ph) for i in range(3)]
            e_up = [sb(f"e_up{i}", 1, I32, stack=ph) for i in range(3)]
            e_down = [sb(f"e_down{i}", 1, I32, stack=ph) for i in range(3)]
            res = sb("res", NS * D, stack=ph)
            bank = [psum(f"bank{i}", 1, ph) for i in range(8)]
            names = ["dve_done", "var_ready", "rstd_ready", "yn_ready", "yt_made", "yt_ready", "logits_made", "logits_read",
                     "shifted", "exp_ready", "onehot_ready", "counts_made", "slots_ready", "ys_ready", "scattered",
                     "rows_loaded", "xin_ready", "xt_made", "xt_ready", "h_made", "hp_ready", "ht_made", "ht_ready", "o_made",
                     "res_ready", "res_stored", "gathered", "var2_ready", "rs_ready", "expert_ready", "e_up_ready", "e_down_ready"]
            q = {n: sem("b_" + n, ph) for n in names}
            THIRD = NS // 3
            with nc.Block() as block:
                @block.sync
                def _(sp):
                    sp.wait_ge(q["scattered"], 16 * NT)
                    sp.dma_start(rows[:].rearrange("p (k d) -> p k d", d=D),
                                 sorted_x.rearrange("(k p) d -> p k d", p=P)).then_inc(q["rows_loaded"], 16)
                    for c in range(3):
                        sp.wait_ge(q["res_ready"], (c + 1) * THIRD)
                        sp.dma_start(sorted_y.rearrange("(k p) d -> p k d", p=P)[:, c * THIRD:(c + 1) * THIRD, :],
                                     res[:, c * THIRD * D:(c + 1) * THIRD * D].rearrange("p (k d) -> p k d", d=D)
                                     ).then_inc(q["res_stored"], 16)
                    sp.wait_ge(q["res_stored"], 48)

                @block.gpsimd
                def _(pool):
                    pool.wait_ge(q["var_ready"], 1)
                    pool.tensor_tensor(small["rstd"][:], small["ve"][:], neg_half[:], ALU.pow).then_inc(q["rstd_ready"], 1)
                    pool.wait_ge(q["slots_ready"], 1)
                    for t in range(NT):
                        if t % 4 == 0:
                            pool.wait_ge(q["ys_ready"], t + 4)
                        pool.indirect_dma_start(out=sorted_x, out_offset=bass.IndirectOffsetOnAxis(ap=slot_i[:, t:t + 1].bitcast(U32), axis=0),
                                                in_=ys[:, t * D:(t + 1) * D], in_offset=None).then_inc(q["scattered"], 16)
                    pool.wait_ge(q["rows_loaded"], 16)
                    pool.wait_ge(q["expert_ready"], 1)

                    def pick(k, slot):
                        if later(k, 3):
                            pool.wait_ge(q["xt_made"], k - 2)
                            pool.wait_ge(q["hp_ready"], k - 2)
                        pool.tensor_copy(e_up[slot][:], expert_i[:, ds(k, 1)]).then_inc(q["e_up_ready"], 1)
                        pool.tensor_copy(xin[slot][:], rows[:, ds(k * D, D)]).then_inc(q["xin_ready"], 1)
                    skewed(pool, NS, 3, (0, pick))
                    pool.wait_ge(q["res_stored"], 48)
                    for t in range(NT):
                        pool.indirect_dma_start(out=ys[:, t * D:(t + 1) * D], out_offset=None,
                                                in_offset=bass.IndirectOffsetOnAxis(ap=slot_i[:, t:t + 1].bitcast(U32), axis=0),
                                                in_=sorted_y).then_inc(q["gathered"], 16)
                    pool.wait_ge(q["gathered"], 16 * NT)
                    pool.wait_ge(q["var2_ready"], 1)
                    pool.tensor_tensor(small["rs"][:], small["ve"][:], neg_half[:], ALU.pow).then_inc(q["rs_ready"], 1)

                @block.vector
                def _(dve):
                    ch = Chain(dve, q["dve_done"])
                    w = small
                    layer_stats(dve, ch, xs, D, st)
                    dve.tensor_scalar(w["ve"][:], st["var"][:], EPS, None, ALU.add).then_inc(q["var_ready"], 1)
                    dve.wait_ge(q["rstd_ready"], 1)
                    dve.wait_ge(moe_loaded, 16 * MOE_LOADS)

                    def normalise(g, slot):
                        if later(g, 2):
                            dve.wait_ge(q["yt_made"], g - 1)
                        for j in range(GT):
                            dve.tensor_scalar(yn[slot][:, j * D:(j + 1) * D], xs[:, ds((g * GT + j) * D, D)], mean(g * GT + j),
                                              w["rstd"][:, ds(g * GT + j, 1)], ALU.subtract, ALU.mult).then_inc(q["yn_ready"], 1)

                    def take_logits(g, slot):
                        dve.wait_ge(q["logits_made"], g + 1)
                        dve.tensor_tensor(r["score"][:, ds(g * GT * EXPERTS, GT * EXPERTS)].rearrange("p (t e) -> p t e", e=EXPERTS),
                                          bank[2 + slot][:, 0:GT * EXPERTS].rearrange("p (t e) -> p t e", e=EXPERTS),
                                          gb[:].unsqueeze(1).to_broadcast((P, GT, EXPERTS)), ALU.add).then_inc(q["logits_read"], 1)
                    skewed(dve, NG, 2, (0, normalise), (2, take_logits))
                    dve.wait_ge(q["logits_read"], NG)

                    def te(name):
                        return r[name][:].rearrange("p (t e) -> p t e", e=EXPERTS)

                    def over_e(ap):
                        return ap.unsqueeze(2).to_broadcast((P, NT, EXPERTS))

                    ch.link(dve.reduce_max(t32["max"][:], te("score"), AX.X))
                    dve.tensor_tensor(te("score"), te("score"), over_e(t32["max"][:]), ALU.subtract).then_inc(q["shifted"], 1)
                    dve.wait_ge(q["exp_ready"], 1)
                    ch.link(dve.reduce_sum(t32["sum"][:], te("key"), AX.X))
                    ch.link(dve.reciprocal(t32["sum"][:], t32["sum"][:]))
                    ch.link(dve.tensor_tensor(te("score"), te("key"), over_e(t32["sum"][:]), ALU.mult))
                    four = (P, NT, EXPERTS, EXPERTS)
                    other = te("score").unsqueeze(2).to_broadcast(four)
                    own = te("score").unsqueeze(3).to_broadcast(four)
                    ca = cmp_a[:].rearrange("p (t e f) -> p t e f", e=EXPERTS, f=EXPERTS)
                    cbv = cmp_b[:].rearrange("p (t e f) -> p t e f", e=EXPERTS, f=EXPERTS)
                    ch.add(dve.tensor_tensor(ca, other, own, ALU.is_gt))
                    ch.link(dve.tensor_tensor(cbv, other, own, ALU.is_equal))
                    ch.link(dve.tensor_tensor(cmp_b[:].rearrange("p (t k) -> p t k", t=NT), cmp_b[:].rearrange("p (t k) -> p t k", t=NT),
                                              const["lower_e"][:, 0:EXPERTS * EXPERTS].unsqueeze(1).to_broadcast((P, NT, EXPERTS * EXPERTS)),
                                              ALU.mult))
                    ch.link(dve.tensor_tensor(cmp_a[:], cmp_a[:], cmp_b[:], ALU.add))
                    ch.link(dve.reduce_sum(te("rank"), ca, AX.X))
                    ch.add(dve.tensor_scalar(r["rank"][:], r["rank"][:], 1.5, None, ALU.is_lt))
                    ch.link(dve.tensor_scalar(r["chosen"][:], r["score"][:], 0.0, None, ALU.is_gt))
                    ch.link(dve.tensor_tensor(r["chosen"][:], r["chosen"][:], r["rank"][:], ALU.mult))
                    ch.link(dve.tensor_tensor(te("key"), te("chosen"), const["lower_e"][:, EXPERTS * EXPERTS:EXPERTS * EXPERTS + EXPERTS]
                                              .unsqueeze(1).to_broadcast((P, NT, EXPERTS)), ALU.mult))
                    ch.link(dve.reduce_max(t32["max"][:], te("key"), AX.X))
                    ch.link(dve.tensor_tensor(te("onehot"), te("key"), over_e(t32["max"][:]), ALU.is_equal))
                    dve.tensor_tensor(r["onehot"][:], r["onehot"][:], r["chosen"][:], ALU.mult).then_inc(q["onehot_ready"], 1)
                    dve.wait_ge(q["onehot_ready"], 1)
                    ch.link(dve.tensor_tensor(r["rank"][:], r["onehot"][:], r["score"][:], ALU.mult))
                    ch.link(dve.reduce_sum(t32["w"][:], te("rank"), AX.X))
                    ch.link(dve.tensor_tensor(w["t1"][:], t32["w"][:], w["rstd"][:], ALU.mult))
                    tiles(dve, lambda t: dve.tensor_scalar(ys[:, ds(t * D, D)], xs[:, ds(t * D, D)], mean(t), w["t1"][:, ds(t, 1)],
                                                           ALU.subtract, ALU.mult).then_inc(q["ys_ready"], 1))
                    dve.wait_ge(q["counts_made"], 1)
                    ch.add(dve.tensor_copy(r["tot"][:], bank[5][:, 0:TE]))
                    ch.link(dve.tensor_copy(r["acc0"][:], bank[5][:, 0:TE]))
                    now, nxt = "acc0", "acc1"
                    step = 1
                    while step < NT:
                        k = step * EXPERTS
                        ch.add(dve.tensor_copy(r[nxt][:, 0:k], r[now][:, 0:k]))
                        ch.link(dve.tensor_tensor(r[nxt][:, k:TE], r[now][:, k:TE], r[now][:, 0:TE - k], ALU.add))
                        now, nxt, step = nxt, now, 2 * step
                    count = r[now][:, TE - EXPERTS:TE]
                    many = cmp_a[:, 0:EXPERTS * NT].rearrange("p (e k) -> p e k", k=NT)
                    ch.link(dve.tensor_scalar(cmp_b[:, 0:NT], const["tile_no"][:, 0:NT], float(P), None, ALU.mult))
                    ch.link(dve.tensor_tensor(many, count.unsqueeze(2).to_broadcast((P, EXPERTS, NT)),
                                              cmp_b[:, 0:NT].unsqueeze(1).to_broadcast((P, EXPERTS, NT)), ALU.is_gt))
                    ch.link(dve.reduce_sum(e8["tiles"][:], many, AX.X))
                    ch.link(dve.tensor_copy(e8["acc0"][:], e8["tiles"][:]))
                    a, b_ = "acc0", "acc1"
                    step = 1
                    while step < EXPERTS:
                        ch.add(dve.tensor_copy(e8[b_][:, 0:step], e8[a][:, 0:step]))
                        ch.link(dve.tensor_tensor(e8[b_][:, step:], e8[a][:, step:], e8[a][:, 0:EXPERTS - step], ALU.add))
                        a, b_, step = b_, a, 2 * step
                    ch.link(dve.tensor_tensor(e8["first"][:], e8[a][:], e8["tiles"][:], ALU.subtract))
                    ch.link(dve.tensor_scalar(e8["first"][:], e8["first"][:], float(P), None, ALU.mult))
                    ch.link(dve.tensor_tensor(r["slot"][:], r[now][:], r["tot"][:], ALU.subtract))
                    ch.link(dve.tensor_tensor(r["slot"][:], bank[4][:, 0:TE], r["slot"][:], ALU.add))
                    ch.link(dve.tensor_tensor(te("slot"), te("slot"), e8["first"][:].unsqueeze(1).to_broadcast((P, NT, EXPERTS)), ALU.add))
                    ch.link(dve.tensor_tensor(r["slot"][:], r["slot"][:], r["onehot"][:], ALU.mult))
                    ch.link(dve.reduce_sum(t32["slot"][:], te("slot"), AX.X))
                    dve.tensor_copy(slot_i[:], t32["slot"][:]).then_inc(q["slots_ready"], 1)
                    ended = cmp_a[:, 0:NS * EXPERTS].rearrange("p (k e) -> p k e", e=EXPERTS)
                    ch.link(dve.tensor_tensor(ended, const["tile_no"][:, 0:NS].unsqueeze(2).to_broadcast((P, NS, EXPERTS)),
                                              e8[a][:].unsqueeze(1).to_broadcast((P, NS, EXPERTS)), ALU.is_ge))
                    ch.link(dve.reduce_sum(expert_f[:], ended, AX.X))
                    ch.link(dve.tensor_scalar(expert_f[:], expert_f[:], float(EXPERTS - 1), None, ALU.min))
                    dve.tensor_copy(expert_i[:], expert_f[:]).then_inc(q["expert_ready"], 1)
                    dve.wait_ge(q["expert_ready"], 1)

                    def expert_in(cell):
                        return nc.values_load(cell[0:1, 0:1], engines=DVE_ENGINE, min_val=0, max_val=EXPERTS - 1)

                    def bias1(k, slot):
                        if later(k, 3):
                            dve.wait_ge(q["res_ready"], k - 2)
                        dve.wait_ge(q["e_up_ready"], k + 1)
                        dve.tensor_copy(e_down[slot][:], expert_i[:, ds(k, 1)]).then_inc(q["e_down_ready"], 1)
                        e = expert_in(e_up[slot])
                        dve.wait_ge(q["e_down_ready"], k + 1)
                        dve.wait_ge(q["h_made"], k + 1)
                        dve.tensor_tensor(hp[slot][:], bank[slot][:], b1s[:, ds(e * HID, HID)], ALU.add).then_inc(q["hp_ready"], 1)

                    def bias2(k, slot):
                        e = expert_in(e_down[slot])
                        dve.wait_ge(q["o_made"], k + 1)
                        dve.tensor_tensor(res[:, ds(k * D, D)], bank[7][:, 0:D], b2s[:, ds(e * D, D)],
                                          ALU.add).then_inc(q["res_ready"], 1)
                    skewed(dve, NS, 3, (0, bias1), (2, bias2))
                    dve.wait_ge(q["gathered"], 16 * NT)
                    layer_stats(dve, ch, ys, D, st)
                    dve.tensor_scalar(w["ve"][:], st["var"][:], EPS, None, ALU.add).then_inc(q["var2_ready"], 1)
                    dve.wait_ge(q["rs_ready"], 1)
                    tiles(dve, lambda t: dve.tensor_scalar(ys[:, ds(t * D, D)], ys[:, ds(t * D, D)], mean(t),
                                                           w["rs"][:, ds(t, 1)], ALU.subtract, ALU.mult).then_inc(ch.sem, 1))
                    ch.n += NT
                    ch.wait()
                    ch.link(dve.tensor_tensor(xs[:], xs[:], ys[:], ALU.add))

                @block.scalar
                def _(act):
                    def turn(g, slot):
                        act.wait_ge(q["yt_made"], g + 1)
                        if later(g, 2):
                            act.wait_ge(q["logits_made"], g - 1)
                        act.activation(yt[slot][:], bank[slot][:], ACT.Copy).then_inc(q["yt_ready"], 1)
                    skewed(act, NG, 2, (0, turn))
                    act.wait_ge(q["shifted"], 1)
                    act.activation(r["key"][:], r["score"][:], ACT.Exp).then_inc(q["exp_ready"], 1)

                    def turn_x(k, slot):
                        act.wait_ge(q["xt_made"], k + 1)
                        if later(k, 3):
                            act.wait_ge(q["h_made"], k - 2)
                        act.activation(xt[slot][:], bank[6][:, 0:P], ACT.Copy).then_inc(q["xt_ready"], 1)

                    def relu(k, slot):
                        act.wait_ge(q["ht_made"], k + 1)
                        if later(k, 3):
                            act.wait_ge(q["o_made"], k - 2)
                        act.activation(ht[slot][:], bank[3 + slot % 3][:], ACT.Relu).then_inc(q["ht_ready"], 1)
                    skewed(act, NS, 3, (0, turn_x), (2, relu))

                @block.tensor
                def _(pe):
                    def turn(g, slot):
                        pe.wait_ge(q["yn_ready"], g * GT + GT)
                        if later(g, 2):
                            pe.wait_ge(q["yt_ready"], g - 1)
                        for j in range(GT):
                            last = pe.transpose(bank[slot][:, j * D:(j + 1) * D], yn[slot][:, j * D:(j + 1) * D], ident[:])
                        last.then_inc(q["yt_made"], 1)

                    def gate(g, slot):
                        pe.wait_ge(q["yt_ready"], g + 1)
                        if later(g, 2):
                            pe.wait_ge(q["logits_read"], g - 1)
                        for j in range(GT):
                            last = pe.matmul(bank[2 + slot][:, j * EXPERTS:(j + 1) * EXPERTS], yt[slot][:, j * P:(j + 1) * P], gw[:],
                                             start=True, stop=True)
                        last.then_inc(q["logits_made"], 1)
                    pe.wait_ge(moe_loaded, 16 * MOE_LOADS)
                    skewed(pe, NG, 2, (0, turn), (1, gate))
                    pe.wait_ge(q["onehot_ready"], 1)
                    pe.matmul(bank[4][:, 0:TE], const["before"], r["onehot"][:], start=True, stop=True)
                    pe.matmul(bank[5][:, 0:TE], ones[:], r["onehot"][:], start=True, stop=True).then_inc(q["counts_made"], 1)
                    pe.wait_ge(q["expert_ready"], 1)

                    def expert_in(cell):
                        return nc.values_load(cell[0:1, 0:1], engines=PE_ENGINE, min_val=0, max_val=EXPERTS - 1)

                    def turn_x(k, slot):
                        pe.wait_ge(q["xin_ready"], k + 1)
                        if later(k, 1):
                            pe.wait_ge(q["xt_ready"], k)
                        pe.transpose(bank[6][:, 0:P], xin[slot][:], ident[:]).then_inc(q["xt_made"], 1)

                    def up(k, slot):
                        e = expert_in(e_up[slot])
                        pe.wait_ge(q["xt_ready"], k + 1)
                        if later(k, 3):
                            pe.wait_ge(q["hp_ready"], k - 2)
                        pe.matmul(bank[slot][:], xt[slot][:], w1[:, ds(e * HID, HID)], start=True, stop=True).then_inc(q["h_made"], 1)

                    def turn_h(k, slot):
                        pe.wait_ge(q["hp_ready"], k + 1)
                        if later(k, 3):
                            pe.wait_ge(q["ht_ready"], k - 2)
                        for c in range(HC):
                            last = pe.transpose(bank[3 + slot][:, c * P:(c + 1) * P], hp[slot][:, c * P:(c + 1) * P], ident[:])
                        last.then_inc(q["ht_made"], 1)

                    def down(k, slot):
                        e = expert_in(e_down[slot])
                        pe.wait_ge(q["ht_ready"], k + 1)
                        if later(k, 1):
                            pe.wait_ge(q["res_ready"], k)
                        for c in range(HC):
                            last = pe.matmul(bank[7][:, 0:D], ht[slot][:, c * P:(c + 1) * P],
                                             w2[:, ds(e * HC * D + c * D, D)], start=(c == 0), stop=(c == HC - 1))
                        last.then_inc(q["o_made"], 1)
                    skewed(pe, NS, 3, (0, turn_x), (1, up), (2, turn_h), (3, down))
        moe.close()

        with ExitStack() as ph:
            W = S
            UNITS = 18
            SQS = SCALE ** 0.5
            wqh, wql = sb("wqh", HEADS * DH, F32R, ph), sb("wql", HEADS * DH, F32R, ph)
            wkh, wkl = sb("wkh", P, F32R, ph), sb("wkl", P, F32R, ph)
            wvh, wvl = sb("wvh", DH, F32R, ph), sb("wvl", DH, F32R, ph)
            ident_r = sb("ident_r", P, F32R, ph)
            causal_r = sb("causal_r", QG * P, F32R, ph)
            zb = [sb(f"zb{i}", W, F32, ph) for i in range(2)]
            xh = [sb(f"xh{i}", W, F32R, ph) for i in range(2)]
            xl = [sb(f"xl{i}", W, F32R, ph) for i in range(2)]
            xf = sb("xf", W, F32, ph)
            qx = [sb(f"qx{i}", HEADS * W, F32R, ph) for i in range(2)]
            qm = [sb(f"qm{i}", HEADS * W, F32R, ph) for i in range(2)]
            kh = [sb(f"kh{i}", W, F32R, ph) for i in range(2)]
            kl = [sb(f"kl{i}", W, F32R, ph) for i in range(2)]
            vv = [sb(f"vv{i}", HALVES * DH, F32, ph) for i in range(2)]
            mx = sb("mx", HALVES * HEADS, F32, ph)
            mts = sb("mts", P, F32R, ph)
            pt0 = [sb(f"pt0{i}", QG * W, F32, ph) for i in range(2)]
            pt1 = [sb(f"pt1{i}", QG * P, F32, ph) for i in range(2)]
            rec = sb("rec", 2 * W, F32, ph)
            ot = [sb(f"ot{i}", PAIRS * W, F32, ph) for i in range(2)]
            oa = sb("oa", NT * D, F32, ph)
            ring = [psum(f"ring{i}", 1, ph) for i in range(3)]
            ps_s = psum("ps_scores", 3, ph)
            ps_o, ps_d = psum("ps_out", 1, ph), psum("ps_den", 1, ph)
            names = ["dve_done", "var_ready", "rstd_ready", "var2_ready", "r2_ready", "weights_high", "weights_split", "const_ready",
                     "zb_ready", "z_made", "xh_ready", "xf_ready", "x_ready", "ring_made", "ring_read", "kh_ready",
                     "qh_ready", "qm_ready", "mts_ready", "max_loaded", "scores_made", "exp_ready", "masked", "pv_made",
                     "rec_ready", "normed", "proj_made", "proj_read", "var3_ready", "rs3_ready", "var4_ready", "rs4_ready", "pool_turn"]
            q = {n: sem("c_" + n, ph) for n in names}

            def batches(eng, prepare, attend):
                prepare(0, 0)
                attend(0, 0, True, False)
                with eng.Fori(0, B // 2 - 1) as i:
                    attend(i * 2 + 1, 1, True, True)
                    attend(i * 2 + 2, 0, True, True)
                attend(B - 1, 1, False, True)

            with nc.Block() as block:
                @block.sync
                def _(sp):
                    def load_max(n, slot):
                        sp.wait_ge(q["mts_ready"], n + 1)
                        for h in range(HALVES):
                            sp.dma_start(qm[slot][DH:DH + 1, :].rearrange("o (e h p) -> o e h p", h=HALVES, p=P)[:, :, h, :].bitcast(F32),
                                         mts[h * HEADS:(h + 1) * HEADS, :].bitcast(F32)).then_inc(q["max_loaded"], 16)
                    batches(sp, load_max, lambda b, slot, prep, before: load_max(b + 1, 1 - slot) if prep else None)
                    sp.wait_ge(q["max_loaded"], 32 * B)

                @block.gpsimd
                def _(pool):
                    pool.wait_ge(q["var_ready"], 1)
                    pool.tensor_tensor(small["rstd"][:], small["ve"][:], neg_half[:], ALU.pow).then_inc(q["rstd_ready"], 1)
                    pool.wait_ge(q["var2_ready"], 1)
                    pool.tensor_tensor(small["rs"][:], small["ve"][:], neg_half[:], ALU.pow).then_inc(q["r2_ready"], 1)

                    def copy_queries(n, slot, u):
                        pool.wait_ge(q["qh_ready"], n * 8 + (2 * u + 2))
                        pool.sem_inc(q["pool_turn"], 1)
                        c = 4 * W
                        pool.tensor_copy(qm[slot][0:DH, u * c:(u + 1) * c], qx[slot][0:DH, u * c:(u + 1) * c]).then_inc(q["qm_ready"], 1)

                    def mask(b, g):
                        pool.wait_ge(q["exp_ready"], b * 8 + (2 * g + 1))
                        pool.sem_inc(q["pool_turn"], 1)
                        v = pt0[g % 2][:].rearrange("p (e i) -> p e i", e=QG)[:, :, 0:P]
                        pool.affine_select(out=v, in_=v, compare_op=ALU.is_ge, fill=0.0, base=0, pattern=[[0, QG], [1, P]],
                                           channel_multiplier=-1).then_inc(q["masked"], 1)
                        pool.wait_ge(q["exp_ready"], b * 8 + (2 * g + 2))
                        pool.sem_inc(q["pool_turn"], 1)
                        v = pt1[g % 2][:].rearrange("p (e i) -> p e i", e=QG)
                        pool.affine_select(out=v, in_=v, compare_op=ALU.is_ge, fill=0.0, base=0, pattern=[[0, QG], [1, P]],
                                           channel_multiplier=-1).then_inc(q["masked"], 1)

                    def prepare(n, slot):
                        for u in range(4):
                            copy_queries(n, slot, u)

                    def attend(b, slot, prep, before):
                        for g in range(NQ):
                            mask(b, g)
                            if prep and g < 2:
                                copy_queries(b + 1, 1 - slot, 2 * g)
                                copy_queries(b + 1, 1 - slot, 2 * g + 1)
                    batches(pool, prepare, attend)
                    pool.wait_ge(q["var3_ready"], 1)
                    pool.tensor_tensor(small["rs"][:], small["ve"][:], neg_half[:], ALU.pow).then_inc(q["rs3_ready"], 1)
                    pool.wait_ge(q["var4_ready"], 1)
                    pool.tensor_tensor(small["rs"][:], small["ve"][:], neg_half[:], ALU.pow).then_inc(q["rs4_ready"], 1)

                @block.vector
                def _(dve):
                    ch = Chain(dve, q["dve_done"])
                    w = small
                    dve.wait_ge(attn_loaded, 16 * 8)
                    for high, low, full in ((wqh, wql, wq), (wkh, wkl, wk2), (wvh, wvl, wv)):
                        ch.link(dve.tensor_copy(high[:], full[:]))
                        ch.link(dve.tensor_tensor(low[:], full[:], high[:].bitcast(F32), ALU.subtract))
                    ch.link(dve.tensor_copy(ident_r[:], ident[:]))
                    ch.link(dve.tensor_copy(causal_r[:].rearrange("p (e j) -> p e j", e=QG), const["causal"].unsqueeze(1).to_broadcast((P, QG, P))))
                    for i in range(2):
                        ch.link(dve.memset(qm[i][DH:P, :].bitcast(F32), 0.0))
                        ch.link(dve.memset(kl[i][DH:P, :].bitcast(F32), 0.0))
                        ch.link(dve.memset(kl[i][DH:DH + 1, :].bitcast(F32), -1.0))
                    dve.sem_inc(q["weights_split"], 1)
                    layer_stats(dve, ch, xs, D, st)
                    dve.tensor_scalar(w["ve"][:], st["var"][:], EPS, None, ALU.add).then_inc(q["var_ready"], 1)
                    dve.wait_ge(q["rstd_ready"], 1)
                    ch.link(dve.tensor_tensor(w["t1"][:], w["rstd"][:], w["rstd"][:], ALU.mult))
                    ch.link(dve.tensor_tensor(w["t1"][:], w["t1"][:], st["var"][:], ALU.mult))
                    dve.tensor_scalar(w["ve"][:], w["t1"][:], EPS, None, ALU.add).then_inc(q["var2_ready"], 1)
                    dve.wait_ge(q["r2_ready"], 1)
                    ch.link(dve.tensor_tensor(w["t2"][:], w["rs"][:], w["rstd"][:], ALU.mult))

                    def normalise(n, slot):
                        for h in range(HALVES):
                            dve.tensor_scalar(zb[slot][:, h * D:(h + 1) * D], xs[:, ds((n * HALVES + h) * D, D)], mean(n * HALVES + h),
                                              w["t2"][:, ds(n * HALVES + h, 1)], ALU.subtract, ALU.mult).then_inc(q["zb_ready"], 1)

                    def low_x(n, slot):
                        dve.wait_ge(q["xh_ready"], n + 1)
                        dve.tensor_scalar(xf[:], ring[0][:, 0:W], lng[:, 0:1], lnb[:, 0:1], ALU.mult, ALU.add).then_inc(q["xf_ready"], 1)
                        dve.wait_ge(q["xf_ready"], n + 1)
                        dve.tensor_tensor(xl[slot][:], xf[:], xh[slot][:].bitcast(F32), ALU.subtract).then_inc(q["x_ready"], 1)

                    def keys(n, slot):
                        dve.wait_ge(q["kh_ready"], n + 1)
                        dve.scalar_tensor_tensor(out=kl[slot][0:DH, :], in0=ring[0][0:DH, W:2 * W], scalar=SQS,
                                                 in1=kh[slot][0:DH, :].bitcast(F32), op0=ALU.mult, op1=ALU.subtract)
                        dve.tensor_copy(vv[slot][:], ring[0][:, 0:HALVES * DH]).then_inc(q["ring_read"], 1)

                    def low_q(n, slot, u):
                        dve.wait_ge(q["qh_ready"], n * 8 + (2 * u + 2))
                        for par in range(2):
                            src = ring[(1 + u) % 3][par * DH:(par + 1) * DH, :].rearrange("p (k i) -> p k i", k=2)
                            v = qx[slot][:].rearrange("p (k e i) -> p k e i", e=2, i=W)[:, 2 * u:2 * u + 2, par, :]
                            last = dve.scalar_tensor_tensor(out=v[DH:P], in0=src, scalar=SCALE * SQS, in1=v[0:DH].bitcast(F32),
                                                            op0=ALU.mult, op1=ALU.subtract)
                        last.then_inc(q["ring_read"], 1)

                    def maxima(n, m):
                        dve.wait_ge(q["ring_made"], n * UNITS + (6 + m))
                        heads = QG if m < NQ else 2
                        at = m * QG if m < NQ else HEADS + (m - NQ) * 2
                        dve.reduce_max(mx[:, at:at + heads], ring[(5 + m) % 3][:].rearrange("p (e j) -> p e j", e=heads),
                                       AX.X).then_inc(q["ring_read"], 1)

                    def take_max(n):
                        dve.wait_ge(q["ring_made"], n * UNITS + UNITS)
                        if later(n, 1):
                            dve.wait_ge(q["max_loaded"], n * 32)
                        dve.tensor_copy(mts[0:HALVES * HEADS, :], ring[(UNITS - 1) % 3][0:HALVES * HEADS, 0:P]).then_inc(q["mts_ready"], 1)

                    def norm(b, slot, g):
                        dve.wait_ge(q["pv_made"], b * NQ + (g + 1))
                        dve.reciprocal(rec[:], ps_d[:]).then_inc(q["rec_ready"], 1)
                        dve.wait_ge(q["rec_ready"], b * NQ + (g + 1))
                        dve.tensor_tensor(ot[slot][:, g * 2 * W:(g + 1) * 2 * W], ps_o[:], rec[:], ALU.mult).then_inc(q["normed"], 1)

                    def prepare(n, slot):
                        normalise(n, slot)
                        low_x(n, slot)
                        keys(n, slot)
                        for u in range(4):
                            low_q(n, slot, u)
                        for m in range(12):
                            maxima(n, m)
                        take_max(n)

                    def attend(b, slot, prep, before):
                        n, other = b + 1, 1 - slot
                        if prep:
                            normalise(n, other)
                            low_x(n, other)
                            keys(n, other)
                            low_q(n, other, 0)
                            low_q(n, other, 1)
                        norm(b, slot, 0)
                        if prep:
                            low_q(n, other, 2)
                            low_q(n, other, 3)
                        norm(b, slot, 1)
                        if prep:
                            for m in range(6):
                                maxima(n, m)
                        norm(b, slot, 2)
                        if prep:
                            for m in range(6, 12):
                                maxima(n, m)
                            take_max(n)
                        norm(b, slot, 3)
                    batches(dve, prepare, attend)

                    dve.wait_ge(q["proj_read"], B)
                    layer_stats(dve, ch, oa, D, st)
                    dve.tensor_scalar(w["ve"][:], st["var"][:], EPS, None, ALU.add).then_inc(q["var3_ready"], 1)
                    dve.wait_ge(q["rs3_ready"], 1)

                    def scale_rows():
                        tiles(dve, lambda t: dve.tensor_scalar(oa[:, ds(t * D, D)], oa[:, ds(t * D, D)], mean(t), w["rs"][:, ds(t, 1)],
                                                               ALU.subtract, ALU.mult).then_inc(ch.sem, 1))
                        ch.n += NT
                        ch.wait()
                    scale_rows()
                    oat = oa[:].rearrange("p (t d) -> p t d", d=D)
                    ch.link(dve.tensor_tensor(oat, oat, lnog[:].unsqueeze(1).to_broadcast((P, NT, D)), ALU.mult))
                    ch.link(dve.tensor_tensor(oat, oat, lnob[:].unsqueeze(1).to_broadcast((P, NT, D)), ALU.add))
                    layer_stats(dve, ch, oa, D, st)
                    dve.tensor_scalar(w["ve"][:], st["var"][:], EPS, None, ALU.add).then_inc(q["var4_ready"], 1)
                    dve.wait_ge(q["rs4_ready"], 1)
                    scale_rows()
                    ch.link(dve.tensor_tensor(xs[:], xs[:], oa[:], ALU.add))

                @block.scalar
                def _(act):
                    def high_x(n, slot):
                        act.wait_ge(q["z_made"], n + 1)
                        act.activation(xh[slot][:], ring[0][:, 0:W], ACT.Identity, scale=lng[:, 0:1], bias=lnb[:, 0:1]).then_inc(q["xh_ready"], 1)

                    def high_k(n, slot):
                        act.wait_ge(q["ring_made"], n * UNITS + 1)
                        act.activation(kh[slot][:], ring[0][:, W:2 * W], ACT.Copy, scale=SQS).then_inc(q["kh_ready"], 1)

                    def high_q(n, slot, u):
                        act.wait_ge(q["ring_made"], n * UNITS + (2 + u))
                        for par in range(2):
                            src = ring[(1 + u) % 3][par * DH:(par + 1) * DH, :].rearrange("p (k i) -> p k i", k=2)
                            v = qx[slot][0:DH, :].rearrange("p (k e i) -> p k e i", e=2, i=W)[:, 2 * u:2 * u + 2, par, :]
                            act.activation(v, src, ACT.Copy, scale=SCALE * SQS).then_inc(q["qh_ready"], 1)

                    def exponent(b, g):
                        act.wait_ge(q["scores_made"], b * 8 + (2 * g + 1))
                        if later(b, 1) or g >= 2:
                            act.wait_ge(q["pv_made"], b * NQ + (g - 1))
                        act.activation(pt0[g % 2][:], ps_s[:, 0:2 * 512], ACT.Exp).then_inc(q["exp_ready"], 1)
                        act.wait_ge(q["scores_made"], b * 8 + (2 * g + 2))
                        act.activation(pt1[g % 2][:], ps_s[:, 2 * 512:3 * 512], ACT.Exp).then_inc(q["exp_ready"], 1)

                    def take_projection(b):
                        act.wait_ge(q["proj_made"], b + 1)
                        act.activation(oa[:, ds(b * W, W)], ps_d[:, 0:W], ACT.Copy).then_inc(q["proj_read"], 1)

                    def prepare(n, slot):
                        high_x(n, slot)
                        high_k(n, slot)
                        for u in range(4):
                            high_q(n, slot, u)

                    def attend(b, slot, prep, before):
                        n, other = b + 1, 1 - slot
                        exponent(b, 0)
                        if before:
                            take_projection(b - 1)
                        if prep:
                            high_x(n, other)
                            high_k(n, other)
                            high_q(n, other, 0)
                            high_q(n, other, 1)
                        exponent(b, 1)
                        if prep:
                            high_q(n, other, 2)
                            high_q(n, other, 3)
                        exponent(b, 2)
                        exponent(b, 3)
                    act.wait_ge(attn_loaded, 16 * 8)
                    batches(act, prepare, attend)
                    take_projection(B - 1)

                @block.tensor
                def _(pe):
                    def three(out_ap, lhs, rhs, start=True):
                        (lh, ll), (rh, rl) = lhs, rhs
                        pe.matmul(out_ap, lh, rl, start=start, stop=False, skip_group_check=True)
                        pe.matmul(out_ap, ll, rh, start=False, stop=False, skip_group_check=True)
                        return pe.matmul(out_ap, lh, rh, start=False, stop=True, skip_group_check=True)

                    def keys(n, slot):
                        pe.wait_ge(q["zb_ready"], n * HALVES + HALVES)
                        wait_unit(n, 0)
                        for h in range(HALVES):
                            last = pe.transpose(ring[0][:, h * P:(h + 1) * P], zb[slot][:, h * D:(h + 1) * D], ident[:])
                        last.then_inc(q["z_made"], 1)
                        pe.wait_ge(q["x_ready"], n + 1)
                        three(ring[0][:, W:2 * W], (wkh[:], wkl[:]), (xh[slot][:], xl[slot][:]))
                        for h in range(HALVES):
                            c = slice(h * P, (h + 1) * P)
                            last = three(ring[0][:, h * DH:(h + 1) * DH], (xh[slot][:, c], xl[slot][:, c]), (wvh[:], wvl[:]))
                        last.then_inc(q["ring_made"], 1)

                    def queries(n, slot, u):
                        k = 1 + u
                        wait_unit(n, k)
                        for j in range(2):
                            c = slice((2 * u + j) * P, (2 * u + j + 1) * P)
                            last = three(ring[k % 3][:, j * W:(j + 1) * W], (wqh[:, c], wql[:, c]), (xh[slot][:], xl[slot][:]))
                        last.then_inc(q["ring_made"], 1)

                    def wait_unit(n, k):
                        if k >= 3:
                            pe.wait_ge(q["ring_read"], n * 17 + (k - 2))
                        elif later(n, 1):
                            if k == 2:
                                pe.wait_ge(q["mts_ready"], n)
                            else:
                                pe.wait_ge(q["ring_read"], n * 17 + (k - 1))

                    def maxima(n, slot, m):
                        k = 5 + m
                        wait_unit(n, k)
                        if m == 0:
                            pe.wait_ge(q["ring_read"], n * 17 + 5)
                        bank = ring[k % 3]
                        if m < NQ:
                            for j in range(QG):
                                h = m * QG + j
                                pe.matmul(bank[:, j * P:(j + 1) * P], qx[slot][:, h * W:h * W + P], kh[slot][:, 0:P],
                                          start=(j == 0), stop=False, skip_group_check=True)
                            last = pe.matmul(bank[:], ident_r[:], causal_r[:], start=False, stop=True, skip_group_check=True)
                        else:
                            for j in range(2):
                                h = (m - NQ) * 2 + j
                                pe.matmul(bank[:, j * W:(j + 1) * W], qx[slot][:, h * W + P:(h + 1) * W], kh[slot][:],
                                          start=(j == 0), stop=False, skip_group_check=True)
                            last = pe.matmul(bank[:].rearrange("p (e j) -> p e j", e=2)[:, :, P:W], ident_r[:],
                                             causal_r[:, 0:2 * P].rearrange("p (e j) -> p e j", e=2), start=False, stop=True,
                                             skip_group_check=True)
                        last.then_inc(q["ring_made"], 1)

                    def turn_max(n):
                        pe.wait_ge(q["ring_read"], n * 17 + 17)
                        pe.transpose(ring[(UNITS - 1) % 3][0:HALVES * HEADS, 0:P], mx[:], ident[:]).then_inc(q["ring_made"], 1)

                    def scores(b, slot, g):
                        if g == 0:
                            pe.wait_ge(q["max_loaded"], b * 32 + 32)
                            pe.wait_ge(q["qm_ready"], b * 4 + 4)
                            if later(b, 1):
                                pe.wait_ge(q["exp_ready"], b * 8)
                        else:
                            pe.wait_ge(q["exp_ready"], b * 8 + 2 * g)
                        for half in range(2):
                            c = slice((QG * g + 2 * half) * W, (QG * g + 2 * half + 2) * W)
                            o = ps_s[:, half * 512:(half + 1) * 512]
                            pe.matmul(o, kh[slot][:, 0:P], qx[slot][:, c], start=True, stop=False)
                            last = pe.matmul(o, kl[slot][:, 0:P], qm[slot][:, c], start=False, stop=True)
                        last.then_inc(q["scores_made"], 1)
                        o = ps_s[:, 2 * 512:3 * 512]

                        def second(t):
                            return t[:, QG * g * W:QG * (g + 1) * W].rearrange("p (e i) -> p e i", i=W)[:, :, P:W]
                        pe.matmul(o, kh[slot][:, P:W], second(qx[slot]), start=True, stop=False)
                        pe.matmul(o, kl[slot][:, P:W], second(qm[slot]), start=False, stop=True).then_inc(q["scores_made"], 1)

                    def values(b, slot, g):
                        pe.wait_ge(q["masked"], b * 8 + (2 * g + 2))
                        if g >= 1:
                            pe.wait_ge(q["normed"], b * NQ + g)
                        elif later(b, 1):
                            pe.wait_ge(q["proj_read"], b)
                        p0 = pt0[g % 2][:].rearrange("p (k e i) -> p k e i", e=2, i=W)
                        p1 = pt1[g % 2][:].rearrange("p (k e i) -> p k e i", e=2, i=P)
                        for o, first, second in ((ps_o, vv[slot][:, 0:DH], vv[slot][:, DH:2 * DH]), (ps_d, ones[:, 0:DH], ones[:, 0:DH])):
                            for par in range(2):
                                rows_ = o[par * DH:(par + 1) * DH, :]
                                pe.matmul(rows_, first, p0[:, :, par, :], start=True, stop=False, skip_group_check=True)
                            for par in range(2):
                                rows_ = o[par * DH:(par + 1) * DH, :].rearrange("p (k i) -> p k i", k=2)[:, :, P:W]
                                last = pe.matmul(rows_, second, p1[:, :, par, :], start=False, stop=True, skip_group_check=True)
                        last.then_inc(q["pv_made"], 1)

                    def project(b, slot):
                        pe.wait_ge(q["normed"], b * NQ + NQ)
                        for h in range(HALVES):
                            for k in range(PAIRS):
                                last = pe.matmul(ps_d[:, h * D:(h + 1) * D], ot[slot][:, k * W + h * P:k * W + (h + 1) * P],
                                                 wo[:, k * D:(k + 1) * D], start=(k == 0), stop=(k == PAIRS - 1), skip_group_check=True)
                        last.then_inc(q["proj_made"], 1)

                    def prepare(n, slot):
                        keys(n, slot)
                        for u in range(4):
                            queries(n, slot, u)
                        for m in range(12):
                            maxima(n, slot, m)
                        turn_max(n)

                    def attend(b, slot, prep, before):
                        n, other = b + 1, 1 - slot
                        scores(b, slot, 0)
                        if before:
                            project(b - 1, other)
                        if prep:
                            keys(n, other)
                            queries(n, other, 0)
                            queries(n, other, 1)
                        scores(b, slot, 1)
                        values(b, slot, 0)
                        if prep:
                            queries(n, other, 2)
                            queries(n, other, 3)
                        scores(b, slot, 2)
                        values(b, slot, 1)
                        if prep:
                            for m in range(6):
                                maxima(n, other, m)
                        scores(b, slot, 3)
                        values(b, slot, 2)
                        if prep:
                            for m in range(6, 12):
                                maxima(n, other, m)
                            turn_max(n)
                        values(b, slot, 3)
                    pe.wait_ge(q["weights_split"], 1)
                    batches(pe, prepare, attend)
                    project(B - 1, 1)

        with ExitStack() as ph:
            full = {n: sb("full_" + n, c, F32, ph) for n, c in
                    [("f1", HID), ("f2", HID), ("h1", HC * HID), ("h2", HC * HID), ("f3", HC * D)]}
            high = {n: sb("high_" + n, c, F32R, ph) for n, c in
                    [("f1", HID), ("f2", HID), ("h1", HC * HID), ("h2", HC * HID), ("f3", HC * D)]}
            low = {n: sb("low_" + n, c, F32R, ph) for n, c in
                   [("f1", HID), ("f2", HID), ("h1", HC * HID), ("h2", HC * HID), ("f3", HC * D)]}
            scl = {n: sb("scl_" + n, HC, F32, ph) for n in ["f1", "f2", "h1", "h2"]}
            scl3 = sb("scl3", D, F32, ph)
            zb = [sb(f"fz{i}", GW, F32, ph) for i in range(2)]
            zh = [sb(f"fzh{i}", GW, F32R, ph) for i in range(2)]
            zl = [sb(f"fzl{i}", GW, F32R, ph) for i in range(2)]
            gate = [sb(f"gate{i}", GW, F32, ph) for i in range(HC)]
            hid = [sb(f"hid{i}", GW, F32, ph) for i in range(HC)]
            hh = [[sb(f"hh{i}{c}", GW, F32R, ph) for c in range(HC)] for i in range(2)]
            hl = [[sb(f"hl{i}{c}", GW, F32R, ph) for c in range(HC)] for i in range(2)]
            oa = sb("ffn_out", NT * D, F32, ph)
            bank_a = [psum(f"bank_a{i}", 1, ph) for i in range(HC)]
            bank_b = [psum(f"bank_b{i}", 1, ph) for i in range(HC)]
            names = ["loaded", "dve_done", "weights_split", "var_ready", "rstd_ready", "zb_ready", "z_made", "zh_ready", "z_ready",
                     "made", "act_ready", "hid_ready", "high_ready", "split_ready", "out_read", "raw_ready", "var2_ready", "rs_ready", "x_ready"]
            q = {n: sem("d_" + n, ph) for n in names}
            CH = 3 * HC
            with nc.Block() as block:
                @block.sync
                def _(sp):
                    for dst, src in ((full["f1"][:], f1t), (full["f2"][:], f2t), (full["h1"][:], h1t), (full["h2"][:], h2t),
                                     (full["f3"][:], f3t), (scl["f1"][:], f1s), (scl["f2"][:], f2s), (scl["h1"][:], h1s),
                                     (scl["h2"][:], h2s), (scl3[:], broadcast(f3s, D))):
                        sp.dma_start(dst, src).then_inc(q["loaded"], 16)
                    for c in range(4):
                        sp.wait_ge(q["x_ready"], c + 1)
                        sp.dma_start(out.rearrange("b (h p) d -> p (b h) d", p=P)[:, c * 8:(c + 1) * 8, :],
                                     xs[:, c * 8 * D:(c + 1) * 8 * D].rearrange("p (t d) -> p t d", d=D)).then_inc(all_stored, 16)
                    sp.wait_ge(all_stored, 64)

                @block.gpsimd
                def _(pool):
                    pool.wait_ge(q["var_ready"], 1)
                    pool.tensor_tensor(small["rstd"][:], small["ve"][:], neg_half[:], ALU.pow).then_inc(q["rstd_ready"], 1)
                    pool.wait_ge(q["var2_ready"], 1)
                    pool.tensor_tensor(small["rs"][:], small["ve"][:], neg_half[:], ALU.pow).then_inc(q["rs_ready"], 1)

                @block.vector
                def _(dve):
                    ch = Chain(dve, q["dve_done"])
                    w = small
                    layer_stats(dve, ch, xs, D, st)
                    dve.tensor_scalar(w["ve"][:], st["var"][:], EPS, None, ALU.add).then_inc(q["var_ready"], 1)
                    dve.wait_ge(q["loaded"], 16 * 10)
                    for n in ("f1", "f2", "h1", "h2", "f3"):
                        ch.link(dve.tensor_copy(high[n][:], full[n][:]))
                        dve.tensor_tensor(low[n][:], full[n][:], high[n][:].bitcast(F32), ALU.subtract).then_inc(q["weights_split"], 1)
                    dve.wait_ge(q["rstd_ready"], 1)

                    def normalise(g, slot):
                        if later(g, 2):
                            dve.wait_ge(q["z_made"], g - 1)
                        for j in range(GT):
                            dve.tensor_scalar(zb[slot][:, j * D:(j + 1) * D], xs[:, ds((g * GT + j) * D, D)], mean(g * GT + j),
                                              w["rstd"][:, ds(g * GT + j, 1)], ALU.subtract, ALU.mult).then_inc(q["zb_ready"], 1)

                    def low_z(g, slot):
                        dve.wait_ge(q["zh_ready"], g + 1)
                        dve.tensor_tensor(zl[slot][:], bank_a[2][:], zh[slot][:].bitcast(F32), ALU.subtract).then_inc(q["z_ready"], 1)

                    def split(g, layer, c):
                        to = layer % 2
                        dve.tensor_copy(hh[to][c][:], hid[c][:]).then_inc(q["high_ready"], 1)
                        dve.wait_ge(q["high_ready"], g * CH + (layer * HC + c + 1))
                        dve.tensor_tensor(hl[to][c][:], hid[c][:], hh[to][c][:].bitcast(F32), ALU.subtract).then_inc(q["split_ready"], 1)

                    def layers(g, slot):
                        for c in range(HC):
                            dve.wait_ge(q["act_ready"], g * CH + (c + 1))
                            dve.scalar_tensor_tensor(out=hid[c][:], in0=bank_b[c][:], scalar=scl["f2"][:, c:c + 1], in1=gate[c][:],
                                                     op0=ALU.mult, op1=ALU.mult).then_inc(q["hid_ready"], 1)
                            dve.wait_ge(q["hid_ready"], g * HC + (c + 1))
                            split(g, 0, c)
                        for layer in (1, 2):
                            for c in range(HC):
                                dve.wait_ge(q["act_ready"], g * CH + (layer * HC + c + 1))
                                split(g, layer, c)

                    def take_out(g, slot):
                        dve.wait_ge(q["made"], g * (CH + 1) + (CH + 1))
                        dve.tensor_tensor(oa[:, ds(g * GW, GW)].rearrange("p (t d) -> p t d", d=D),
                                          bank_a[3][:].rearrange("p (t d) -> p t d", d=D),
                                          scl3[:].unsqueeze(1).to_broadcast((P, GT, D)), ALU.mult).then_inc(q["out_read"], 1)
                        dve.wait_ge(q["out_read"], g + 1)
                        for j in range(GT):
                            dve.bn_stats(st["raw"][:, ds((g * GT + j) * 6, 6)], oa[:, ds((g * GT + j) * D, D)]).then_inc(q["raw_ready"], 1)

                    def step(g, slot, more=True):
                        if more:
                            normalise(g + 1, 1 - slot)
                        layers(g, slot)
                        if more:
                            low_z(g + 1, 1 - slot)
                        take_out(g, slot)
                    normalise(0, 0)
                    low_z(0, 0)
                    groups(dve, step)
                    dve.wait_ge(q["raw_ready"], NT)
                    combine_stats(ch, st)
                    dve.tensor_scalar(w["ve"][:], st["var"][:], EPS, None, ALU.add).then_inc(q["var2_ready"], 1)
                    dve.wait_ge(q["rs_ready"], 1)
                    tiles(dve, lambda t: dve.tensor_scalar(oa[:, ds(t * D, D)], oa[:, ds(t * D, D)], mean(t), w["rs"][:, ds(t, 1)],
                                                           ALU.subtract, ALU.mult).then_inc(ch.sem, 1))
                    ch.n += NT
                    ch.wait()
                    for c in range(4):
                        v = slice(c * 8 * D, (c + 1) * 8 * D)
                        dve.tensor_tensor(xs[:, v], xs[:, v], oa[:, v], ALU.add).then_inc(q["x_ready"], 1)

                @block.scalar
                def _(act):
                    def high_z(g, slot):
                        act.wait_ge(q["z_made"], g + 1)
                        act.activation(zh[slot][:], bank_a[2][:], ACT.Copy).then_inc(q["zh_ready"], 1)

                    def curve(g, layer, c):
                        act.wait_ge(q["made"], g * (CH + 1) + (layer * HC + c + 1))
                        if layer:
                            act.wait_ge(q["split_ready"], g * CH + ((layer - 1) * HC + c + 1))
                        src = (bank_a, bank_a, bank_b)[layer][c]
                        scale = scl[("f1", "h1", "h2")[layer]][:, c:c + 1]
                        act.activation((hid if layer else gate)[c][:], src[:], ACT.Gelu if layer else ACT.Silu,
                                       scale=scale).then_inc(q["act_ready"], 1)

                    def step(g, slot, more=True):
                        for layer in range(3):
                            for c in range(HC):
                                curve(g, layer, c)
                        if more:
                            high_z(g + 1, 1 - slot)
                    act.wait_ge(q["loaded"], 16 * 10)
                    high_z(0, 0)
                    groups(act, step)

                @block.tensor
                def _(pe):
                    def three(out_ap, lhs, rhs, start=True, stop=True):
                        (lh, ll), (rh, rl) = lhs, rhs
                        pe.matmul(out_ap, lh, rl, start=start, stop=False, skip_group_check=True)
                        pe.matmul(out_ap, ll, rh, start=False, stop=False, skip_group_check=True)
                        return pe.matmul(out_ap, lh, rh, start=False, stop=stop, skip_group_check=True)

                    def turn(g, slot):
                        pe.wait_ge(q["zb_ready"], g * GT + GT)
                        for j in range(GT):
                            last = pe.transpose(bank_a[2][:, j * P:(j + 1) * P], zb[slot][:, j * D:(j + 1) * D], ident[:])
                        last.then_inc(q["z_made"], 1)

                    def gated(g, slot):
                        pe.wait_ge(q["z_ready"], g + 1)
                        for c in range(HC):
                            if c == 3 and later(g, 1):
                                pe.wait_ge(q["out_read"], g)
                            m = slice(c * P, (c + 1) * P)
                            for o, n in ((bank_a[c], "f1"), (bank_b[c], "f2")):
                                last = three(o[:], (high[n][:, m], low[n][:, m]), (zh[slot][:], zl[slot][:]))
                            last.then_inc(q["made"], 1)

                    def hidden(g, layer):
                        n, banks, src = ("h1", bank_a, 0) if layer == 1 else ("h2", bank_b, 1)
                        for k in range(HC):
                            pe.wait_ge(q["split_ready"], g * CH + ((layer - 1) * HC + k + 1))
                            for c in range(HC):
                                if layer == 1 and k == 0 and c:
                                    pe.wait_ge(q["split_ready"], g * CH + (c + 1))
                                m = slice(k * HID + c * P, k * HID + (c + 1) * P)
                                last = three(banks[c][:], (high[n][:, m], low[n][:, m]), (hh[src][k][:], hl[src][k][:]),
                                             start=(k == 0), stop=(k == HC - 1))
                                if k == HC - 1:
                                    last.then_inc(q["made"], 1)

                    def outward(g):
                        pe.wait_ge(q["split_ready"], g * CH + CH)
                        for t in range(GT):
                            for k in range(HC):
                                m = slice(t * P, (t + 1) * P)
                                last = three(bank_a[3][:, m], (hh[0][k][:, m], hl[0][k][:, m]),
                                             (high["f3"][:, k * D:(k + 1) * D], low["f3"][:, k * D:(k + 1) * D]),
                                             start=(k == 0), stop=(k == HC - 1))
                        last.then_inc(q["made"], 1)

                    def step(g, slot, more=True):
                        gated(g, slot)
                        hidden(g, 1)
                        hidden(g, 2)
                        if more:
                            turn(g + 1, 1 - slot)
                        outward(g)
                    pe.wait_ge(q["weights_split"], 5)
                    turn(0, 0)
                    groups(pe, step)


def constants():
    import numpy as np
    r = np.arange(P)
    c = {}
    c["diff"] = (r[:, None] == r[None, :] + 1) * 1.0 - (r[:, None] == r[None, :]) * 1.0
    c["cross"] = ((r[:, None] == 0) & (r[None, :] == P - 1)) * 1.0
    window = min(8, S - 1)
    band = np.zeros((S, S), np.float32)
    for s in range(1, S):
        w = min(s, window)
        for j in range(w):
            band[s - w + j, s] = np.float32(0.1) + np.float32(0.9) * np.float32(j) / np.float32(max(w - 1, 1)) if w > 1 else 0.1
    c["band00"], c["band10"], c["band11"] = band[:P, :P], band[:P, P:], band[P:, P:]
    c["causal"] = np.where(r[None, :] > r[:, None], MASKED, 0.0)
    c["before"] = (r[:, None] < r[None, :]) * 1.0
    e = np.arange(EXPERTS)
    low = np.zeros((P, P))
    low[:, :EXPERTS * EXPERTS] = (e[None, :] < e[:, None]).reshape(1, -1)
    low[:, EXPERTS * EXPERTS:EXPERTS * EXPERTS + EXPERTS] = e + 1
    c["lower_e"] = low
    c["tile_no"] = np.broadcast_to(r[None, :], (P, P))
    return np.concatenate([c[n] for n in CONSTS], axis=1).astype(np.float32)


def kernel(**inputs):
    import numpy as np
    import concourse.bacc as bacc
    from concourse.bass_utils import run_bass_kernel_spmd as run

    a = {n: np.asarray(v) for n, v in inputs.items()}
    wkt, wvt = a["L1_attn_w_kv"][:DH].T, a["L1_attn_w_kv"][DH:].T

    def chunked(w):
        return w.T.reshape(-1, P, w.shape[0]).transpose(1, 0, 2).reshape(P, -1)

    def columns(v):
        return v.reshape(-1, P).T

    laid = [
        a["L0_attn_embeddings"], a["L0_attn_guidance_trajectories"],
        a["L0_ffn_gate_w"].T, a["L0_ffn_gate_b"],
        a["L0_ffn_w1"].transpose(2, 0, 1).reshape(D, -1), a["L0_ffn_b1"].reshape(-1),
        a["L0_ffn_w2"].reshape(EXPERTS, D, HC, P).transpose(3, 0, 2, 1).reshape(P, -1), a["L0_ffn_b2"].reshape(-1),
        a["L1_attn_w_q"].T, np.concatenate([wkt, wkt], axis=1), wvt, chunked(a["L1_attn_w_out"]),
        a["L1_attn_ln_g"].reshape(P, 1), a["L1_attn_ln_b"].reshape(P, 1), a["L1_attn_lno_g"], a["L1_attn_lno_b"],
        a["L1_ffn_w1_w"].T, columns(a["L1_ffn_w1_s"]), a["L1_ffn_w2_w"].T, columns(a["L1_ffn_w2_s"]),
        chunked(a["L1_ffn_h1_w"]), columns(a["L1_ffn_h1_s"]), chunked(a["L1_ffn_h2_w"]), columns(a["L1_ffn_h2_s"]),
        chunked(a["L1_ffn_w3_w"]), a["L1_ffn_w3_s"],
        constants(),
    ]
    nc = bacc.Bacc("TRN2", target_bir_lowering=False, num_devices=1)
    arrays, args = {}, []
    for i, v in enumerate(laid):
        v = np.ascontiguousarray(v)
        arrays[f"in_{i}"] = v
        args.append(nc.dram_tensor(f"in_{i}", v.shape, mybir.dt.from_np(v.dtype), kind="ExternalInput").ap())
    args.append(nc.dram_tensor("out_0", (B, S, D), F32, kind="ExternalOutput").ap())
    program(nc, *args)
    return run(nc, [arrays], core_ids=[0]).results[0]["out_0"]
```

```python
from contextlib import ExitStack

import concourse.bass as bass
from concourse import mybir

F32 = mybir.dt.float32
F32R = mybir.dt.float32r
I32 = mybir.dt.int32
U32 = mybir.dt.uint32
ALU = mybir.AluOpType
ACT = mybir.ActivationFunctionType
AX = mybir.AxisListType
PE_ENGINE = [mybir.EngineType.PE]
DVE_ENGINE = [mybir.EngineType.DVE]

P = 128
B, S, D = 16, 256, 128
HALVES = S // P
NT = B * HALVES
GT = 4
NG = NT // GT
GW = GT * D
GUIDES = 64
ZW = D + 1
EXPERTS = 8
HID = 4 * D
HC = HID // P
NS = NT + EXPERTS - 1
HEADS, DH = 16, 64
PAIRS = HEADS // 2
QG = 4
NQ = HEADS // QG
EPS = 1e-5
GUIDE_W = 0.4
EPS_MAG = 1e-6
EPS_COS = 1e-8
EPS_WSUM = 1e-8
SCALE = DH ** -0.5
MASKED = -1e30
CONSTS = ["diff", "cross", "band00", "band10", "band11", "causal", "before", "lower_e", "tile_no"]


def ds(start, size):
    return bass.ds(start, size)


def skewed(eng, n, unroll, *stages):
    reach = max(lag for lag, _ in stages)
    first = -(-(reach + unroll) // unroll) * unroll
    for s in range(first):
        for lag, f in stages:
            if s >= lag:
                f(s - lag, (s - lag) % unroll)
    with eng.Fori(first // unroll, n // unroll) as i:
        for u in range(unroll):
            for lag, f in stages:
                f(i * unroll + (u - lag), (u - lag) % unroll)
    for s in range(n, n + reach):
        for lag, f in stages:
            if s - lag < n:
                f(s - lag, (s - lag) % unroll)


def later(g, n):
    return not isinstance(g, int) or g >= n


def groups(eng, step):
    step(0, 0)
    step(1, 1)
    with eng.Fori(1, NG // 2 - 1) as i:
        step(i * 2, 0)
        step(i * 2 + 1, 1)
    step(NG - 2, 0)
    step(NG - 1, 1, False)


def tiles(eng, f, unroll=4):
    with eng.Fori(0, NT // unroll) as i:
        for u in range(unroll):
            f(i * unroll + u)


class Chain:

    def __init__(self, eng, sem):
        self.eng, self.sem, self.n = eng, sem, 0

    def add(self, ins, n=1):
        ins.then_inc(self.sem, 1)
        self.n += n

    def wait(self):
        self.eng.wait_ge(self.sem, self.n)

    def link(self, ins):
        self.add(ins)
        self.wait()


def layer_stats(dve, ch, src, width, st):
    tiles(dve, lambda t: dve.bn_stats(st["raw"][:, ds(t * 6, 6)], src[:, ds(t * width, D)]).then_inc(ch.sem, 1))
    ch.n += NT
    ch.wait()
    combine_stats(ch, st)


def combine_stats(ch, st):
    dve = ch.eng
    raw = st["raw"][:].rearrange("p (t k) -> p t k", k=6)
    dve.tensor_tensor(st["mean"][:], raw[:, :, 1], raw[:, :, 4], ALU.add).then_inc(ch.sem, 1)
    dve.tensor_tensor(st["diff"][:], raw[:, :, 1], raw[:, :, 4], ALU.subtract).then_inc(ch.sem, 1)
    dve.tensor_tensor(st["var"][:], raw[:, :, 2], raw[:, :, 5], ALU.add).then_inc(ch.sem, 1)
    ch.n += 3
    ch.wait()
    dve.tensor_scalar(st["mean"][:], st["mean"][:], 0.5, None, ALU.mult).then_inc(ch.sem, 1)
    dve.scalar_tensor_tensor(out=st["diff"][:], in0=st["diff"][:], scalar=0.25, in1=st["diff"][:], op0=ALU.mult,
                             op1=ALU.mult).then_inc(ch.sem, 1)
    ch.n += 2
    ch.wait()
    ch.link(dve.scalar_tensor_tensor(out=st["var"][:], in0=st["var"][:], scalar=1.0 / D, in1=st["diff"][:], op0=ALU.mult,
                                     op1=ALU.add))


def program(nc, x, guides, gate_wt, gate_b, w1t, b1, w2t, b2, wqt, wkt2, wvt, wot, ln_g, ln_b, lno_g, lno_b,
            f1t, f1s, f2t, f2s, h1t, h1s, h2t, h2s, f3t, f3s, consts, out):
    sorted_x = nc.dram_tensor("sorted_x", (NS * P, D), F32).ap()
    sorted_y = nc.dram_tensor("sorted_y", (NS * P, D), F32).ap()
    with ExitStack() as whole:
        def sem(name, stack=whole):
            return stack.enter_context(nc.semaphore(name))

        def sb(name, cols, dt=F32, stack=whole):
            return stack.enter_context(nc.sbuf_tensor(name, [P, cols], dt))

        def psum(name, banks, stack):
            return stack.enter_context(nc.psum_tensor(name, [P, banks * 512], F32))

        xs = sb("xs", NT * D)
        ident = sb("ident", P)
        neg_half = sb("neg_half", NT)
        half = sb("half", NT)
        st = {"raw": sb("stats_raw", NT * 6), "mean": sb("stats_mean", NT), "var": sb("stats_var", NT),
              "diff": sb("stats_diff", NT)}

        def mean(t):
            return st["mean"][:, ds(t, 1)]

        small = {n: sb("small_" + n, NT) for n in
                 ["ve", "rstd", "mag2", "mag", "inv", "ra", "an", "mw", "c6", "wsum", "rs", "t1", "t2"]}
        cb = sb("consts_sb", len(CONSTS) * P)
        const = {n: cb[:, i * P:(i + 1) * P] for i, n in enumerate(CONSTS)}
        ones = sb("ones", P)
        slot_i = sb("slot_i", NT, I32)
        mv_all = sb("mv_all", NT * 2)
        x_loaded, consts_loaded, setup_done = sem("x_loaded"), sem("consts_loaded"), sem("setup_done")
        moe_loaded, attn_loaded, ffn_loaded = sem("moe_loaded"), sem("attn_loaded"), sem("ffn_loaded")
        sorted_zeroed = sem("sorted_zeroed")
        all_stored = sem("all_stored")

        wq = sb("wq", HEADS * DH)
        wk2 = sb("wk2", P)
        wv = sb("wv", DH)
        wo = sb("wo", PAIRS * D)
        lng, lnb = sb("lng", 1), sb("lnb", 1)
        lnog, lnob = sb("lnog", D), sb("lnob", D)

        def broadcast(ap, n):
            return ap.rearrange("(a n) -> a n", a=1).to_broadcast((P, n))

        moe = ExitStack()
        w1 = sb("w1", EXPERTS * HID, stack=moe)
        w2 = sb("w2", EXPERTS * HID, stack=moe)
        b1s = sb("b1s", EXPERTS * HID, stack=moe)
        b2s = sb("b2s", EXPERTS * D, stack=moe)
        gw = sb("gw", EXPERTS, stack=moe)
        gb = sb("gb", EXPERTS, stack=moe)
        rows = sb("rows", NS * D, stack=moe)
        MOE_LOADS = 6

        with ExitStack() as ph:
            y = sb("y", NT * D, stack=ph)
            dif = sb("dif", NT * D, stack=ph)
            sq = [sb(f"sq{i}", GW, stack=ph) for i in range(2)]
            z = sb("z", NT * ZW, stack=ph)
            zt = z[:].rearrange("p (t k) -> p t k", k=ZW)
            nh = [sb(f"nh{i}", GW, stack=ph) for i in range(2)]
            nht = [sb(f"nht{i}", GW, stack=ph) for i in range(2)]
            et = [sb(f"et{i}", GW, stack=ph) for i in range(2)]
            guide = sb("guide", ZW, stack=ph)
            guide_n = sb("guide_n", D, stack=ph)
            guide_sq = sb("guide_sq", D, stack=ph)
            gt = sb("gt", GUIDES, stack=ph)
            gs = sb("gs", 4, stack=ph)
            c4 = [sb(f"c4{i}", GT, stack=ph) for i in range(2)]
            u = sb("u", NT * ZW, stack=ph)
            ut = u[:].rearrange("p (t k) -> p t k", k=ZW)
            ps_a = [psum(f"ps_a{i}", 1, ph) for i in range(2)]
            ps_s = [psum(f"ps_s{i}", 1, ph) for i in range(2)]
            ps_i = [psum(f"ps_i{i}", 2, ph) for i in range(2)]
            names = ["dve_done", "guide_loaded", "guide_mag2", "guide_mag", "guide_scaled", "guide_t", "guide_ready",
                     "var_ready", "rstd_ready", "y_ready", "diff_made", "diff_copied", "sq_free", 
                     "mag_ready", "mag_for_tanh", "tanh_ready", "nh_ready", "nht_made", "nht_ready", "sims_made",
                     "exp_ready", "infl_made", "infl_free", "z_ready", "u_made", "u_ready", "var2_ready",
                     "rs_ready", "et_zero", "sq_ready"]
            q = {n: sem("a_" + n, ph) for n in names}
            with nc.Block() as block:
                @block.sync
                def _(sp):
                    for c in range(4):
                        sp.dma_start(xs[:, c * 8 * D:(c + 1) * 8 * D].rearrange("p (t d) -> p t d", d=D),
                                     x.rearrange("b (h p) d -> p (b h) d", p=P)[:, c * 8:(c + 1) * 8, :]).then_inc(x_loaded, 16)
                    sp.dma_start(cb[:], consts).then_inc(consts_loaded, 16)
                    sp.dma_start(guide[0:GUIDES, 0:D], guides).then_inc(q["guide_loaded"], 16)
                    sp.wait_ge(setup_done, 6)
                    sp.dma_start(sorted_x.rearrange("(k p) d -> p k d", p=P),
                                 rows[:].rearrange("p (k d) -> p k d", d=D)).then_inc(sorted_zeroed, 16)
                    for dst, src in ((w1[:], w1t), (w2[:], w2t), (b1s[:], broadcast(b1, EXPERTS * HID)),
                                     (b2s[:], broadcast(b2, EXPERTS * D)), (gw[:], gate_wt),
                                     (gb[:], broadcast(gate_b, EXPERTS))):
                        sp.dma_start(dst, src).then_inc(moe_loaded, 16)
                    for dst, src in ((wq[:], wqt), (wk2[:], wkt2), (wv[:], wvt), (wo[:], wot), (lng[:], ln_g), (lnb[:], ln_b),
                                     (lnog[:], broadcast(lno_g, D)), (lnob[:], broadcast(lno_b, D))):
                        sp.dma_start(dst, src).then_inc(attn_loaded, 16)
                    sp.wait_ge(consts_loaded, 16)
                    sp.wait_ge(sorted_zeroed, 16)

                @block.gpsimd
                def _(pool):
                    pool.memset(neg_half[:], -0.5).then_inc(setup_done, 1)
                    pool.memset(half[:], 0.5).then_inc(setup_done, 1)
                    pool.memset(ident[:], 0.0).then_inc(setup_done, 1)
                    pool.memset(ones[:], 1.0).then_inc(setup_done, 1)
                    pool.wait_ge(setup_done, 4)
                    pool.affine_select(out=ident[:], in_=ident[:], compare_op=ALU.not_equal, fill=1.0, base=0,
                                       pattern=[[-1, P]], channel_multiplier=1).then_inc(setup_done, 1)
                    pool.memset(rows[:], 0.0).then_inc(setup_done, 1)
                    pool.wait_ge(q["guide_mag2"], 1)
                    pool.tensor_tensor(gs[0:GUIDES, 1:2], gs[0:GUIDES, 0:1], half[0:GUIDES, 0:1], ALU.pow).then_inc(q["guide_mag"], 1)
                    pool.wait_ge(q["var_ready"], 1)
                    pool.tensor_tensor(small["rstd"][:], small["ve"][:], neg_half[:], ALU.pow).then_inc(q["rstd_ready"], 1)
                    pool.wait_ge(q["sq_free"], NG)
                    pool.tensor_tensor(small["mag"][:], small["mag2"][:], half[:], ALU.pow).then_inc(q["mag_ready"], 1)
                    pool.wait_ge(q["var2_ready"], 1)
                    pool.tensor_tensor(small["rs"][:], small["ve"][:], neg_half[:], ALU.pow).then_inc(q["rs_ready"], 1)

                @block.vector
                def _(dve):
                    ch = Chain(dve, q["dve_done"])
                    dve.memset(guide[GUIDES:P, :], 0.0).then_inc(q["et_zero"], 1)
                    for i in range(2):
                        dve.memset(et[i][GUIDES:P, :], 0.0).then_inc(q["et_zero"], 1)
                    dve.wait_ge(q["guide_loaded"], 16)
                    ch.link(dve.tensor_tensor(guide_sq[0:GUIDES, :], guide[0:GUIDES, 0:D], guide[0:GUIDES, 0:D], ALU.mult))
                    ch.link(dve.memset(guide[0:GUIDES, D:ZW], 1.0))
                    dve.reduce_sum(gs[0:GUIDES, 0:1], guide_sq[0:GUIDES, :], AX.X).then_inc(q["guide_mag2"], 1)
                    dve.wait_ge(x_loaded, 64)
                    layer_stats(dve, ch, xs, D, st)
                    dve.tensor_scalar(small["ve"][:], st["var"][:], EPS, None, ALU.add).then_inc(q["var_ready"], 1)
                    dve.wait_ge(q["guide_mag"], 1)
                    ch.link(dve.tensor_scalar(gs[0:GUIDES, 2:3], gs[0:GUIDES, 1:2], EPS_COS, None, ALU.max))
                    ch.link(dve.reciprocal(gs[0:GUIDES, 3:4], gs[0:GUIDES, 2:3]))
                    dve.tensor_scalar(guide_n[0:GUIDES, :], guide[0:GUIDES, 0:D], gs[0:GUIDES, 3:4], None,
                                      ALU.mult).then_inc(q["guide_scaled"], 1)
                    dve.wait_ge(q["rstd_ready"], 1)
                    tiles(dve, lambda t: dve.tensor_scalar(y[:, ds(t * D, D)], xs[:, ds(t * D, D)], mean(t),
                                                           small["rstd"][:, ds(t, 1)], ALU.subtract,
                                                           ALU.mult).then_inc(q["y_ready"], 1))

                    def mag2(g, slot):
                        dve.wait_ge(q["sq_ready"], g + 1)
                        dve.reduce_sum(small["mag2"][:, ds(g * GT, GT)], sq[slot][:].rearrange("p (t d) -> p t d", d=D),
                                       AX.X).then_inc(q["sq_free"], 1)
                    skewed(dve, NG, 2, (0, mag2))
                    dve.wait_ge(q["mag_ready"], 1)
                    w = small
                    ch.link(dve.tensor_scalar(w["t1"][:], w["mag"][:], EPS_MAG, None, ALU.is_gt))
                    ch.link(dve.tensor_scalar(w["t2"][:], w["mag"][:], EPS_MAG, None, ALU.max))
                    ch.link(dve.reciprocal(w["inv"][:], w["t2"][:]))
                    ch.link(dve.tensor_tensor(w["inv"][:], w["inv"][:], w["t1"][:], ALU.mult))
                    ch.link(dve.tensor_tensor(w["an"][:], w["mag"][:], w["inv"][:], ALU.mult))
                    ch.link(dve.tensor_scalar(w["an"][:], w["an"][:], EPS_COS, None, ALU.max))
                    ch.link(dve.reciprocal(w["ra"][:], w["an"][:]))
                    ch.link(dve.tensor_tensor(w["ra"][:], w["ra"][:], w["inv"][:], ALU.mult))
                    dve.wait_ge(q["tanh_ready"], 1)
                    ch.link(dve.scalar_tensor_tensor(out=w["c6"][:], in0=w["inv"][:], scalar=1.0 - GUIDE_W, in1=w["mw"][:],
                                                     op0=ALU.mult, op1=ALU.mult))
                    ch.link(dve.tensor_copy(zt[:, :, D], w["mw"][:]))

                    def scale_dirs(g, slot):
                        def one(j):
                            return dve.tensor_scalar(nh[slot][:, j * D:(j + 1) * D], dif[:, ds((g * GT + j) * D, D)],
                                                     w["ra"][:, ds(g * GT + j, 1)], None, ALU.mult)
                        if later(g, 2):
                            dve.wait_ge(q["nht_made"], g - 1)
                        for j in range(GT):
                            one(j).then_inc(q["nh_ready"], 1)

                    base = ch.n
                    PER = 2 + GT

                    def blend(g, slot):
                        pi = ps_i[slot][:].rearrange("p (k c) -> p k c", k=2)[:, :, 0:2 * ZW].rearrange("p k (j c) -> p k j c", c=ZW)
                        dve.wait_ge(q["infl_made"], g + 1)
                        c = c4[slot][:].rearrange("p (k j) -> p k j", k=2)
                        dve.reciprocal(c, pi[:, :, :, D]).then_inc(ch.sem, 1)
                        dve.wait_ge(ch.sem, g * PER + (base + 1))
                        dve.scalar_tensor_tensor(out=c4[slot][:], in0=c4[slot][:], scalar=GUIDE_W,
                                                 in1=w["mw"][:, ds(g * GT, GT)], op0=ALU.mult, op1=ALU.mult).then_inc(ch.sem, 1)
                        dve.wait_ge(ch.sem, g * PER + (base + 2))
                        for j in range(GT):
                            dve.tensor_scalar(z[:, ds((g * GT + j) * ZW, D)], pi[:, j // 2, j % 2, 0:D], c4[slot][:, j:j + 1], None,
                                              ALU.mult).then_inc(ch.sem, 1)
                        dve.wait_ge(ch.sem, g * PER + (base + 2 + GT))
                        for j in range(GT):
                            dve.scalar_tensor_tensor(out=z[:, ds((g * GT + j) * ZW, D)], in0=dif[:, ds((g * GT + j) * D, D)],
                                                     scalar=w["c6"][:, ds(g * GT + j, 1)], in1=z[:, ds((g * GT + j) * ZW, D)],
                                                     op0=ALU.mult, op1=ALU.add).then_inc(q["z_ready"], 1)
                    skewed(dve, NG, 2, (0, scale_dirs), (2, blend))
                    ch.n += NG * PER
                    dve.wait_ge(q["u_ready"], 2 * NG)
                    layer_stats(dve, ch, u, ZW, st)
                    ch.link(dve.tensor_scalar(w["wsum"][:], ut[:, :, D], EPS_WSUM, None, ALU.max))
                    ch.link(dve.reciprocal(w["t1"][:], w["wsum"][:]))
                    ch.link(dve.tensor_tensor(w["t2"][:], w["t1"][:], w["t1"][:], ALU.mult))
                    ch.link(dve.tensor_tensor(w["ve"][:], st["var"][:], w["t2"][:], ALU.mult))
                    dve.tensor_scalar(w["ve"][:], w["ve"][:], EPS, None, ALU.add).then_inc(q["var2_ready"], 1)
                    dve.wait_ge(q["rs_ready"], 1)
                    ch.link(dve.tensor_tensor(w["rs"][:], w["rs"][:], w["t1"][:], ALU.mult))
                    tiles(dve, lambda t: dve.tensor_scalar(u[:, ds(t * ZW, D)], u[:, ds(t * ZW, D)], mean(t),
                                                           w["rs"][:, ds(t, 1)], ALU.subtract, ALU.mult).then_inc(ch.sem, 1))
                    ch.n += NT
                    ch.wait()
                    xst = xs[:].rearrange("p (t d) -> p t d", d=D)
                    ch.link(dve.tensor_tensor(xst, xst, ut[:, :, 0:D], ALU.add))

                @block.scalar
                def _(act):
                    act.wait_ge(q["guide_t"], 1)
                    act.activation(gt[:], ps_s[0][:, 0:GUIDES], ACT.Copy).then_inc(q["guide_ready"], 1)

                    def square(g, slot):
                        act.wait_ge(q["diff_made"], g + 1)
                        act.activation(dif[:, ds(g * GW, GW)], ps_a[slot][:], ACT.Copy).then_inc(q["diff_copied"], 1)
                        if later(g, 2):
                            act.wait_ge(q["sq_free"], g - 1)
                        act.activation(sq[slot][:], ps_a[slot][:], ACT.Square).then_inc(q["sq_ready"], 1)
                    skewed(act, NG, 2, (0, square))
                    act.wait_ge(q["mag_ready"], 1)
                    act.activation(small["mw"][:], small["mag"][:], ACT.Tanh, scale=2.0).then_inc(q["tanh_ready"], 1)

                    def turn(g, slot):
                        act.wait_ge(q["nht_made"], g + 1)
                        act.activation(nht[slot][:], ps_a[slot][:], ACT.Copy).then_inc(q["nht_ready"], 1)

                    def weigh(g, slot):
                        act.wait_ge(q["sims_made"], g + 1)
                        act.activation(et[slot][0:GUIDES, :], ps_s[slot][0:GUIDES, :], ACT.Exp, scale=2.0).then_inc(q["exp_ready"], 1)
                    skewed(act, NG, 2, (0, turn), (1, weigh))

                    def copy_u(g, slot):
                        act.wait_ge(q["u_made"], g + 1)
                        uv = u[:, ds(g * GT * ZW, GT * ZW)].rearrange("p (b h c) -> p b h c", b=2, h=2)
                        for h in range(2):
                            act.activation(uv[:, :, h, :], ps_i[slot][:, h * 512:h * 512 + 2 * ZW].rearrange("p (b c) -> p b c", b=2),
                                           ACT.Copy).then_inc(q["u_ready"], 1)
                    skewed(act, NG, 2, (0, copy_u))

                @block.tensor
                def _(pe):
                    pe.wait_ge(setup_done, 6)
                    pe.wait_ge(q["guide_scaled"], 1)
                    pe.transpose(ps_s[0][:, 0:GUIDES], guide_n[0:GUIDES, :], ident[0:GUIDES, 0:GUIDES]).then_inc(q["guide_t"], 1)
                    pe.wait_ge(consts_loaded, 16)

                    def differences(g, slot):
                        pe.wait_ge(q["y_ready"], g * GT + GT)
                        if later(g, 2):
                            pe.wait_ge(q["sq_ready"], g - 1)
                        yg = y[:, ds(g * GW, GW)]
                        pe.matmul(ps_a[slot][:], const["diff"], yg, start=True, stop=False)
                        pe.matmul(ps_a[slot][:].rearrange("p (b h d) -> p b h d", b=2, h=2)[:, :, 0, :], const["cross"],
                                  yg.rearrange("p (b h d) -> p b h d", b=2, h=2)[:, :, 1, :],
                                  start=False, stop=True).then_inc(q["diff_made"], 1)
                    skewed(pe, NG, 2, (0, differences))
                    pe.wait_ge(q["sq_ready"], NG)
                    pe.wait_ge(q["guide_ready"], 1)
                    pe.wait_ge(q["et_zero"], 3)

                    def turn(g, slot):
                        pe.wait_ge(q["nh_ready"], g * GT + GT)
                        if later(g, 2):
                            pe.wait_ge(q["nht_ready"], g - 1)
                        for j in range(GT):
                            last = pe.transpose(ps_a[slot][:, j * D:(j + 1) * D], nh[slot][:, j * D:(j + 1) * D], ident[:])
                        last.then_inc(q["nht_made"], 1)

                    def sims(g, slot):
                        pe.wait_ge(q["nht_ready"], g + 1)
                        if later(g, 2):
                            pe.wait_ge(q["exp_ready"], g - 1)
                        pe.matmul(ps_s[slot][0:GUIDES, :], gt[:], nht[slot][:], start=True, stop=True).then_inc(q["sims_made"], 1)

                    def influence(g, slot):
                        pe.wait_ge(q["exp_ready"], g + 1)
                        if later(g, 2):
                            pe.wait_ge(q["z_ready"], (g - 1) * GT)
                        for j in range(GT):
                            last = pe.matmul(ps_i[slot][:, (j // 2) * 512 + (j % 2) * ZW:][:, 0:ZW], et[slot][:, j * D:(j + 1) * D],
                                             guide[:], start=(j % 2 == 0), stop=True, skip_group_check=True)
                        last.then_inc(q["infl_made"], 1)
                    skewed(pe, NG, 2, (0, turn), (1, sims), (2, influence))

                    def window(g, slot):
                        pe.wait_ge(q["z_ready"], NT)
                        if later(g, 2):
                            pe.wait_ge(q["u_ready"], 2 * g - 2)
                        zg = z[:, ds(g * GT * ZW, GT * ZW)].rearrange("p (b h c) -> p b h c", b=2, h=2)
                        o = [ps_i[slot][:, h * 512:h * 512 + 2 * ZW].rearrange("p (b c) -> p b c", b=2) for h in range(2)]
                        pe.matmul(o[0], const["band00"], zg[:, :, 0, :], start=True, stop=True)
                        pe.matmul(o[1], const["band10"], zg[:, :, 0, :], start=True, stop=False)
                        pe.matmul(o[1], const["band11"], zg[:, :, 1, :], start=False, stop=True).then_inc(q["u_made"], 1)
                    skewed(pe, NG, 2, (0, window))



        with ExitStack() as ph:
            yn = [sb(f"yn{i}", GW, stack=ph) for i in range(2)]
            yt = [sb(f"yt{i}", GW, stack=ph) for i in range(2)]
            ys = sb("ys", NT * D, stack=ph)
            TE = NT * EXPERTS
            r = {n: sb("r_" + n, TE, stack=ph) for n in ["score", "rank", "chosen", "key", "onehot", "tot", "acc0", "acc1", "slot"]}
            cmp_a = sb("cmp_a", TE * EXPERTS, stack=ph)
            cmp_b = sb("cmp_b", TE * EXPERTS, stack=ph)
            e8 = {n: sb("e8_" + n, EXPERTS, stack=ph) for n in ["tiles", "acc0", "acc1", "first"]}
            t32 = {n: sb("t32_" + n, NT, stack=ph) for n in ["max", "sum", "w", "slot"]}
            expert_f = sb("expert_f", NS, stack=ph)
            expert_i = sb("expert_i", NS, I32, stack=ph)
            xin = [sb(f"xin{i}", D, stack=ph) for i in range(3)]
            xt = [sb(f"xt{i}", P, stack=ph) for i in range(3)]
            hp = [sb(f"hp{i}", HID, stack=ph) for i in range(3)]
            ht = [sb(f"ht{i}", HID, stack=ph) for i in range(3)]
            e_up = [sb(f"e_up{i}", 1, I32, stack=ph) for i in range(3)]
            e_down = [sb(f"e_down{i}", 1, I32, stack=ph) for i in range(3)]
            res = sb("res", NS * D, stack=ph)
            bank = [psum(f"bank{i}", 1, ph) for i in range(8)]
            names = ["dve_done", "var_ready", "rstd_ready", "yn_ready", "yt_made", "yt_ready", "logits_made", "logits_read",
                     "shifted", "exp_ready", "onehot_ready", "counts_made", "slots_ready", "ys_ready", "scattered",
                     "rows_loaded", "xin_ready", "xt_made", "xt_ready", "h_made", "hp_ready", "ht_made", "ht_ready", "o_made",
                     "res_ready", "res_stored", "expert_ready", "e_up_ready", "e_down_ready"]
            q = {n: sem("b_" + n, ph) for n in names}
            THIRD = NS // 3
            with nc.Block() as block:
                @block.sync
                def _(sp):
                    sp.wait_ge(q["scattered"], 16 * NT)
                    sp.dma_start(rows[:].rearrange("p (k d) -> p k d", d=D),
                                 sorted_x.rearrange("(k p) d -> p k d", p=P)).then_inc(q["rows_loaded"], 16)
                    for c in range(3):
                        sp.wait_ge(q["res_ready"], (c + 1) * THIRD)
                        sp.dma_start(sorted_y.rearrange("(k p) d -> p k d", p=P)[:, c * THIRD:(c + 1) * THIRD, :],
                                     res[:, c * THIRD * D:(c + 1) * THIRD * D].rearrange("p (k d) -> p k d", d=D)
                                     ).then_inc(q["res_stored"], 16)
                    sp.wait_ge(q["res_stored"], 48)

                @block.gpsimd
                def _(pool):
                    pool.wait_ge(q["var_ready"], 1)
                    pool.tensor_tensor(small["rstd"][:], small["ve"][:], neg_half[:], ALU.pow).then_inc(q["rstd_ready"], 1)
                    pool.wait_ge(q["slots_ready"], 1)
                    for t in range(NT):
                        if t % 4 == 0:
                            pool.wait_ge(q["ys_ready"], t + 4)
                        pool.indirect_dma_start(out=sorted_x, out_offset=bass.IndirectOffsetOnAxis(ap=slot_i[:, t:t + 1].bitcast(U32), axis=0),
                                                in_=ys[:, t * D:(t + 1) * D], in_offset=None).then_inc(q["scattered"], 16)
                    pool.wait_ge(q["rows_loaded"], 16)
                    pool.wait_ge(q["expert_ready"], 1)

                    def pick(k, slot):
                        if later(k, 3):
                            pool.wait_ge(q["xt_made"], k - 2)
                            pool.wait_ge(q["hp_ready"], k - 2)
                        pool.tensor_copy(e_up[slot][:], expert_i[:, ds(k, 1)]).then_inc(q["e_up_ready"], 1)
                        pool.tensor_copy(xin[slot][:], rows[:, ds(k * D, D)]).then_inc(q["xin_ready"], 1)
                    skewed(pool, NS, 3, (0, pick))

                @block.vector
                def _(dve):
                    ch = Chain(dve, q["dve_done"])
                    w = small
                    layer_stats(dve, ch, xs, D, st)
                    dve.tensor_scalar(w["ve"][:], st["var"][:], EPS, None, ALU.add).then_inc(q["var_ready"], 1)
                    dve.wait_ge(q["rstd_ready"], 1)
                    dve.wait_ge(moe_loaded, 16 * MOE_LOADS)

                    def normalise(g, slot):
                        if later(g, 2):
                            dve.wait_ge(q["yt_made"], g - 1)
                        for j in range(GT):
                            dve.tensor_scalar(yn[slot][:, j * D:(j + 1) * D], xs[:, ds((g * GT + j) * D, D)], mean(g * GT + j),
                                              w["rstd"][:, ds(g * GT + j, 1)], ALU.subtract, ALU.mult).then_inc(q["yn_ready"], 1)

                    def take_logits(g, slot):
                        dve.wait_ge(q["logits_made"], g + 1)
                        dve.tensor_tensor(r["score"][:, ds(g * GT * EXPERTS, GT * EXPERTS)].rearrange("p (t e) -> p t e", e=EXPERTS),
                                          bank[2 + slot][:, 0:GT * EXPERTS].rearrange("p (t e) -> p t e", e=EXPERTS),
                                          gb[:].unsqueeze(1).to_broadcast((P, GT, EXPERTS)), ALU.add).then_inc(q["logits_read"], 1)
                    skewed(dve, NG, 2, (0, normalise), (2, take_logits))
                    dve.wait_ge(q["logits_read"], NG)

                    def te(name):
                        return r[name][:].rearrange("p (t e) -> p t e", e=EXPERTS)

                    def over_e(ap):
                        return ap.unsqueeze(2).to_broadcast((P, NT, EXPERTS))

                    ch.link(dve.reduce_max(t32["max"][:], te("score"), AX.X))
                    dve.tensor_tensor(te("score"), te("score"), over_e(t32["max"][:]), ALU.subtract).then_inc(q["shifted"], 1)
                    dve.wait_ge(q["exp_ready"], 1)
                    ch.link(dve.reduce_sum(t32["sum"][:], te("key"), AX.X))
                    ch.link(dve.reciprocal(t32["sum"][:], t32["sum"][:]))
                    ch.link(dve.tensor_tensor(te("score"), te("key"), over_e(t32["sum"][:]), ALU.mult))
                    four = (P, NT, EXPERTS, EXPERTS)
                    other = te("score").unsqueeze(2).to_broadcast(four)
                    own = te("score").unsqueeze(3).to_broadcast(four)
                    ca = cmp_a[:].rearrange("p (t e f) -> p t e f", e=EXPERTS, f=EXPERTS)
                    cbv = cmp_b[:].rearrange("p (t e f) -> p t e f", e=EXPERTS, f=EXPERTS)
                    ch.add(dve.tensor_tensor(ca, other, own, ALU.is_gt))
                    ch.link(dve.tensor_tensor(cbv, other, own, ALU.is_equal))
                    ch.link(dve.tensor_tensor(cmp_b[:].rearrange("p (t k) -> p t k", t=NT), cmp_b[:].rearrange("p (t k) -> p t k", t=NT),
                                              const["lower_e"][:, 0:EXPERTS * EXPERTS].unsqueeze(1).to_broadcast((P, NT, EXPERTS * EXPERTS)),
                                              ALU.mult))
                    ch.link(dve.tensor_tensor(cmp_a[:], cmp_a[:], cmp_b[:], ALU.add))
                    ch.link(dve.reduce_sum(te("rank"), ca, AX.X))
                    ch.add(dve.tensor_scalar(r["rank"][:], r["rank"][:], 1.5, None, ALU.is_lt))
                    ch.link(dve.tensor_scalar(r["chosen"][:], r["score"][:], 0.0, None, ALU.is_gt))
                    ch.link(dve.tensor_tensor(r["chosen"][:], r["chosen"][:], r["rank"][:], ALU.mult))
                    ch.link(dve.tensor_tensor(te("key"), te("chosen"), const["lower_e"][:, EXPERTS * EXPERTS:EXPERTS * EXPERTS + EXPERTS]
                                              .unsqueeze(1).to_broadcast((P, NT, EXPERTS)), ALU.mult))
                    ch.link(dve.reduce_max(t32["max"][:], te("key"), AX.X))
                    ch.link(dve.tensor_tensor(te("onehot"), te("key"), over_e(t32["max"][:]), ALU.is_equal))
                    dve.tensor_tensor(r["onehot"][:], r["onehot"][:], r["chosen"][:], ALU.mult).then_inc(q["onehot_ready"], 1)
                    dve.wait_ge(q["onehot_ready"], 1)
                    ch.link(dve.tensor_tensor(r["rank"][:], r["onehot"][:], r["score"][:], ALU.mult))
                    ch.link(dve.reduce_sum(t32["w"][:], te("rank"), AX.X))
                    ch.link(dve.tensor_tensor(w["t1"][:], t32["w"][:], w["rstd"][:], ALU.mult))
                    tiles(dve, lambda t: dve.tensor_scalar(ys[:, ds(t * D, D)], xs[:, ds(t * D, D)], mean(t), w["t1"][:, ds(t, 1)],
                                                           ALU.subtract, ALU.mult).then_inc(q["ys_ready"], 1))
                    dve.wait_ge(q["counts_made"], 1)
                    ch.add(dve.tensor_copy(r["tot"][:], bank[5][:, 0:TE]))
                    ch.link(dve.tensor_copy(r["acc0"][:], bank[5][:, 0:TE]))
                    now, nxt = "acc0", "acc1"
                    step = 1
                    while step < NT:
                        k = step * EXPERTS
                        ch.add(dve.tensor_copy(r[nxt][:, 0:k], r[now][:, 0:k]))
                        ch.link(dve.tensor_tensor(r[nxt][:, k:TE], r[now][:, k:TE], r[now][:, 0:TE - k], ALU.add))
                        now, nxt, step = nxt, now, 2 * step
                    count = r[now][:, TE - EXPERTS:TE]
                    many = cmp_a[:, 0:EXPERTS * NT].rearrange("p (e k) -> p e k", k=NT)
                    ch.link(dve.tensor_scalar(cmp_b[:, 0:NT], const["tile_no"][:, 0:NT], float(P), None, ALU.mult))
                    ch.link(dve.tensor_tensor(many, count.unsqueeze(2).to_broadcast((P, EXPERTS, NT)),
                                              cmp_b[:, 0:NT].unsqueeze(1).to_broadcast((P, EXPERTS, NT)), ALU.is_gt))
                    ch.link(dve.reduce_sum(e8["tiles"][:], many, AX.X))
                    ch.link(dve.tensor_copy(e8["acc0"][:], e8["tiles"][:]))
                    a, b_ = "acc0", "acc1"
                    step = 1
                    while step < EXPERTS:
                        ch.add(dve.tensor_copy(e8[b_][:, 0:step], e8[a][:, 0:step]))
                        ch.link(dve.tensor_tensor(e8[b_][:, step:], e8[a][:, step:], e8[a][:, 0:EXPERTS - step], ALU.add))
                        a, b_, step = b_, a, 2 * step
                    ch.link(dve.tensor_tensor(e8["first"][:], e8[a][:], e8["tiles"][:], ALU.subtract))
                    ch.link(dve.tensor_scalar(e8["first"][:], e8["first"][:], float(P), None, ALU.mult))
                    ch.link(dve.tensor_tensor(r["slot"][:], r[now][:], r["tot"][:], ALU.subtract))
                    ch.link(dve.tensor_tensor(r["slot"][:], bank[4][:, 0:TE], r["slot"][:], ALU.add))
                    ch.link(dve.tensor_tensor(te("slot"), te("slot"), e8["first"][:].unsqueeze(1).to_broadcast((P, NT, EXPERTS)), ALU.add))
                    ch.link(dve.tensor_tensor(r["slot"][:], r["slot"][:], r["onehot"][:], ALU.mult))
                    ch.link(dve.reduce_sum(t32["slot"][:], te("slot"), AX.X))
                    dve.tensor_copy(slot_i[:], t32["slot"][:]).then_inc(q["slots_ready"], 1)
                    ended = cmp_a[:, 0:NS * EXPERTS].rearrange("p (k e) -> p k e", e=EXPERTS)
                    ch.link(dve.tensor_tensor(ended, const["tile_no"][:, 0:NS].unsqueeze(2).to_broadcast((P, NS, EXPERTS)),
                                              e8[a][:].unsqueeze(1).to_broadcast((P, NS, EXPERTS)), ALU.is_ge))
                    ch.link(dve.reduce_sum(expert_f[:], ended, AX.X))
                    ch.link(dve.tensor_scalar(expert_f[:], expert_f[:], float(EXPERTS - 1), None, ALU.min))
                    dve.tensor_copy(expert_i[:], expert_f[:]).then_inc(q["expert_ready"], 1)
                    dve.wait_ge(q["expert_ready"], 1)

                    def expert_in(cell):
                        return nc.values_load(cell[0:1, 0:1], engines=DVE_ENGINE, min_val=0, max_val=EXPERTS - 1)

                    def bias1(k, slot):
                        if later(k, 3):
                            dve.wait_ge(q["res_ready"], k - 2)
                        dve.wait_ge(q["e_up_ready"], k + 1)
                        dve.tensor_copy(e_down[slot][:], expert_i[:, ds(k, 1)]).then_inc(q["e_down_ready"], 1)
                        e = expert_in(e_up[slot])
                        dve.wait_ge(q["e_down_ready"], k + 1)
                        dve.wait_ge(q["h_made"], k + 1)
                        dve.tensor_tensor(hp[slot][:], bank[slot][:], b1s[:, ds(e * HID, HID)], ALU.add).then_inc(q["hp_ready"], 1)

                    def bias2(k, slot):
                        e = expert_in(e_down[slot])
                        dve.wait_ge(q["o_made"], k + 1)
                        dve.tensor_tensor(res[:, ds(k * D, D)], bank[7][:, 0:D], b2s[:, ds(e * D, D)],
                                          ALU.add).then_inc(q["res_ready"], 1)
                    skewed(dve, NS, 3, (0, bias1), (2, bias2))

                @block.scalar
                def _(act):
                    def turn(g, slot):
                        act.wait_ge(q["yt_made"], g + 1)
                        if later(g, 2):
                            act.wait_ge(q["logits_made"], g - 1)
                        act.activation(yt[slot][:], bank[slot][:], ACT.Copy).then_inc(q["yt_ready"], 1)
                    skewed(act, NG, 2, (0, turn))
                    act.wait_ge(q["shifted"], 1)
                    act.activation(r["key"][:], r["score"][:], ACT.Exp).then_inc(q["exp_ready"], 1)

                    def turn_x(k, slot):
                        act.wait_ge(q["xt_made"], k + 1)
                        if later(k, 3):
                            act.wait_ge(q["h_made"], k - 2)
                        act.activation(xt[slot][:], bank[6][:, 0:P], ACT.Copy).then_inc(q["xt_ready"], 1)

                    def relu(k, slot):
                        act.wait_ge(q["ht_made"], k + 1)
                        if later(k, 3):
                            act.wait_ge(q["o_made"], k - 2)
                        act.activation(ht[slot][:], bank[3 + slot % 3][:], ACT.Relu).then_inc(q["ht_ready"], 1)
                    skewed(act, NS, 3, (0, turn_x), (2, relu))

                @block.tensor
                def _(pe):
                    def turn(g, slot):
                        pe.wait_ge(q["yn_ready"], g * GT + GT)
                        if later(g, 2):
                            pe.wait_ge(q["yt_ready"], g - 1)
                        for j in range(GT):
                            last = pe.transpose(bank[slot][:, j * D:(j + 1) * D], yn[slot][:, j * D:(j + 1) * D], ident[:])
                        last.then_inc(q["yt_made"], 1)

                    def gate(g, slot):
                        pe.wait_ge(q["yt_ready"], g + 1)
                        if later(g, 2):
                            pe.wait_ge(q["logits_read"], g - 1)
                        for j in range(GT):
                            last = pe.matmul(bank[2 + slot][:, j * EXPERTS:(j + 1) * EXPERTS], yt[slot][:, j * P:(j + 1) * P], gw[:],
                                             start=True, stop=True)
                        last.then_inc(q["logits_made"], 1)
                    pe.wait_ge(moe_loaded, 16 * MOE_LOADS)
                    skewed(pe, NG, 2, (0, turn), (1, gate))
                    pe.wait_ge(q["onehot_ready"], 1)
                    pe.matmul(bank[4][:, 0:TE], const["before"], r["onehot"][:], start=True, stop=True)
                    pe.matmul(bank[5][:, 0:TE], ones[:], r["onehot"][:], start=True, stop=True).then_inc(q["counts_made"], 1)
                    pe.wait_ge(q["expert_ready"], 1)

                    def expert_in(cell):
                        return nc.values_load(cell[0:1, 0:1], engines=PE_ENGINE, min_val=0, max_val=EXPERTS - 1)

                    def turn_x(k, slot):
                        pe.wait_ge(q["xin_ready"], k + 1)
                        if later(k, 1):
                            pe.wait_ge(q["xt_ready"], k)
                        pe.transpose(bank[6][:, 0:P], xin[slot][:], ident[:]).then_inc(q["xt_made"], 1)

                    def up(k, slot):
                        e = expert_in(e_up[slot])
                        pe.wait_ge(q["xt_ready"], k + 1)
                        if later(k, 3):
                            pe.wait_ge(q["hp_ready"], k - 2)
                        pe.matmul(bank[slot][:], xt[slot][:], w1[:, ds(e * HID, HID)], start=True, stop=True).then_inc(q["h_made"], 1)

                    def turn_h(k, slot):
                        pe.wait_ge(q["hp_ready"], k + 1)
                        if later(k, 3):
                            pe.wait_ge(q["ht_ready"], k - 2)
                        for c in range(HC):
                            last = pe.transpose(bank[3 + slot][:, c * P:(c + 1) * P], hp[slot][:, c * P:(c + 1) * P], ident[:])
                        last.then_inc(q["ht_made"], 1)

                    def down(k, slot):
                        e = expert_in(e_down[slot])
                        pe.wait_ge(q["ht_ready"], k + 1)
                        if later(k, 1):
                            pe.wait_ge(q["res_ready"], k)
                        for c in range(HC):
                            last = pe.matmul(bank[7][:, 0:D], ht[slot][:, c * P:(c + 1) * P],
                                             w2[:, ds(e * HC * D + c * D, D)], start=(c == 0), stop=(c == HC - 1))
                        last.then_inc(q["o_made"], 1)
                    skewed(pe, NS, 3, (0, turn_x), (1, up), (2, turn_h), (3, down))
        moe.close()

        full = {n: sb("full_" + n, c) for n, c in [("f1", HID), ("f2", HID), ("h1", HC * HID), ("h2", HC * HID), ("f3", HC * D)]}
        scl = {n: sb("scl_" + n, HC) for n in ["f1", "f2", "h1", "h2"]}
        scl3 = sb("scl3", D)
        with ExitStack() as ph:
            W = S
            VW = 96
            UNITS = 18
            SQS = SCALE ** 0.5
            wqh, wql = sb("wqh", HEADS * DH, F32R, ph), sb("wql", HEADS * DH, F32R, ph)
            wkh, wkl = sb("wkh", P, F32R, ph), sb("wkl", P, F32R, ph)
            wvh, wvl = sb("wvh", DH, F32R, ph), sb("wvl", DH, F32R, ph)
            ident_r = sb("ident_r", P, F32R, ph)
            causal_r = sb("causal_r", QG * P, F32R, ph)
            zb = [sb(f"zb{i}", W, F32, ph) for i in range(2)]
            xh = [sb(f"xh{i}", W, F32R, ph) for i in range(2)]
            xl = [sb(f"xl{i}", W, F32R, ph) for i in range(2)]
            xf = sb("xf", W, F32, ph)
            qx = [sb(f"qx{i}", HEADS * W, F32R, ph) for i in range(2)]
            qm = [sb(f"qm{i}", HEADS * W, F32R, ph) for i in range(2)]
            kh = [sb(f"kh{i}", W, F32R, ph) for i in range(2)]
            kl = [sb(f"kl{i}", W, F32R, ph) for i in range(2)]
            vv = [sb(f"vv{i}", HALVES * VW, F32, ph) for i in range(2)]
            mx = sb("mx", HALVES * HEADS, F32, ph)
            mts = sb("mts", P, F32R, ph)
            pt0 = [sb(f"pt0{i}", QG * W, F32, ph) for i in range(2)]
            pt1 = [sb(f"pt1{i}", QG * P, F32, ph) for i in range(2)]
            rec = sb("rec", HALVES * QG, F32, ph)
            on = sb("on", HALVES * HEADS * DH, F32, ph)
            ot = sb("ot", NQ * 4 * P, F32, ph)
            yb = [sb(f"yb{i}", W, F32, ph) for i in range(2)]
            row_i = [sb(f"row_i{i}", HALVES, I32, ph) for i in range(2)]
            ob = sb("ob", W, F32, ph)
            raw_f, raw_t = sb("raw_f", 6 * HALVES, F32, ph), sb("raw_t", 6 * HALVES, F32, ph)
            mv_y, mv_o = sb("mv_y", 2 * HALVES, F32, ph), sb("mv_o", 2 * HALVES, F32, ph)
            mv_x = [sb(f"mv_x{i}", 2 * HALVES, F32, ph) for i in range(2)]
            ve_y, ve_x, ve_o = sb("ve_y", HALVES, F32, ph), sb("ve_x", HALVES, F32, ph), sb("ve_o", HALVES, F32, ph)
            rs_y, rs_o = sb("rs_y", HALVES, F32, ph), sb("rs_o", HALVES, F32, ph)
            rs_x = [sb(f"rs_x{i}", HALVES, F32, ph) for i in range(2)]
            ring = [psum(f"ring{i}", 1, ph) for i in range(3)]
            ps_s = psum("ps_scores", 3, ph)
            ps_o = psum("ps_out", HALVES, ph)
            names = ["dve_done", "weights_split", "zb_ready", "z_made", "xh_ready", "xf_ready", "x_ready", "ring_made",
                     "ring_read", "kh_ready", "qh_ready", "ot_made", "ot_ready", "mts_ready", "max_loaded", "qm_loaded", "scores_made",
                     "exp_ready", "masked", "pv_made", "rec_ready", "normed", "proj_made", "proj_read", "pool_turn",
                     "row_ready", "gathered0", "gathered1", "feed_own", "var_y", "pow_y", "var_x", "pow_x",
                     "tail_own", "var_o", "pow_o", "var_p", "pow_p", "tail_done", "dve_turn"]
            q = {n: sem("c_" + n, ph) for n in names}
            FEED, TAIL = 11, 19

            ffn_loads = ((full["f1"][:], f1t), (full["f2"][:], f2t), (full["h1"][:], h1t), (full["h2"][:], h2t), (full["f3"][:], f3t),
                         (scl["f1"][:], f1s), (scl["f2"][:], f2s), (scl["h1"][:], h1s), (scl["h2"][:], h2s),
                         (scl3[:], broadcast(f3s, D)))

            def within(b, k):
                return not isinstance(b, int) or b + k < B

            def sequences(attend):
                def run(eng):
                    for b in range(3):
                        attend(b, b % 2)
                    with eng.Fori(1, B // 2 - 2) as i:
                        attend(i * 2 + 1, 1)
                        attend(i * 2 + 2, 0)
                    for b in range(B - 3, B):
                        attend(b, b % 2)
                return run

            with nc.Block() as block:
                @block.sync
                def _(sp):
                    def load_max(n, slot):
                        sp.wait_ge(q["mts_ready"], n + 1)
                        for h in range(HALVES):
                            sp.dma_start(qm[slot][DH:DH + 1, :].rearrange("o (e h p) -> o e h p", h=HALVES, p=P)[:, :, h, :].bitcast(F32),
                                         mts[h * HEADS:(h + 1) * HEADS, :].bitcast(F32)).then_inc(q["max_loaded"], 16)
                    def copy_high(n, slot):
                        sp.wait_ge(q["qh_ready"], n * 8 + 8)
                        sp.dma_start(qm[slot][0:DH, :].bitcast(F32), qx[slot][0:DH, :].bitcast(F32)).then_inc(q["qm_loaded"], 16)

                    def attend(b, slot):
                        if within(b, 1):
                            copy_high(b + 1, 1 - slot)
                            load_max(b + 1, 1 - slot)
                    copy_high(0, 0)
                    load_max(0, 0)
                    for dst, src in ffn_loads:
                        sp.dma_start(dst, src).then_inc(ffn_loaded, 16)
                    sequences(attend)(sp)
                    sp.wait_ge(q["max_loaded"], 32 * B)
                    sp.wait_ge(q["qm_loaded"], 16 * B)

                @block.gpsimd
                def _(pool):
                    def gather(n, slot):
                        if later(n, 2):
                            pool.wait_ge(q["feed_own"], (n - 1) * FEED - 4)
                        pool.tensor_copy(row_i[slot][:], slot_i[:, ds(n * HALVES, HALVES)]).then_inc(q["row_ready"], 1)
                        pool.wait_ge(q["row_ready"], n + 1)
                        pool.sem_inc(q["pool_turn"], 1)
                        for h in range(HALVES):
                            pool.indirect_dma_start(out=yb[slot][:, h * D:(h + 1) * D], out_offset=None,
                                                    in_offset=bass.IndirectOffsetOnAxis(ap=row_i[slot][:, h:h + 1].bitcast(U32), axis=0),
                                                    in_=sorted_y).then_inc(q[f"gathered{slot}"], 16)

                    def power(out_, in_, ready, n, done):
                        pool.wait_ge(q[ready], n + 1)
                        pool.sem_inc(q["pool_turn"], 1)
                        pool.tensor_tensor(out_[:], in_[:], neg_half[:, 0:HALVES], ALU.pow).then_inc(q[done], 1)

                    def mask(b, g):
                        pool.wait_ge(q["exp_ready"], b * 8 + (2 * g + 1))
                        pool.sem_inc(q["pool_turn"], 1)
                        v = pt0[g % 2][:].rearrange("p (e i) -> p e i", e=QG)[:, :, 0:P]
                        pool.affine_select(out=v, in_=v, compare_op=ALU.is_ge, fill=0.0, base=0, pattern=[[0, QG], [1, P]],
                                           channel_multiplier=-1).then_inc(q["masked"], 1)
                        pool.wait_ge(q["exp_ready"], b * 8 + (2 * g + 2))
                        pool.sem_inc(q["pool_turn"], 1)
                        v = pt1[g % 2][:].rearrange("p (e i) -> p e i", e=QG)
                        pool.affine_select(out=v, in_=v, compare_op=ALU.is_ge, fill=0.0, base=0, pattern=[[0, QG], [1, P]],
                                           channel_multiplier=-1).then_inc(q["masked"], 1)

                    def attend(b, slot):
                        mask(b, 1)
                        if within(b, 2):
                            power(rs_x[slot], ve_x, "var_x", b + 2, "pow_x")
                        if later(b, 1):
                            power(rs_o, ve_o, "var_o", b - 1, "pow_o")
                        if within(b, 3):
                            gather(b + 3, 1 - slot)
                        mask(b, 2)
                        if later(b, 1):
                            power(rs_o, ve_o, "var_p", b - 1, "pow_p")
                        mask(b, 3)
                        if within(b, 1):
                            mask(b + 1, 0)
                        if within(b, 3):
                            power(rs_y, ve_y, "var_y", b + 3, "pow_y")
                    for n in range(2):
                        gather(n, n)
                    for n in range(2):
                        power(rs_y, ve_y, "var_y", n, "pow_y")
                        power(rs_x[n], ve_x, "var_x", n, "pow_x")
                        if n == 0:
                            gather(2, 0)
                    mask(0, 0)
                    power(rs_y, ve_y, "var_y", 2, "pow_y")
                    sequences(attend)(pool)
                    power(rs_o, ve_o, "var_o", B - 1, "pow_o")
                    power(rs_o, ve_o, "var_p", B - 1, "pow_p")

                @block.vector
                def _(dve):
                    ch = Chain(dve, q["dve_done"])
                    w = small
                    dve.wait_ge(attn_loaded, 16 * 8)
                    for high, low, full in ((wqh, wql, wq), (wkh, wkl, wk2), (wvh, wvl, wv)):
                        ch.link(dve.tensor_copy(high[:], full[:]))
                        ch.link(dve.tensor_tensor(low[:], full[:], high[:].bitcast(F32), ALU.subtract))
                    ch.link(dve.tensor_copy(ident_r[:], ident[:]))
                    ch.link(dve.tensor_copy(causal_r[:].rearrange("p (e j) -> p e j", e=QG), const["causal"].unsqueeze(1).to_broadcast((P, QG, P))))
                    for i in range(2):
                        ch.link(dve.memset(qm[i][DH:P, :].bitcast(F32), 0.0))
                        ch.link(dve.memset(kl[i][DH:P, :].bitcast(F32), 0.0))
                        ch.link(dve.memset(kl[i][DH:DH + 1, :].bitcast(F32), -1.0))
                        ch.link(dve.memset(vv[i][:], 0.0))
                        ch.link(dve.memset(vv[i][:].rearrange("p (h c) -> p h c", c=VW)[:, :, DH], 1.0))
                    dve.sem_inc(q["weights_split"], 1)

                    def row(n, h):
                        return xs[:, ds((n * HALVES + h) * D, D)]

                    def halves_stats(srcs, raw, mv, own, at):
                        for h in range(HALVES):
                            dve.bn_stats(raw[:, h * 6:(h + 1) * 6], srcs[h]).then_inc(q[own], 1)
                        dve.wait_ge(q[own], at + HALVES)
                        dve.sem_inc(q["dve_turn"], 1)
                        for h in range(HALVES):
                            dve.bn_aggr(mv[:, h * 2:(h + 1) * 2], raw[:, h * 6:(h + 1) * 6]).then_inc(q[own], 1)
                        dve.wait_ge(q[own], at + 2 * HALVES)

                    def var(mv):
                        return mv[:].rearrange("p (h k) -> p h k", k=2)[:, :, 1]

                    def scale(buf, mv, rs, own, at):
                        for h in range(HALVES):
                            v = buf[:, h * D:(h + 1) * D]
                            dve.tensor_scalar(v, v, mv[:, h * 2:h * 2 + 1], rs[:, h:h + 1], ALU.subtract, ALU.mult).then_inc(q[own], 1)
                        dve.wait_ge(q[own], at + HALVES)

                    def feed_first(n, slot):
                        dve.wait_ge(q[f"gathered{slot}"], (n - slot) * 16 + 32)
                        halves_stats([yb[slot][:, 0:D], yb[slot][:, D:W]], raw_f, mv_y, "feed_own", n * FEED)
                        dve.tensor_scalar(ve_y[:], var(mv_y), EPS, None, ALU.add).then_inc(q["var_y"], 1)

                    def feed_second(n, slot):
                        dve.wait_ge(q["pow_y"], n + 1)
                        scale(yb[slot], mv_y, rs_y, "feed_own", n * FEED + 4)
                        dve.tensor_tensor(xs[:, ds(n * W, W)], xs[:, ds(n * W, W)], yb[slot][:], ALU.add).then_inc(q["feed_own"], 1)
                        dve.wait_ge(q["feed_own"], n * FEED + 7)
                        halves_stats([row(n, 0), row(n, 1)], raw_f, mv_x[slot], "feed_own", n * FEED + 7)
                        dve.tensor_scalar(ve_x[:], var(mv_x[slot]), 1.0 + EPS, EPS * EPS, ALU.mult, ALU.add).then_inc(q["var_x"], 1)

                    def tail_first(b):
                        dve.wait_ge(q["proj_read"], b + 1)
                        halves_stats([ob[:, 0:D], ob[:, D:W]], raw_t, mv_o, "tail_own", b * TAIL)
                        dve.tensor_scalar(ve_o[:], var(mv_o), EPS, None, ALU.add).then_inc(q["var_o"], 1)

                    def tail_second(b):
                        dve.wait_ge(q["pow_o"], b + 1)
                        scale(ob, mv_o, rs_o, "tail_own", b * TAIL + 4)
                        v = ob[:].rearrange("p (h d) -> p h d", h=HALVES)
                        dve.tensor_tensor(v, v, lnog[:].unsqueeze(1).to_broadcast((P, HALVES, D)), ALU.mult).then_inc(q["tail_own"], 1)
                        dve.wait_ge(q["tail_own"], b * TAIL + 7)
                        dve.tensor_tensor(v, v, lnob[:].unsqueeze(1).to_broadcast((P, HALVES, D)), ALU.add).then_inc(q["tail_own"], 1)
                        dve.wait_ge(q["tail_own"], b * TAIL + 8)
                        halves_stats([ob[:, 0:D], ob[:, D:W]], raw_t, mv_o, "tail_own", b * TAIL + 8)
                        dve.tensor_scalar(ve_o[:], var(mv_o), EPS, None, ALU.add).then_inc(q["var_p"], 1)

                    def tail_third(b):
                        dve.wait_ge(q["pow_p"], b + 1)
                        scale(ob, mv_o, rs_o, "tail_own", b * TAIL + 12)
                        dve.tensor_tensor(xs[:, ds(b * W, W)], xs[:, ds(b * W, W)], ob[:], ALU.add).then_inc(q["tail_own"], 1)
                        dve.wait_ge(q["tail_own"], b * TAIL + 15)
                        halves_stats([row(b, 0), row(b, 1)], raw_t, mv_o, "tail_own", b * TAIL + 15)
                        dve.tensor_copy(mv_all[:, ds(b * 4, 4)], mv_o[:]).then_inc(q["tail_done"], 1)

                    def normalise(n, slot):
                        dve.wait_ge(q["pow_x"], n + 1)
                        for h in range(HALVES):
                            dve.tensor_scalar(zb[slot][:, h * D:(h + 1) * D], row(n, h), mv_x[slot][:, h * 2:h * 2 + 1],
                                              rs_x[slot][:, h:h + 1], ALU.subtract, ALU.mult).then_inc(q["zb_ready"], 1)

                    def low_x(n, slot):
                        dve.wait_ge(q["xh_ready"], n + 1)
                        dve.tensor_scalar(xf[:], ring[0][:, 0:W], lng[:, 0:1], lnb[:, 0:1], ALU.mult, ALU.add).then_inc(q["xf_ready"], 1)
                        dve.wait_ge(q["xf_ready"], n + 1)
                        dve.tensor_tensor(xl[slot][:], xf[:], xh[slot][:].bitcast(F32), ALU.subtract).then_inc(q["x_ready"], 1)

                    def keys(n, slot):
                        dve.wait_ge(q["kh_ready"], n + 1)
                        dve.scalar_tensor_tensor(out=kl[slot][0:DH, :], in0=ring[0][0:DH, W:2 * W], scalar=SQS,
                                                 in1=kh[slot][0:DH, :].bitcast(F32), op0=ALU.mult, op1=ALU.subtract)
                        dve.tensor_copy(vv[slot][:].rearrange("p (h c) -> p h c", c=VW)[:, :, 0:DH],
                                        ring[0][:, 0:HALVES * DH].rearrange("p (h c) -> p h c", c=DH)).then_inc(q["ring_read"], 1)

                    def low_q(n, slot, u):
                        dve.wait_ge(q["qh_ready"], n * 8 + (2 * u + 2))
                        for par in range(2):
                            src = ring[(1 + u) % 3][par * DH:(par + 1) * DH, :].rearrange("p (k i) -> p k i", k=2)
                            v = qx[slot][:].rearrange("p (k e i) -> p k e i", e=2, i=W)[:, 2 * u:2 * u + 2, par, :]
                            last = dve.scalar_tensor_tensor(out=v[DH:P], in0=src, scalar=SCALE * SQS, in1=v[0:DH].bitcast(F32),
                                                            op0=ALU.mult, op1=ALU.subtract)
                        last.then_inc(q["ring_read"], 1)

                    def maxima(n, m):
                        dve.wait_ge(q["ring_made"], n * UNITS + (6 + m))
                        heads = QG if m < NQ else 2
                        at = m * QG if m < NQ else HEADS + (m - NQ) * 2
                        dve.reduce_max(mx[:, at:at + heads], ring[(5 + m) % 3][:].rearrange("p (e j) -> p e j", e=heads),
                                       AX.X).then_inc(q["ring_read"], 1)

                    def take_max(n):
                        dve.wait_ge(q["ring_made"], n * UNITS + UNITS)
                        if later(n, 1):
                            dve.wait_ge(q["max_loaded"], n * 32)
                        dve.tensor_copy(mts[0:HALVES * HEADS, :], ring[(UNITS - 1) % 3][0:HALVES * HEADS, 0:P]).then_inc(q["mts_ready"], 1)

                    def norm(b, g):
                        dve.wait_ge(q["pv_made"], b * NQ + (g + 1))
                        o = ps_o[:].rearrange("p (h k) -> p h k", h=HALVES)[:, :, 0:QG * VW].rearrange("p h (e c) -> p h e c", c=VW)
                        r3 = rec[:].rearrange("p (h e) -> p h e", h=HALVES)
                        dve.reciprocal(r3, o[:, :, :, DH]).then_inc(q["rec_ready"], 1)
                        dve.wait_ge(q["rec_ready"], b * NQ + (g + 1))
                        dve.tensor_tensor(on[:].rearrange("p (h e c) -> p h e c", h=HALVES, c=DH)[:, :, g * QG:(g + 1) * QG, :],
                                          o[:, :, :, 0:DH], r3.unsqueeze(3).to_broadcast((P, HALVES, QG, DH)),
                                          ALU.mult).then_inc(q["normed"], 1)

                    def attend(b, slot):
                        n, other, prep, further = b + 1, 1 - slot, within(b, 1), within(b, 2)
                        if further:
                            feed_second(b + 2, slot)
                        if prep:
                            low_q(n, other, 2)
                            low_q(n, other, 3)
                        if later(b, 1):
                            tail_first(b - 1)
                        norm(b, 0)
                        if prep:
                            for m in range(4):
                                maxima(n, m)
                        if later(b, 1):
                            tail_second(b - 1)
                        norm(b, 1)
                        if prep:
                            for m in range(4, 9):
                                maxima(n, m)
                        if further:
                            normalise(b + 2, slot)
                        if later(b, 1):
                            tail_third(b - 1)
                        norm(b, 2)
                        if prep:
                            for m in range(9, 12):
                                maxima(n, m)
                            take_max(n)
                        if further:
                            low_x(b + 2, slot)
                        if within(b, 3):
                            feed_first(b + 3, other)
                        norm(b, 3)
                        if further:
                            keys(b + 2, slot)
                            low_q(b + 2, slot, 0)
                            low_q(b + 2, slot, 1)
                    for n in range(2):
                        feed_first(n, n)
                        feed_second(n, n)
                    normalise(0, 0)
                    low_x(0, 0)
                    keys(0, 0)
                    for u in range(4):
                        low_q(0, 0, u)
                    normalise(1, 1)
                    for m in range(12):
                        maxima(0, m)
                    take_max(0)
                    low_x(1, 1)
                    keys(1, 1)
                    low_q(1, 1, 0)
                    low_q(1, 1, 1)
                    feed_first(2, 0)
                    sequences(attend)(dve)
                    tail_first(B - 1)
                    tail_second(B - 1)
                    tail_third(B - 1)

                @block.scalar
                def _(act):
                    def high_x(n, slot):
                        act.wait_ge(q["z_made"], n + 1)
                        act.activation(xh[slot][:], ring[0][:, 0:W], ACT.Identity, scale=lng[:, 0:1], bias=lnb[:, 0:1]).then_inc(q["xh_ready"], 1)

                    def high_k(n, slot):
                        act.wait_ge(q["ring_made"], n * UNITS + 1)
                        act.activation(kh[slot][:], ring[0][:, W:2 * W], ACT.Copy, scale=SQS).then_inc(q["kh_ready"], 1)

                    def high_q(n, slot, u):
                        act.wait_ge(q["ring_made"], n * UNITS + (2 + u))
                        for par in range(2):
                            src = ring[(1 + u) % 3][par * DH:(par + 1) * DH, :].rearrange("p (k i) -> p k i", k=2)
                            v = qx[slot][0:DH, :].rearrange("p (k e i) -> p k e i", e=2, i=W)[:, 2 * u:2 * u + 2, par, :]
                            act.activation(v, src, ACT.Copy, scale=SCALE * SQS).then_inc(q["qh_ready"], 1)

                    def exponent(b, g):
                        act.wait_ge(q["scores_made"], b * 8 + (2 * g + 1))
                        if later(b, 1) or g >= 2:
                            act.wait_ge(q["pv_made"], b * NQ + (g - 1))
                        act.activation(pt0[g % 2][:], ps_s[:, 0:2 * 512], ACT.Exp).then_inc(q["exp_ready"], 1)
                        act.wait_ge(q["scores_made"], b * 8 + (2 * g + 2))
                        act.activation(pt1[g % 2][:], ps_s[:, 2 * 512:3 * 512], ACT.Exp).then_inc(q["exp_ready"], 1)

                    def take_heads(b, g):
                        act.wait_ge(q["ot_made"], b * NQ + (g + 1))
                        act.activation(ot[:, g * 512:(g + 1) * 512], ps_o[:, 0:512], ACT.Copy).then_inc(q["ot_ready"], 1)

                    def take_projection(b):
                        act.wait_ge(q["proj_made"], b + 1)
                        if later(b, 1):
                            act.wait_ge(q["tail_own"], b * TAIL - 4)
                        act.activation(ob[:], ps_o[:, 512:512 + W], ACT.Copy).then_inc(q["proj_read"], 1)

                    def attend(b, slot):
                        n, other = b + 1, 1 - slot
                        exponent(b, 1)
                        if later(b, 1):
                            take_projection(b - 1)
                        if within(b, 1):
                            high_q(n, other, 2)
                            high_q(n, other, 3)
                        take_heads(b, 0)
                        exponent(b, 2)
                        take_heads(b, 1)
                        exponent(b, 3)
                        take_heads(b, 2)
                        if within(b, 2):
                            high_x(b + 2, slot)
                        if within(b, 1):
                            exponent(n, 0)
                        if within(b, 2):
                            high_k(b + 2, slot)
                            high_q(b + 2, slot, 0)
                        take_heads(b, 3)
                        if within(b, 2):
                            high_q(b + 2, slot, 1)
                    act.wait_ge(attn_loaded, 16 * 8)
                    high_x(0, 0)
                    high_k(0, 0)
                    for u in range(4):
                        high_q(0, 0, u)
                    high_x(1, 1)
                    exponent(0, 0)
                    high_k(1, 1)
                    high_q(1, 1, 0)
                    high_q(1, 1, 1)
                    sequences(attend)(act)
                    take_projection(B - 1)

                @block.tensor
                def _(pe):
                    def three(out_ap, lhs, rhs, start=True):
                        (lh, ll), (rh, rl) = lhs, rhs
                        pe.matmul(out_ap, lh, rl, start=start, stop=False, skip_group_check=True)
                        pe.matmul(out_ap, ll, rh, start=False, stop=False, skip_group_check=True)
                        return pe.matmul(out_ap, lh, rh, start=False, stop=True, skip_group_check=True)

                    def turn_z(n, slot):
                        pe.wait_ge(q["zb_ready"], n * HALVES + HALVES)
                        wait_unit(n, 0)
                        for h in range(HALVES):
                            last = pe.transpose(ring[0][:, h * P:(h + 1) * P], zb[slot][:, h * D:(h + 1) * D], ident[:])
                        last.then_inc(q["z_made"], 1)

                    def keys(n, slot):
                        pe.wait_ge(q["x_ready"], n + 1)
                        three(ring[0][:, W:2 * W], (wkh[:], wkl[:]), (xh[slot][:], xl[slot][:]))
                        for h in range(HALVES):
                            c = slice(h * P, (h + 1) * P)
                            last = three(ring[0][:, h * DH:(h + 1) * DH], (xh[slot][:, c], xl[slot][:, c]), (wvh[:], wvl[:]))
                        last.then_inc(q["ring_made"], 1)

                    def queries(n, slot, u):
                        k = 1 + u
                        wait_unit(n, k)
                        for j in range(2):
                            c = slice((2 * u + j) * P, (2 * u + j + 1) * P)
                            last = three(ring[k % 3][:, j * W:(j + 1) * W], (wqh[:, c], wql[:, c]), (xh[slot][:], xl[slot][:]))
                        last.then_inc(q["ring_made"], 1)

                    def wait_unit(n, k):
                        if k >= 3:
                            pe.wait_ge(q["ring_read"], n * 17 + (k - 2))
                        elif later(n, 1):
                            if k == 2:
                                pe.wait_ge(q["mts_ready"], n)
                            else:
                                pe.wait_ge(q["ring_read"], n * 17 + (k - 1))

                    def maxima(n, slot, m):
                        k = 5 + m
                        wait_unit(n, k)
                        if m == 0:
                            pe.wait_ge(q["ring_read"], n * 17 + 5)
                        bank = ring[k % 3]
                        if m < NQ:
                            for j in range(QG):
                                h = m * QG + j
                                pe.matmul(bank[:, j * P:(j + 1) * P], qx[slot][:, h * W:h * W + P], kh[slot][:, 0:P],
                                          start=(j == 0), stop=False, skip_group_check=True)
                            last = pe.matmul(bank[:], ident_r[:], causal_r[:], start=False, stop=True, skip_group_check=True)
                        else:
                            for j in range(2):
                                h = (m - NQ) * 2 + j
                                pe.matmul(bank[:, j * W:(j + 1) * W], qx[slot][:, h * W + P:(h + 1) * W], kh[slot][:],
                                          start=(j == 0), stop=False, skip_group_check=True)
                            last = pe.matmul(bank[:].rearrange("p (e j) -> p e j", e=2)[:, :, P:W], ident_r[:],
                                             causal_r[:, 0:2 * P].rearrange("p (e j) -> p e j", e=2), start=False, stop=True,
                                             skip_group_check=True)
                        last.then_inc(q["ring_made"], 1)

                    def turn_max(n):
                        pe.wait_ge(q["ring_read"], n * 17 + 17)
                        pe.transpose(ring[(UNITS - 1) % 3][0:HALVES * HEADS, 0:P], mx[:], ident[:]).then_inc(q["ring_made"], 1)

                    def scores(b, slot, g):
                        if g == 0:
                            pe.wait_ge(q["max_loaded"], b * 32 + 32)
                            pe.wait_ge(q["qm_loaded"], b * 16 + 16)
                            if later(b, 1):
                                pe.wait_ge(q["exp_ready"], b * 8)
                        else:
                            pe.wait_ge(q["exp_ready"], b * 8 + 2 * g)
                        for half in range(2):
                            c = slice((QG * g + 2 * half) * W, (QG * g + 2 * half + 2) * W)
                            o = ps_s[:, half * 512:(half + 1) * 512]
                            pe.matmul(o, kh[slot][:, 0:P], qx[slot][:, c], start=True, stop=False)
                            last = pe.matmul(o, kl[slot][:, 0:P], qm[slot][:, c], start=False, stop=True)
                        last.then_inc(q["scores_made"], 1)
                        o = ps_s[:, 2 * 512:3 * 512]

                        def second(t):
                            return t[:, QG * g * W:QG * (g + 1) * W].rearrange("p (e i) -> p e i", i=W)[:, :, P:W]
                        pe.matmul(o, kh[slot][:, P:W], second(qx[slot]), start=True, stop=False)
                        pe.matmul(o, kl[slot][:, P:W], second(qm[slot]), start=False, stop=True).then_inc(q["scores_made"], 1)

                    def values(b, slot, g):
                        pe.wait_ge(q["masked"], b * 8 + (2 * g + 2))
                        if g >= 1:
                            pe.wait_ge(q["ot_ready"], b * NQ + g)
                        elif later(b, 1):
                            pe.wait_ge(q["proj_read"], b)
                        for e in range(QG):
                            first, second = ps_o[:, e * VW:(e + 1) * VW], ps_o[:, 512 + e * VW:512 + (e + 1) * VW]
                            keys0, keys1 = vv[slot][:, 0:VW], vv[slot][:, VW:2 * VW]
                            pe.matmul(first, pt0[g % 2][:, e * W:e * W + P], keys0, start=True, stop=True, skip_group_check=True)
                            pe.matmul(second, pt0[g % 2][:, e * W + P:(e + 1) * W], keys0, start=True, stop=False, skip_group_check=True)
                            last = pe.matmul(second, pt1[g % 2][:, e * P:(e + 1) * P], keys1, start=False, stop=True,
                                             skip_group_check=True)
                        last.then_inc(q["pv_made"], 1)

                    def turn_heads(b, g):
                        pe.wait_ge(q["normed"], b * NQ + (g + 1))
                        for h in range(HALVES):
                            for k in range(2):
                                c = h * HEADS * DH + (2 * g + k) * P
                                last = pe.transpose(ps_o[:, (2 * h + k) * P:(2 * h + k + 1) * P], on[:, c:c + P], ident[:])
                        last.then_inc(q["ot_made"], 1)

                    def project(b):
                        pe.wait_ge(q["ot_ready"], b * NQ + NQ)
                        for h in range(HALVES):
                            for k in range(PAIRS):
                                c = (k // 2) * 512 + (2 * h + k % 2) * P
                                last = pe.matmul(ps_o[:, 512 + h * D:512 + (h + 1) * D], ot[:, c:c + P],
                                                 wo[:, k * D:(k + 1) * D], start=(k == 0), stop=(k == PAIRS - 1), skip_group_check=True)
                        last.then_inc(q["proj_made"], 1)

                    def attend(b, slot):
                        n, other, prep, further = b + 1, 1 - slot, within(b, 1), within(b, 2)
                        scores(b, slot, 1)
                        if later(b, 1):
                            project(b - 1)
                        if prep:
                            queries(n, other, 2)
                            queries(n, other, 3)
                        values(b, slot, 0)
                        if prep:
                            maxima(n, other, 0)
                            maxima(n, other, 1)
                        turn_heads(b, 0)
                        if prep:
                            maxima(n, other, 2)
                            maxima(n, other, 3)
                        scores(b, slot, 2)
                        values(b, slot, 1)
                        if prep:
                            for m in range(4, 7):
                                maxima(n, other, m)
                        turn_heads(b, 1)
                        if prep:
                            for m in range(7, 9):
                                maxima(n, other, m)
                        scores(b, slot, 3)
                        values(b, slot, 2)
                        if prep:
                            for m in range(9, 12):
                                maxima(n, other, m)
                        turn_heads(b, 2)
                        if prep:
                            turn_max(n)
                        if further:
                            turn_z(b + 2, slot)
                        values(b, slot, 3)
                        if prep:
                            scores(n, other, 0)
                        if further:
                            keys(b + 2, slot)
                            queries(b + 2, slot, 0)
                        turn_heads(b, 3)
                        if further:
                            queries(b + 2, slot, 1)
                    pe.wait_ge(q["weights_split"], 1)
                    turn_z(0, 0)
                    keys(0, 0)
                    for u in range(4):
                        queries(0, 0, u)
                    for m in range(12):
                        maxima(0, 0, m)
                    turn_max(0)
                    turn_z(1, 1)
                    scores(0, 0, 0)
                    keys(1, 1)
                    queries(1, 1, 0)
                    queries(1, 1, 1)
                    sequences(attend)(pe)
                    project(B - 1)

        with ExitStack() as ph:
            high = {n: sb("high_" + n, c, F32R, ph) for n, c in
                    [("f1", HID), ("f2", HID), ("h1", HC * HID), ("h2", HC * HID)]}
            low = {n: sb("low_" + n, c, F32R, ph) for n, c in
                   [("f1", HID), ("f2", HID), ("h1", HC * HID), ("h2", HC * HID)]}
            zb = [sb(f"fz{i}", GW, F32, ph) for i in range(2)]
            zh = [sb(f"fzh{i}", GW, F32R, ph) for i in range(2)]
            zl = [sb(f"fzl{i}", GW, F32R, ph) for i in range(2)]
            gate = [sb(f"gate{i}", GW, F32, ph) for i in range(HC)]
            hid = [sb(f"hid{i}", GW, F32, ph) for i in range(HC)]
            top = [sb(f"top{i}", GW, F32, ph) for i in range(HC)]
            hh = [[sb(f"hh{i}{c}", GW, F32R, ph) for c in range(HC)] for i in range(2)]
            hl = [[sb(f"hl{i}{c}", GW, F32R, ph) for c in range(HC)] for i in range(2)]
            oa = sb("ffn_out", GW, F32, ph)
            raw_o, mv_o = sb("raw_out", 6 * GT, F32, ph), sb("mv_out", 2 * GT, F32, ph)
            ve_o, rs_o = sb("ve_out", GT, F32, ph), sb("rs_out", GT, F32, ph)
            bank_a = [psum(f"bank_a{i}", 1, ph) for i in range(HC)]
            bank_b = [psum(f"bank_b{i}", 1, ph) for i in range(HC)]
            names = ["dve_turn", "big_high", "weights_split", "var_ready", "rstd_ready", "zb_ready", "z_made", "zh_ready", "z_ready",
                     "gate_made", "line_made", "one_made", "two_made", "out_made", "gate_ready", "one_ready", "top_ready",
                     "hid_ready", "high_ready", "split_ready", "out_own", "out_read", "var_out", "rs_ready", "x_ready"]
            q = {n: sem("d_" + n, ph) for n in names}
            OUT = 12
            with nc.Block() as block:
                @block.sync
                def _(sp):
                    def put(g):
                        sp.wait_ge(q["x_ready"], g + 1)
                        sp.dma_start(out.rearrange("b (h p) d -> p (b h) d", p=P)[:, ds(g * GT, GT), :],
                                     xs[:, ds(g * GW, GW)].rearrange("p (t d) -> p t d", d=D)).then_inc(all_stored, 16)
                    with sp.Fori(0, NG) as g:
                        put(g)
                    sp.wait_ge(all_stored, 16 * NG)

                @block.gpsimd
                def _(pool):
                    pool.wait_ge(q["var_ready"], 1)
                    pool.tensor_tensor(small["rstd"][:, 0:GT], small["ve"][:, 0:GT], neg_half[:, 0:GT], ALU.pow).then_inc(q["rstd_ready"], 1)
                    pool.tensor_tensor(small["rstd"][:, GT:NT], small["ve"][:, GT:NT], neg_half[:, GT:NT], ALU.pow).then_inc(q["rstd_ready"], 1)
                    with pool.Fori(0, NG) as g:
                        pool.wait_ge(q["var_out"], g + 1)
                        pool.tensor_tensor(rs_o[:], ve_o[:], neg_half[:, 0:GT], ALU.pow).then_inc(q["rs_ready"], 1)

                @block.vector
                def _(dve):
                    w = small
                    mva = mv_all[:].rearrange("p (t k) -> p t k", k=2)
                    dve.tensor_scalar(w["ve"][:], mva[:, :, 1], EPS, None, ALU.add).then_inc(q["var_ready"], 1)
                    dve.wait_ge(ffn_loaded, 16 * 10)
                    for i, n in enumerate(("f1", "f2")):
                        dve.tensor_copy(high[n][:], full[n][:]).then_inc(q["dve_turn"], 1)
                        dve.wait_ge(q["dve_turn"], i + 1)
                        dve.tensor_tensor(low[n][:], full[n][:], high[n][:].bitcast(F32), ALU.subtract).then_inc(q["weights_split"], 1)

                    def low_hidden(i, n):
                        dve.wait_ge(q["big_high"], i + 1)
                        dve.tensor_tensor(low[n][:], full[n][:], high[n][:].bitcast(F32), ALU.subtract).then_inc(q["weights_split"], 1)

                    def normalise(g, slot):
                        if not later(g, 2):
                            dve.wait_ge(q["rstd_ready"], g + 1)
                        else:
                            dve.wait_ge(q["z_made"], g - 1)
                        for j in range(GT):
                            dve.tensor_scalar(zb[slot][:, j * D:(j + 1) * D], xs[:, ds((g * GT + j) * D, D)], mv_all[:, ds((g * GT + j) * 2, 1)],
                                              w["rstd"][:, ds(g * GT + j, 1)], ALU.subtract, ALU.mult).then_inc(q["zb_ready"], 1)

                    def low_z(g, slot):
                        dve.wait_ge(q["zh_ready"], g + 1)
                        dve.tensor_tensor(zl[slot][:], bank_b[1][:], zh[slot][:].bitcast(F32), ALU.subtract).then_inc(q["z_ready"], 1)

                    def split(g, layer, c):
                        dve.tensor_copy(hh[layer][c][:], hid[c][:]).then_inc(q["high_ready"], 1)
                        dve.wait_ge(q["high_ready"], g * 2 * HC + (layer * HC + c + 1))
                        dve.tensor_tensor(hl[layer][c][:], hid[c][:], hh[layer][c][:].bitcast(F32), ALU.subtract).then_inc(q["split_ready"], 1)

                    def gated(g):
                        for c in range(HC):
                            dve.wait_ge(q["gate_ready"], g * HC + (c + 1))
                            dve.wait_ge(q["line_made"], g * HC + (c + 1))
                            dve.scalar_tensor_tensor(out=hid[c][:], in0=bank_b[c][:], scalar=scl["f2"][:, c:c + 1], in1=gate[c][:],
                                                     op0=ALU.mult, op1=ALU.mult).then_inc(q["hid_ready"], 1)
                            dve.wait_ge(q["hid_ready"], g * HC + (c + 1))
                            split(g, 0, c)

                    def hidden(g):
                        for c in range(HC):
                            dve.wait_ge(q["one_ready"], g * HC + (c + 1))
                            split(g, 1, c)

                    def take_out(g):
                        dve.wait_ge(q["out_made"], g + 1)
                        if later(g, 1):
                            dve.wait_ge(q["x_ready"], g)
                        dve.tensor_tensor(oa[:].rearrange("p (t d) -> p t d", d=D), bank_b[0][:].rearrange("p (t d) -> p t d", d=D),
                                          scl3[:].unsqueeze(1).to_broadcast((P, GT, D)), ALU.mult).then_inc(q["out_read"], 1)
                        dve.wait_ge(q["out_read"], g + 1)
                        for j in range(GT):
                            dve.bn_stats(raw_o[:, j * 6:(j + 1) * 6], oa[:, j * D:(j + 1) * D]).then_inc(q["out_own"], 1)
                        dve.wait_ge(q["out_own"], g * OUT + 4)
                        dve.sem_inc(q["dve_turn"], 1)
                        for j in range(GT):
                            dve.bn_aggr(mv_o[:, j * 2:(j + 1) * 2], raw_o[:, j * 6:(j + 1) * 6]).then_inc(q["out_own"], 1)
                        dve.wait_ge(q["out_own"], g * OUT + 8)
                        dve.tensor_scalar(ve_o[:], mv_o[:].rearrange("p (t k) -> p t k", k=2)[:, :, 1], EPS, None, ALU.add).then_inc(q["var_out"], 1)

                    def finish(g):
                        dve.wait_ge(q["rs_ready"], g + 1)
                        for j in range(GT):
                            v = oa[:, j * D:(j + 1) * D]
                            dve.tensor_scalar(v, v, mv_o[:, j * 2:j * 2 + 1], rs_o[:, j:j + 1], ALU.subtract, ALU.mult).then_inc(q["out_own"], 1)
                        dve.wait_ge(q["out_own"], g * OUT + 12)
                        dve.tensor_tensor(xs[:, ds(g * GW, GW)], xs[:, ds(g * GW, GW)], oa[:], ALU.add).then_inc(q["x_ready"], 1)

                    def step(g, slot, more=True):
                        first = isinstance(g, int) and g == 0
                        if more:
                            normalise(g + 1, 1 - slot)
                        gated(g)
                        if first:
                            low_hidden(1, "h2")
                        else:
                            take_out(g - 1)
                        if more:
                            low_z(g + 1, 1 - slot)
                        hidden(g)
                        if not first:
                            finish(g - 1)
                    normalise(0, 0)
                    low_z(0, 0)
                    low_hidden(0, "h1")
                    groups(dve, step)
                    take_out(NG - 1)
                    finish(NG - 1)

                @block.scalar
                def _(act):
                    def high_z(g, slot):
                        act.wait_ge(q["z_made"], g + 1)
                        act.activation(zh[slot][:], bank_b[1][:], ACT.Copy).then_inc(q["zh_ready"], 1)

                    def step(g, slot, more=True):
                        for c in range(HC):
                            act.wait_ge(q["gate_made"], g * HC + (c + 1))
                            act.activation(gate[c][:], bank_a[c][:], ACT.Silu, scale=scl["f1"][:, c:c + 1]).then_inc(q["gate_ready"], 1)
                        if more:
                            high_z(g + 1, 1 - slot)
                        for c in range(HC):
                            act.wait_ge(q["one_made"], g * HC + (c + 1))
                            act.activation(hid[c][:], bank_a[c][:], ACT.Gelu, scale=scl["h1"][:, c:c + 1]).then_inc(q["one_ready"], 1)
                        for c in range(HC):
                            act.wait_ge(q["two_made"], g * HC + (c + 1))
                            act.activation(top[c][:], bank_b[c][:], ACT.Gelu, scale=scl["h2"][:, c:c + 1]).then_inc(q["top_ready"], 1)
                    act.wait_ge(ffn_loaded, 16 * 10)
                    act.activation(high["h1"][:], full["h1"][:], ACT.Copy).then_inc(q["big_high"], 1)
                    high_z(0, 0)
                    act.activation(high["h2"][:], full["h2"][:], ACT.Copy).then_inc(q["big_high"], 1)
                    groups(act, step)

                @block.tensor
                def _(pe):
                    def three(out_ap, lhs, rhs, start=True, stop=True):
                        (lh, ll), (rh, rl) = lhs, rhs
                        pe.matmul(out_ap, lh, rl, start=start, stop=False, skip_group_check=True)
                        pe.matmul(out_ap, ll, rh, start=False, stop=False, skip_group_check=True)
                        return pe.matmul(out_ap, lh, rh, start=False, stop=stop, skip_group_check=True)

                    def turn(g, slot):
                        pe.wait_ge(q["zb_ready"], g * GT + GT)
                        if later(g, 1):
                            pe.wait_ge(q["hid_ready"], g * HC - 2)
                        for j in range(GT):
                            last = pe.transpose(bank_b[1][:, j * P:(j + 1) * P], zb[slot][:, j * D:(j + 1) * D], ident[:])
                        last.then_inc(q["z_made"], 1)

                    def gated(g, slot):
                        pe.wait_ge(q["z_ready"], g + 1)
                        for n, banks, made in (("f1", bank_a, "gate_made"), ("f2", bank_b, "line_made")):
                            for c in range(HC):
                                if n == "f2" and later(g, 1):
                                    pe.wait_ge(q["top_ready"], g * HC + (c + 1 - HC))
                                m = slice(c * P, (c + 1) * P)
                                three(banks[c][:], (high[n][:, m], low[n][:, m]), (zh[slot][:], zl[slot][:])).then_inc(q[made], 1)

                    def hidden(g, layer, more):
                        n, banks, made = (("h1", bank_a, "one_made"), ("h2", bank_b, "two_made"))[layer]
                        if layer == 0:
                            pe.wait_ge(q["gate_ready"], g * HC + HC)
                        else:
                            if later(g, 1):
                                pe.wait_ge(q["out_read"], g)
                            if more:
                                pe.wait_ge(q["z_ready"], g + 2)
                        for k in range(HC):
                            pe.wait_ge(q["split_ready"], g * 2 * HC + (layer * HC + k + 1))
                            for c in range(HC):
                                m = slice(k * HID + c * P, k * HID + (c + 1) * P)
                                last = three(banks[c][:], (high[n][:, m], low[n][:, m]), (hh[layer][k][:], hl[layer][k][:]),
                                             start=(k == 0), stop=(k == HC - 1))
                                if k == HC - 1:
                                    last.then_inc(q[made], 1)

                    def outward(g, ready):
                        if ready is not None:
                            pe.wait_ge(q["hid_ready"], ready)
                        pe.wait_ge(q["top_ready"], g * HC + HC)
                        for t in range(GT):
                            for k in range(HC):
                                m = slice(t * P, (t + 1) * P)
                                last = pe.matmul(bank_b[0][:, m], top[k][:, m], full["f3"][:, k * D:(k + 1) * D],
                                                 start=(k == 0), stop=(k == HC - 1), skip_group_check=True)
                        last.then_inc(q["out_made"], 1)

                    def step(g, slot, more=True):
                        first = isinstance(g, int) and g == 0
                        gated(g, slot)
                        if not first:
                            outward(g - 1, g * HC + 1)
                        if more:
                            turn(g + 1, 1 - slot)
                        if first:
                            pe.wait_ge(q["weights_split"], 3)
                        hidden(g, 0, more)
                        if first:
                            pe.wait_ge(q["weights_split"], 4)
                        hidden(g, 1, more)
                    turn(0, 0)
                    pe.wait_ge(q["weights_split"], 2)
                    groups(pe, step)
                    outward(NG - 1, None)


def constants():
    import numpy as np
    r = np.arange(P)
    c = {}
    c["diff"] = (r[:, None] == r[None, :] + 1) * 1.0 - (r[:, None] == r[None, :]) * 1.0
    c["cross"] = ((r[:, None] == 0) & (r[None, :] == P - 1)) * 1.0
    window = min(8, S - 1)
    band = np.zeros((S, S), np.float32)
    for s in range(1, S):
        w = min(s, window)
        for j in range(w):
            band[s - w + j, s] = np.float32(0.1) + np.float32(0.9) * np.float32(j) / np.float32(max(w - 1, 1)) if w > 1 else 0.1
    c["band00"], c["band10"], c["band11"] = band[:P, :P], band[:P, P:], band[P:, P:]
    c["causal"] = np.where(r[None, :] > r[:, None], MASKED, 0.0)
    c["before"] = (r[:, None] < r[None, :]) * 1.0
    e = np.arange(EXPERTS)
    low = np.zeros((P, P))
    low[:, :EXPERTS * EXPERTS] = (e[None, :] < e[:, None]).reshape(1, -1)
    low[:, EXPERTS * EXPERTS:EXPERTS * EXPERTS + EXPERTS] = e + 1
    c["lower_e"] = low
    c["tile_no"] = np.broadcast_to(r[None, :], (P, P))
    return np.concatenate([c[n] for n in CONSTS], axis=1).astype(np.float32)


def kernel(**inputs):
    import numpy as np
    import concourse.bacc as bacc
    from concourse.bass_utils import run_bass_kernel_spmd as run

    a = {n: np.asarray(v) for n, v in inputs.items()}
    wkt, wvt = a["L1_attn_w_kv"][:DH].T, a["L1_attn_w_kv"][DH:].T

    def chunked(w):
        return w.T.reshape(-1, P, w.shape[0]).transpose(1, 0, 2).reshape(P, -1)

    def columns(v):
        return v.reshape(-1, P).T

    laid = [
        a["L0_attn_embeddings"], a["L0_attn_guidance_trajectories"],
        a["L0_ffn_gate_w"].T, a["L0_ffn_gate_b"],
        a["L0_ffn_w1"].transpose(2, 0, 1).reshape(D, -1), a["L0_ffn_b1"].reshape(-1),
        a["L0_ffn_w2"].reshape(EXPERTS, D, HC, P).transpose(3, 0, 2, 1).reshape(P, -1), a["L0_ffn_b2"].reshape(-1),
        a["L1_attn_w_q"].T, np.concatenate([wkt, wkt], axis=1), wvt, chunked(a["L1_attn_w_out"]),
        a["L1_attn_ln_g"].reshape(P, 1), a["L1_attn_ln_b"].reshape(P, 1), a["L1_attn_lno_g"], a["L1_attn_lno_b"],
        a["L1_ffn_w1_w"].T, columns(a["L1_ffn_w1_s"]), a["L1_ffn_w2_w"].T, columns(a["L1_ffn_w2_s"]),
        chunked(a["L1_ffn_h1_w"]), columns(a["L1_ffn_h1_s"]), chunked(a["L1_ffn_h2_w"]), columns(a["L1_ffn_h2_s"]),
        chunked(a["L1_ffn_w3_w"]), a["L1_ffn_w3_s"],
        constants(),
    ]
    nc = bacc.Bacc("TRN2", target_bir_lowering=False, num_devices=1)
    arrays, args = {}, []
    for i, v in enumerate(laid):
        v = np.ascontiguousarray(v)
        arrays[f"in_{i}"] = v
        args.append(nc.dram_tensor(f"in_{i}", v.shape, mybir.dt.from_np(v.dtype), kind="ExternalInput").ap())
    args.append(nc.dram_tensor("out_0", (B, S, D), F32, kind="ExternalOutput").ap())
    program(nc, *args)
    return run(nc, [arrays], core_ids=[0]).results[0]["out_0"]
```

```python
from contextlib import ExitStack

import concourse.bass as bass
from concourse import mybir

F32 = mybir.dt.float32
F32R = mybir.dt.float32r
I32 = mybir.dt.int32
U32 = mybir.dt.uint32
ALU = mybir.AluOpType
ACT = mybir.ActivationFunctionType
AX = mybir.AxisListType
PE_ENGINE = [mybir.EngineType.PE]
DVE_ENGINE = [mybir.EngineType.DVE]

P = 128
B, S, D = 16, 256, 128
HALVES = S // P
NT = B * HALVES
GT = 4
NG = NT // GT
GW = GT * D
GUIDES = 64
ZW = D + 1
EXPERTS = 8
HID = 4 * D
HC = HID // P
NS = NT + EXPERTS - 1
HEADS, DH = 16, 64
PAIRS = HEADS // 2
QG = 4
NQ = HEADS // QG
EPS = 1e-5
GUIDE_W = 0.4
EPS_MAG = 1e-6
EPS_COS = 1e-8
EPS_WSUM = 1e-8
SCALE = DH ** -0.5
MASKED = -1e30
CONSTS = ["diff", "cross", "band00", "band10", "band11", "causal", "before", "index_e", "tile_no"]


def ds(start, size):
    return bass.ds(start, size)


def skewed(eng, n, unroll, *stages):
    reach = max(lag for lag, _ in stages)
    first = -(-(reach + unroll) // unroll) * unroll
    for s in range(first):
        for lag, f in stages:
            if s >= lag:
                f(s - lag, (s - lag) % unroll)
    with eng.Fori(first // unroll, n // unroll) as i:
        for u in range(unroll):
            for lag, f in stages:
                f(i * unroll + (u - lag), (u - lag) % unroll)
    for s in range(n, n + reach):
        for lag, f in stages:
            if s - lag < n:
                f(s - lag, (s - lag) % unroll)


def later(g, n):
    return not isinstance(g, int) or g >= n


def groups(eng, step):
    step(0, 0)
    step(1, 1)
    with eng.Fori(1, NG // 2 - 1) as i:
        step(i * 2, 0)
        step(i * 2 + 1, 1)
    step(NG - 2, 0)
    step(NG - 1, 1, False)


def tiles(eng, f, unroll=4):
    with eng.Fori(0, NT // unroll) as i:
        for u in range(unroll):
            f(i * unroll + u)


class Chain:

    def __init__(self, eng, sem):
        self.eng, self.sem, self.n = eng, sem, 0

    def add(self, ins, n=1):
        ins.then_inc(self.sem, 1)
        self.n += n

    def wait(self):
        self.eng.wait_ge(self.sem, self.n)

    def link(self, ins):
        self.add(ins)
        self.wait()


def power_by_group(pool, out_, in_, exponent, done):
    for g in range(NG):
        c = slice(g * GT, (g + 1) * GT)
        pool.tensor_tensor(out_[:, c], in_[:, c], exponent[:, c], ALU.pow).then_inc(done, 1)


def combine_stats(ch, st):
    dve = ch.eng
    raw = st["raw"][:].rearrange("p (t k) -> p t k", k=6)
    dve.tensor_tensor(st["mean"][:], raw[:, :, 1], raw[:, :, 4], ALU.add).then_inc(ch.sem, 1)
    dve.tensor_tensor(st["diff"][:], raw[:, :, 1], raw[:, :, 4], ALU.subtract).then_inc(ch.sem, 1)
    dve.tensor_tensor(st["var"][:], raw[:, :, 2], raw[:, :, 5], ALU.add).then_inc(ch.sem, 1)
    ch.n += 3
    ch.wait()
    dve.tensor_scalar(st["mean"][:], st["mean"][:], 0.5, None, ALU.mult).then_inc(ch.sem, 1)
    dve.scalar_tensor_tensor(out=st["diff"][:], in0=st["diff"][:], scalar=0.25, in1=st["diff"][:], op0=ALU.mult,
                             op1=ALU.mult).then_inc(ch.sem, 1)
    ch.n += 2
    ch.wait()
    ch.link(dve.scalar_tensor_tensor(out=st["var"][:], in0=st["var"][:], scalar=1.0 / D, in1=st["diff"][:], op0=ALU.mult,
                                     op1=ALU.add))


def program(nc, x, guides, gate_wt, gate_b, w1t, b1, w2t, b2, wqt, wkt2, wvt, wot, ln_g, ln_b, lno_g, lno_b,
            f1t, f1s, f2t, f2s, h1t, h1s, h2t, h2s, f3t, f3s, consts, out):
    sorted_x = nc.dram_tensor("sorted_x", (NS * P, D), F32).ap()
    sorted_y = nc.dram_tensor("sorted_y", (NS * P, D), F32).ap()
    with ExitStack() as whole:
        def sem(name, stack=whole):
            return stack.enter_context(nc.semaphore(name))

        def sb(name, cols, dt=F32, stack=whole):
            return stack.enter_context(nc.sbuf_tensor(name, [P, cols], dt))

        def psum(name, banks, stack):
            return stack.enter_context(nc.psum_tensor(name, [P, banks * 512], F32))

        xs = sb("xs", NT * D)
        ident = sb("ident", P)
        neg_half = sb("neg_half", NT)
        half = sb("half", NT)
        st = {"raw": sb("stats_raw", NT * 6), "mean": sb("stats_mean", NT), "var": sb("stats_var", NT),
              "diff": sb("stats_diff", NT)}

        def mean(t):
            return st["mean"][:, ds(t, 1)]

        small = {n: sb("small_" + n, NT) for n in
                 ["ve", "rstd", "mag2", "mag", "inv", "ra", "an", "mw", "c6", "wsum", "rs", "shift", "t1", "t2"]}
        cb = sb("consts_sb", len(CONSTS) * P)
        const = {n: cb[:, i * P:(i + 1) * P] for i, n in enumerate(CONSTS)}
        ones = sb("ones", P)
        slot_i = sb("slot_i", NT, I32)
        mv_all = sb("mv_all", NT * 2)
        x_loaded = [sem(f"x_loaded{c}") for c in range(4)]
        consts_loaded, setup_done = sem("consts_loaded"), sem("setup_done")
        moe_loaded, attn_loaded, ffn_loaded = sem("moe_loaded"), sem("attn_loaded"), sem("ffn_loaded")
        sorted_zeroed, sorted_stored = sem("sorted_zeroed"), sem("sorted_stored")
        all_stored = sem("all_stored")

        wq = sb("wq", HEADS * DH)
        wk2 = sb("wk2", P)
        wv = sb("wv", DH)
        wo = sb("wo", PAIRS * D)
        lng, lnb = sb("lng", 1), sb("lnb", 1)
        lnog, lnob = sb("lnog", D), sb("lnob", D)

        def broadcast(ap, n):
            return ap.rearrange("(a n) -> a n", a=1).to_broadcast((P, n))

        moe = ExitStack()
        w1 = sb("w1", EXPERTS * HID, stack=moe)
        w2 = sb("w2", EXPERTS * HID, stack=moe)
        b1s = sb("b1s", EXPERTS * HID, stack=moe)
        b2s = sb("b2s", EXPERTS * D, stack=moe)
        gw = sb("gw", EXPERTS, stack=moe)
        gb = sb("gb", EXPERTS, stack=moe)
        rows = sb("rows", NS * D, stack=moe)
        score = sb("score", NT * EXPERTS, stack=moe)
        MOE_LOADS = 6

        with ExitStack() as ph:
            y = sb("y", NT * D, stack=ph)
            dif = sb("dif", NT * D, stack=ph)
            sq = [sb(f"sq{i}", GW, stack=ph) for i in range(2)]
            z = sb("z", NT * ZW, stack=ph)
            zt = z[:].rearrange("p (t k) -> p t k", k=ZW)
            nh = [sb(f"nh{i}", GW, stack=ph) for i in range(2)]
            nht = [sb(f"nht{i}", GW, stack=ph) for i in range(2)]
            et = [sb(f"et{i}", GW, stack=ph) for i in range(2)]
            guide = sb("guide", ZW, stack=ph)
            guide_n = sb("guide_n", D, stack=ph)
            guide_sq = sb("guide_sq", D, stack=ph)
            gt = sb("gt", GUIDES, stack=ph)
            gs = sb("gs", 4, stack=ph)
            c4 = [sb(f"c4{i}", GT, stack=ph) for i in range(2)]
            raw_x = [sb(f"sum_raw{i}", 6 * GT, stack=ph) for i in range(2)]
            mv_x = [sb(f"sum_mv{i}", 2 * GT, stack=ph) for i in range(2)]
            u = sb("u", NT * ZW, stack=ph)
            ut = u[:].rearrange("p (t k) -> p t k", k=ZW)
            ps_a = [psum(f"ps_a{i}", 1, ph) for i in range(2)]
            ps_s = [psum(f"ps_s{i}", 1, ph) for i in range(2)]
            ps_i = [psum(f"ps_i{i}", 2, ph) for i in range(2)]
            names = ["dve_done", "guide_loaded", "guide_mag2", "guide_mag", "guide_scaled", "guide_t", "guide_ready",
                     "var_ready", "rstd_ready", "y_ready", "diff_made", "sq_free", 
                     "mag_ready", "tanh_ready", "nh_ready", "nht_made", "nht_ready", "sims_made",
                     "exp_ready", "infl_made", "z_ready", "u_made", "u_ready", "var2_ready",
                     "rs_ready", "et_zero", "sq_ready", "scaled", "shift_ready", "moved", "added",
                     "raw_ready", "mv_ready", "added_mean", "var_x", "rstd_x", "xn_ready", "xt_made", "xt_ready", "logits_made", "logits_read",
                     "dve_turn"]
            q = {n: sem("a_" + n, ph) for n in names}
            with nc.Block() as block:
                @block.sync
                def _(sp):
                    for c in range(4):
                        sp.dma_start(xs[:, c * 8 * D:(c + 1) * 8 * D].rearrange("p (t d) -> p t d", d=D),
                                     x.rearrange("b (h p) d -> p (b h) d", p=P)[:, c * 8:(c + 1) * 8, :]).then_inc(x_loaded[c], 16)
                    sp.dma_start(cb[:], consts).then_inc(consts_loaded, 16)
                    sp.dma_start(guide[0:GUIDES, 0:D], guides).then_inc(q["guide_loaded"], 16)
                    sp.wait_ge(setup_done, 6)
                    sp.dma_start(sorted_x.rearrange("(k p) d -> p k d", p=P),
                                 rows[:].rearrange("p (k d) -> p k d", d=D)).then_inc(sorted_zeroed, 16)
                    for dst, src in ((w1[:], w1t), (w2[:], w2t), (b1s[:], broadcast(b1, EXPERTS * HID)),
                                     (b2s[:], broadcast(b2, EXPERTS * D)), (gw[:], gate_wt),
                                     (gb[:], broadcast(gate_b, EXPERTS))):
                        sp.dma_start(dst, src).then_inc(moe_loaded, 16)
                    for dst, src in ((wq[:], wqt), (wk2[:], wkt2), (wv[:], wvt), (wo[:], wot), (lng[:], ln_g), (lnb[:], ln_b),
                                     (lnog[:], broadcast(lno_g, D)), (lnob[:], broadcast(lno_b, D))):
                        sp.dma_start(dst, src).then_inc(attn_loaded, 16)
                    sp.wait_ge(consts_loaded, 16)
                    sp.wait_ge(sorted_zeroed, 16)

                @block.gpsimd
                def _(pool):
                    pool.memset(neg_half[:], -0.5).then_inc(setup_done, 1)
                    pool.memset(half[:], 0.5).then_inc(setup_done, 1)
                    pool.memset(ident[:], 0.0).then_inc(setup_done, 1)
                    pool.memset(ones[:], 1.0).then_inc(setup_done, 1)
                    pool.wait_ge(setup_done, 4)
                    pool.affine_select(out=ident[:], in_=ident[:], compare_op=ALU.not_equal, fill=1.0, base=0,
                                       pattern=[[-1, P]], channel_multiplier=1).then_inc(setup_done, 1)
                    pool.memset(rows[:], 0.0).then_inc(setup_done, 1)
                    pool.wait_ge(q["var_ready"], 1)
                    power_by_group(pool, small["rstd"], small["ve"], neg_half, q["rstd_ready"])
                    pool.wait_ge(q["guide_mag2"], 1)
                    pool.tensor_tensor(gs[0:GUIDES, 1:2], gs[0:GUIDES, 0:1], half[0:GUIDES, 0:1], ALU.pow).then_inc(q["guide_mag"], 1)
                    for g in range(NG):
                        c = slice(g * GT, (g + 1) * GT)
                        pool.wait_ge(q["sq_free"], g + 1)
                        pool.tensor_tensor(small["mag"][:, c], small["mag2"][:, c], half[:, c], ALU.pow).then_inc(q["mag_ready"], 1)
                    pool.wait_ge(q["var2_ready"], 1)
                    power_by_group(pool, small["rs"], small["ve"], neg_half, q["rs_ready"])
                    for g in range(NG):
                        c = slice(g * GT, (g + 1) * GT)
                        pool.wait_ge(q["var_x"], g + 1)
                        pool.tensor_tensor(small["rstd"][:, c], small["ve"][:, c], neg_half[:, c], ALU.pow).then_inc(q["rstd_x"], 1)

                @block.vector
                def _(dve):
                    ch = Chain(dve, q["dve_done"])
                    dve.memset(guide[GUIDES:P, :], 0.0).then_inc(q["et_zero"], 1)
                    for i in range(2):
                        dve.memset(et[i][GUIDES:P, :], 0.0).then_inc(q["et_zero"], 1)
                    for c in range(4):
                        dve.wait_ge(x_loaded[c], 16)
                        for t in range(c * NT // 4, (c + 1) * NT // 4):
                            ch.add(dve.bn_stats(st["raw"][:, t * 6:(t + 1) * 6], xs[:, t * D:(t + 1) * D]))
                    ch.wait()
                    combine_stats(ch, st)
                    dve.tensor_scalar(small["ve"][:], st["var"][:], EPS, None, ALU.add).then_inc(q["var_ready"], 1)
                    dve.wait_ge(q["guide_loaded"], 16)
                    ch.link(dve.tensor_tensor(guide_sq[0:GUIDES, :], guide[0:GUIDES, 0:D], guide[0:GUIDES, 0:D], ALU.mult))
                    ch.link(dve.memset(guide[0:GUIDES, D:ZW], 1.0))
                    dve.reduce_sum(gs[0:GUIDES, 0:1], guide_sq[0:GUIDES, :], AX.X).then_inc(q["guide_mag2"], 1)

                    def normalise(g, slot):
                        dve.wait_ge(q["rstd_ready"], g + 1)
                        for j in range(GT):
                            t = g * GT + j
                            dve.tensor_scalar(y[:, ds(t * D, D)], xs[:, ds(t * D, D)], mean(t), small["rstd"][:, ds(t, 1)], ALU.subtract,
                                              ALU.mult).then_inc(q["y_ready"], 1)

                    def mag2(g, slot):
                        dve.wait_ge(q["sq_ready"], g + 1)
                        dve.reduce_sum(small["mag2"][:, ds(g * GT, GT)], sq[slot][:].rearrange("p (t d) -> p t d", d=D),
                                       AX.X).then_inc(q["sq_free"], 1)
                    skewed(dve, NG, 2, (0, normalise), (2, mag2))
                    dve.wait_ge(q["guide_mag"], 1)
                    ch.link(dve.tensor_scalar(gs[0:GUIDES, 2:3], gs[0:GUIDES, 1:2], EPS_COS, None, ALU.max))
                    ch.link(dve.reciprocal(gs[0:GUIDES, 3:4], gs[0:GUIDES, 2:3]))
                    dve.tensor_scalar(guide_n[0:GUIDES, :], guide[0:GUIDES, 0:D], gs[0:GUIDES, 3:4], None,
                                      ALU.mult).then_inc(q["guide_scaled"], 1)
                    dve.wait_ge(q["mag_ready"], NG)
                    w = small
                    ch.link(dve.tensor_scalar(w["t1"][:], w["mag"][:], EPS_MAG, None, ALU.is_gt))
                    ch.link(dve.tensor_scalar(w["t2"][:], w["mag"][:], EPS_MAG, None, ALU.max))
                    ch.link(dve.reciprocal(w["inv"][:], w["t2"][:]))
                    ch.link(dve.tensor_tensor(w["inv"][:], w["inv"][:], w["t1"][:], ALU.mult))
                    ch.link(dve.tensor_tensor(w["an"][:], w["mag"][:], w["inv"][:], ALU.mult))
                    ch.link(dve.tensor_scalar(w["an"][:], w["an"][:], EPS_COS, None, ALU.max))
                    ch.link(dve.reciprocal(w["ra"][:], w["an"][:]))
                    ch.link(dve.tensor_tensor(w["ra"][:], w["ra"][:], w["inv"][:], ALU.mult))
                    dve.wait_ge(q["tanh_ready"], 1)
                    ch.link(dve.scalar_tensor_tensor(out=w["c6"][:], in0=w["inv"][:], scalar=1.0 - GUIDE_W, in1=w["mw"][:],
                                                     op0=ALU.mult, op1=ALU.mult))
                    ch.link(dve.tensor_copy(zt[:, :, D], w["mw"][:]))

                    def scale_dirs(g, slot):
                        def one(j):
                            return dve.tensor_scalar(nh[slot][:, j * D:(j + 1) * D], dif[:, ds((g * GT + j) * D, D)],
                                                     w["ra"][:, ds(g * GT + j, 1)], None, ALU.mult)
                        if later(g, 2):
                            dve.wait_ge(q["nht_made"], g - 1)
                        for j in range(GT):
                            one(j).then_inc(q["nh_ready"], 1)

                    base = ch.n
                    PER = 2 + GT

                    def blend(g, slot):
                        pi = ps_i[slot][:].rearrange("p (k c) -> p k c", k=2)[:, :, 0:2 * ZW].rearrange("p k (j c) -> p k j c", c=ZW)
                        dve.wait_ge(q["infl_made"], g + 1)
                        c = c4[slot][:].rearrange("p (k j) -> p k j", k=2)
                        dve.reciprocal(c, pi[:, :, :, D]).then_inc(ch.sem, 1)
                        dve.wait_ge(ch.sem, g * PER + (base + 1))
                        dve.scalar_tensor_tensor(out=c4[slot][:], in0=c4[slot][:], scalar=GUIDE_W,
                                                 in1=w["mw"][:, ds(g * GT, GT)], op0=ALU.mult, op1=ALU.mult).then_inc(ch.sem, 1)
                        dve.wait_ge(ch.sem, g * PER + (base + 2))
                        for j in range(GT):
                            dve.tensor_scalar(z[:, ds((g * GT + j) * ZW, D)], pi[:, j // 2, j % 2, 0:D], c4[slot][:, j:j + 1], None,
                                              ALU.mult).then_inc(ch.sem, 1)
                        dve.wait_ge(ch.sem, g * PER + (base + 2 + GT))
                        for j in range(GT):
                            dve.scalar_tensor_tensor(out=z[:, ds((g * GT + j) * ZW, D)], in0=dif[:, ds((g * GT + j) * D, D)],
                                                     scalar=w["c6"][:, ds(g * GT + j, 1)], in1=z[:, ds((g * GT + j) * ZW, D)],
                                                     op0=ALU.mult, op1=ALU.add).then_inc(q["z_ready"], 1)
                    skewed(dve, NG, 2, (0, scale_dirs), (3, blend))
                    ch.n += NG * PER

                    def stats_of_u(g, slot):
                        dve.wait_ge(q["u_ready"], 2 * g + 2)
                        for j in range(GT):
                            dve.bn_stats(st["raw"][:, ds((g * GT + j) * 6, 6)], u[:, ds((g * GT + j) * ZW, D)]).then_inc(ch.sem, 1)
                    skewed(dve, NG, 2, (0, stats_of_u))
                    ch.n += NT
                    ch.wait()
                    combine_stats(ch, st)
                    ch.link(dve.tensor_scalar(w["wsum"][:], ut[:, :, D], EPS_WSUM, None, ALU.max))
                    ch.link(dve.reciprocal(w["t1"][:], w["wsum"][:]))
                    ch.link(dve.tensor_tensor(w["t2"][:], w["t1"][:], w["t1"][:], ALU.mult))
                    ch.link(dve.tensor_tensor(w["ve"][:], st["var"][:], w["t2"][:], ALU.mult))
                    dve.tensor_scalar(w["ve"][:], w["ve"][:], EPS, None, ALU.add).then_inc(q["var2_ready"], 1)

                    def scale_and_shift(g, slot):
                        c = ds(g * GT, GT)
                        dve.wait_ge(q["rs_ready"], g + 1)
                        dve.tensor_tensor(w["rs"][:, c], w["rs"][:, c], w["t1"][:, c], ALU.mult).then_inc(q["scaled"], 1)
                        dve.wait_ge(q["scaled"], g + 1)
                        dve.scalar_tensor_tensor(out=w["shift"][:, c], in0=st["mean"][:, c], scalar=-1.0, in1=w["rs"][:, c], op0=ALU.mult,
                                                 op1=ALU.mult).then_inc(q["shift_ready"], 1)

                    def add(g, slot):
                        dve.wait_ge(q["moved"], g * GT + GT)
                        xg = xs[:, ds(g * GW, GW)].rearrange("p (t d) -> p t d", d=D)
                        ug = u[:, ds(g * GT * ZW, GT * ZW)].rearrange("p (t k) -> p t k", k=ZW)[:, :, 0:D]
                        dve.tensor_tensor(xg, xg, ug, ALU.add).then_inc(q["added"], 1)
                        dve.wait_ge(q["added"], g + 1)
                        for j in range(GT):
                            dve.bn_stats(raw_x[slot][:, j * 6:(j + 1) * 6], xs[:, ds((g * GT + j) * D, D)]).then_inc(q["raw_ready"], 1)
                        dve.wait_ge(q["raw_ready"], g * GT + GT)
                        dve.sem_inc(q["dve_turn"], 1)
                        for j in range(GT):
                            dve.bn_aggr(mv_x[slot][:, j * 2:(j + 1) * 2], raw_x[slot][:, j * 6:(j + 1) * 6]).then_inc(q["mv_ready"], 1)
                        dve.wait_ge(q["mv_ready"], g * GT + GT)
                        mv = mv_x[slot][:].rearrange("p (t k) -> p t k", k=2)
                        dve.tensor_scalar(w["ve"][:, ds(g * GT, GT)], mv[:, :, 1], EPS, None, ALU.add).then_inc(q["var_x"], 1)
                        dve.tensor_copy(st["mean"][:, ds(g * GT, GT)], mv[:, :, 0]).then_inc(q["added_mean"], 1)

                    def normalise_x(g, slot):
                        if later(g, 2):
                            dve.wait_ge(q["xt_made"], g - 1)
                        dve.wait_ge(q["added_mean"], g + 1)
                        dve.wait_ge(q["rstd_x"], g + 1)
                        for j in range(GT):
                            dve.tensor_scalar(nh[slot][:, j * D:(j + 1) * D], xs[:, ds((g * GT + j) * D, D)], mean(g * GT + j),
                                              w["rstd"][:, ds(g * GT + j, 1)], ALU.subtract, ALU.mult).then_inc(q["xn_ready"], 1)

                    def take_logits(g, slot):
                        dve.wait_ge(q["logits_made"], g + 1)
                        dve.tensor_tensor(score[:, ds(g * GT * EXPERTS, GT * EXPERTS)].rearrange("p (t e) -> p t e", e=EXPERTS),
                                          ps_s[slot][:, 0:GT * EXPERTS].rearrange("p (t e) -> p t e", e=EXPERTS),
                                          gb[:].unsqueeze(1).to_broadcast((P, GT, EXPERTS)), ALU.add).then_inc(q["logits_read"], 1)
                    dve.wait_ge(moe_loaded, 16 * MOE_LOADS)
                    skewed(dve, NG, 2, (0, scale_and_shift), (1, add), (2, normalise_x), (4, take_logits))
                    dve.wait_ge(q["logits_read"], NG)

                @block.scalar
                def _(act):

                    def square(g, slot):
                        act.wait_ge(q["diff_made"], g + 1)
                        act.activation(dif[:, ds(g * GW, GW)], ps_a[slot][:], ACT.Copy)
                        if later(g, 2):
                            act.wait_ge(q["sq_free"], g - 1)
                        act.activation(sq[slot][:], ps_a[slot][:], ACT.Square).then_inc(q["sq_ready"], 1)
                    skewed(act, NG, 2, (0, square))
                    act.wait_ge(q["guide_t"], 1)
                    act.activation(gt[:], ps_s[0][:, 0:GUIDES], ACT.Copy).then_inc(q["guide_ready"], 1)
                    act.wait_ge(q["mag_ready"], NG)
                    act.activation(small["mw"][:], small["mag"][:], ACT.Tanh, scale=2.0).then_inc(q["tanh_ready"], 1)

                    def turn(g, slot):
                        act.wait_ge(q["nht_made"], g + 1)
                        act.activation(nht[slot][:], ps_a[slot][:], ACT.Copy).then_inc(q["nht_ready"], 1)

                    def weigh(g, slot):
                        act.wait_ge(q["sims_made"], g + 1)
                        act.activation(et[slot][0:GUIDES, :], ps_s[slot][0:GUIDES, :], ACT.Exp, scale=2.0).then_inc(q["exp_ready"], 1)
                    skewed(act, NG, 2, (0, turn), (1, weigh))

                    def copy_u(g, slot):
                        act.wait_ge(q["u_made"], g + 1)
                        uv = u[:, ds(g * GT * ZW, GT * ZW)].rearrange("p (b h c) -> p b h c", b=2, h=2)
                        for h, bank in enumerate((ps_a[slot], ps_s[slot])):
                            act.activation(uv[:, :, h, :], bank[:, 0:2 * ZW].rearrange("p (b c) -> p b c", b=2),
                                           ACT.Copy).then_inc(q["u_ready"], 1)
                    skewed(act, NG, 2, (0, copy_u))

                    def move(g, slot):
                        act.wait_ge(q["shift_ready"], g + 1)
                        for j in range(GT):
                            t = g * GT + j
                            act.activation(u[:, ds(t * ZW, D)], u[:, ds(t * ZW, D)], ACT.Identity, scale=small["rs"][:, ds(t, 1)],
                                           bias=small["shift"][:, ds(t, 1)]).then_inc(q["moved"], 1)

                    def turn_x(g, slot):
                        act.wait_ge(q["xt_made"], g + 1)
                        if later(g, 2):
                            act.wait_ge(q["logits_made"], g - 1)
                        act.activation(nht[slot][:], ps_a[slot][:], ACT.Copy).then_inc(q["xt_ready"], 1)
                    skewed(act, NG, 2, (0, move), (3, turn_x))

                @block.tensor
                def _(pe):
                    pe.wait_ge(setup_done, 6)
                    pe.wait_ge(consts_loaded, 16)

                    def differences(g, slot):
                        pe.wait_ge(q["y_ready"], g * GT + GT)
                        if later(g, 2):
                            pe.wait_ge(q["sq_ready"], g - 1)
                        yg = y[:, ds(g * GW, GW)]
                        pe.matmul(ps_a[slot][:], const["diff"], yg, start=True, stop=False)
                        pe.matmul(ps_a[slot][:].rearrange("p (b h d) -> p b h d", b=2, h=2)[:, :, 0, :], const["cross"],
                                  yg.rearrange("p (b h d) -> p b h d", b=2, h=2)[:, :, 1, :],
                                  start=False, stop=True).then_inc(q["diff_made"], 1)
                    skewed(pe, NG, 2, (0, differences))
                    pe.wait_ge(q["sq_ready"], NG)
                    pe.wait_ge(q["guide_scaled"], 1)
                    pe.transpose(ps_s[0][:, 0:GUIDES], guide_n[0:GUIDES, :], ident[0:GUIDES, 0:GUIDES]).then_inc(q["guide_t"], 1)
                    pe.wait_ge(q["guide_ready"], 1)
                    pe.wait_ge(q["et_zero"], 3)

                    def turn(g, slot):
                        pe.wait_ge(q["nh_ready"], g * GT + GT)
                        if later(g, 2):
                            pe.wait_ge(q["nht_ready"], g - 1)
                        for j in range(GT):
                            last = pe.transpose(ps_a[slot][:, j * D:(j + 1) * D], nh[slot][:, j * D:(j + 1) * D], ident[:])
                        last.then_inc(q["nht_made"], 1)

                    def sims(g, slot):
                        pe.wait_ge(q["nht_ready"], g + 1)
                        if later(g, 2):
                            pe.wait_ge(q["exp_ready"], g - 1)
                        pe.matmul(ps_s[slot][0:GUIDES, :], gt[:], nht[slot][:], start=True, stop=True).then_inc(q["sims_made"], 1)

                    def influence(g, slot):
                        pe.wait_ge(q["exp_ready"], g + 1)
                        if later(g, 2):
                            pe.wait_ge(q["z_ready"], (g - 1) * GT)
                        for j in range(GT):
                            last = pe.matmul(ps_i[slot][:, (j // 2) * 512 + (j % 2) * ZW:][:, 0:ZW], et[slot][:, j * D:(j + 1) * D],
                                             guide[:], start=(j % 2 == 0), stop=True, skip_group_check=True)
                        last.then_inc(q["infl_made"], 1)
                    skewed(pe, NG, 2, (0, turn), (1, sims), (2, influence))

                    def window(g, slot):
                        pe.wait_ge(q["z_ready"], g * GT + GT)
                        if later(g, 2):
                            pe.wait_ge(q["u_ready"], 2 * g - 2)
                        zg = z[:, ds(g * GT * ZW, GT * ZW)].rearrange("p (b h c) -> p b h c", b=2, h=2)
                        o = [bank[:, 0:2 * ZW].rearrange("p (b c) -> p b c", b=2) for bank in (ps_a[slot], ps_s[slot])]
                        pe.matmul(o[0], const["band00"], zg[:, :, 0, :], start=True, stop=True)
                        pe.matmul(o[1], const["band10"], zg[:, :, 0, :], start=True, stop=False)
                        pe.matmul(o[1], const["band11"], zg[:, :, 1, :], start=False, stop=True).then_inc(q["u_made"], 1)
                    skewed(pe, NG, 2, (0, window))
                    pe.wait_ge(moe_loaded, 16 * MOE_LOADS)

                    def turn_x(g, slot):
                        pe.wait_ge(q["xn_ready"], g * GT + GT)
                        if later(g, 2):
                            pe.wait_ge(q["xt_ready"], g - 1)
                        for j in range(GT):
                            last = pe.transpose(ps_a[slot][:, j * D:(j + 1) * D], nh[slot][:, j * D:(j + 1) * D], ident[:])
                        last.then_inc(q["xt_made"], 1)

                    def gate(g, slot):
                        pe.wait_ge(q["xt_ready"], g + 1)
                        if later(g, 2):
                            pe.wait_ge(q["logits_read"], g - 1)
                        for j in range(GT):
                            last = pe.matmul(ps_s[slot][:, j * EXPERTS:(j + 1) * EXPERTS], nht[slot][:, j * P:(j + 1) * P], gw[:],
                                             start=True, stop=True)
                        last.then_inc(q["logits_made"], 1)
                    skewed(pe, NG, 2, (0, turn_x), (1, gate))


        with ExitStack() as ph:
            ys = sb("ys", NT * D, stack=ph)
            TE = NT * EXPERTS
            r = {n: sb("r_" + n, TE, stack=ph) for n in ["rank", "chosen", "key", "onehot", "tot", "acc0", "acc1", "slot"]}
            r["score"] = score
            cmp_a = sb("cmp_a", TE * EXPERTS, stack=ph)
            cmp_b = sb("cmp_b", TE * EXPERTS, stack=ph)
            e8 = {n: sb("e8_" + n, EXPERTS, stack=ph) for n in ["tiles", "acc0", "acc1", "first"]}
            t32 = {n: sb("t32_" + n, NT, stack=ph) for n in ["max", "sum", "w", "slot"]}
            expert_f = sb("expert_f", NS, stack=ph)
            expert_i = sb("expert_i", NS, I32, stack=ph)
            xin = [sb(f"xin{i}", D, stack=ph) for i in range(3)]
            xt = [sb(f"xt{i}", P, stack=ph) for i in range(3)]
            hp = [sb(f"hp{i}", HID, stack=ph) for i in range(3)]
            ht = [sb(f"ht{i}", HID, stack=ph) for i in range(3)]
            e_up = [sb(f"e_up{i}", 1, I32, stack=ph) for i in range(3)]
            e_down = [sb(f"e_down{i}", 1, I32, stack=ph) for i in range(3)]
            res = sb("res", NS * D, stack=ph)
            bank = [psum(f"bank{i}", 1, ph) for i in range(8)]
            names = ["dve_done",
                     "shifted", "exp_ready", "onehot_ready", "counts_made", "slots_ready", "ys_ready", "scattered",
                     "first_loaded", "rows_loaded", "xin_ready", "xt_made", "xt_ready", "h_made", "hp_ready", "ht_made", "ht_ready", "o_made",
                     "res_ready", "expert_ready", "e_up_ready", "e_down_ready"]
            q = {n: sem("b_" + n, ph) for n in names}
            AHEAD = 3
            with nc.Block() as block:
                @block.sync
                def _(sp):
                    sp.wait_ge(q["scattered"], 16 * NT)
                    for a, b, loaded in ((0, AHEAD, "first_loaded"), (AHEAD, NS, "rows_loaded")):
                        sp.dma_start(rows[:, a * D:b * D].rearrange("p (k d) -> p k d", d=D),
                                     sorted_x.rearrange("(k p) d -> p k d", p=P)[:, a:b, :]).then_inc(q[loaded], 16)
                    for a, b in ((0, NS // 2), (NS // 2, NS - AHEAD), (NS - AHEAD, NS)):
                        sp.wait_ge(q["res_ready"], b)
                        sp.dma_start(sorted_y.rearrange("(k p) d -> p k d", p=P)[:, a:b, :],
                                     res[:, a * D:b * D].rearrange("p (k d) -> p k d", d=D)).then_inc(sorted_stored, 16)

                @block.gpsimd
                def _(pool):
                    pool.wait_ge(q["slots_ready"], 1)
                    for t in range(NT):
                        if t % 4 == 0:
                            pool.wait_ge(q["ys_ready"], t + 4)
                        pool.indirect_dma_start(out=sorted_x, out_offset=bass.IndirectOffsetOnAxis(ap=slot_i[:, t:t + 1].bitcast(U32), axis=0),
                                                in_=ys[:, t * D:(t + 1) * D], in_offset=None).then_inc(q["scattered"], 16)
                    pool.wait_ge(q["expert_ready"], 1)

                    def pick(k, slot):
                        pool.wait_ge(q["rows_loaded" if later(k, AHEAD) else "first_loaded"], 16)
                        if later(k, 3):
                            pool.wait_ge(q["xt_made"], k - 2)
                            pool.wait_ge(q["hp_ready"], k - 2)
                        pool.tensor_copy(e_up[slot][:], expert_i[:, ds(k, 1)]).then_inc(q["e_up_ready"], 1)
                        pool.tensor_copy(xin[slot][:], rows[:, ds(k * D, D)]).then_inc(q["xin_ready"], 1)
                    skewed(pool, NS, 3, (0, pick))

                @block.vector
                def _(dve):
                    ch = Chain(dve, q["dve_done"])
                    w = small
                    def te(name):
                        return r[name][:].rearrange("p (t e) -> p t e", e=EXPERTS)

                    def over_e(ap):
                        return ap.unsqueeze(2).to_broadcast((P, NT, EXPERTS))

                    ch.link(dve.reduce_max(t32["max"][:], te("score"), AX.X))
                    dve.tensor_tensor(te("score"), te("score"), over_e(t32["max"][:]), ALU.subtract).then_inc(q["shifted"], 1)
                    dve.wait_ge(q["exp_ready"], 1)
                    ch.link(dve.reduce_sum(t32["sum"][:], te("key"), AX.X))
                    ch.link(dve.reciprocal(t32["sum"][:], t32["sum"][:]))
                    ch.link(dve.tensor_tensor(te("score"), te("key"), over_e(t32["sum"][:]), ALU.mult))
                    rising = const["index_e"][:, 0:EXPERTS].unsqueeze(1).to_broadcast((P, NT, EXPERTS))
                    falling = const["index_e"][:, EXPERTS:2 * EXPERTS].unsqueeze(1).to_broadcast((P, NT, EXPERTS))

                    def first_largest(out_, of):
                        ch.link(dve.reduce_max(t32["max"][:], te(of), AX.X))
                        ch.link(dve.tensor_tensor(te("key"), te(of), over_e(t32["max"][:]), ALU.is_equal))
                        ch.link(dve.tensor_tensor(te("key"), te("key"), falling, ALU.mult))
                        ch.link(dve.reduce_max(t32["max"][:], te("key"), AX.X))
                        ch.link(dve.tensor_tensor(te(out_), te("key"), over_e(t32["max"][:]), ALU.is_equal))
                    first_largest("rank", "score")
                    ch.link(dve.scalar_tensor_tensor(out=r["slot"][:], in0=r["rank"][:], scalar=-2.0, in1=r["score"][:],
                                                     op0=ALU.mult, op1=ALU.add))
                    first_largest("chosen", "slot")
                    ch.link(dve.tensor_tensor(r["chosen"][:], r["chosen"][:], r["rank"][:], ALU.add))
                    ch.link(dve.scalar_tensor_tensor(out=r["chosen"][:], in0=r["score"][:], scalar=0.0, in1=r["chosen"][:],
                                                     op0=ALU.is_gt, op1=ALU.mult))
                    ch.link(dve.tensor_tensor(te("key"), te("chosen"), rising, ALU.mult))
                    ch.link(dve.reduce_max(t32["max"][:], te("key"), AX.X))
                    ch.link(dve.tensor_tensor(te("onehot"), te("key"), over_e(t32["max"][:]), ALU.is_equal))
                    dve.tensor_tensor(r["onehot"][:], r["onehot"][:], r["chosen"][:], ALU.mult).then_inc(q["onehot_ready"], 1)
                    dve.wait_ge(q["onehot_ready"], 1)
                    ch.link(dve.tensor_tensor(r["rank"][:], r["onehot"][:], r["score"][:], ALU.mult))
                    ch.link(dve.reduce_sum(t32["w"][:], te("rank"), AX.X))
                    ch.link(dve.tensor_tensor(w["t1"][:], t32["w"][:], w["rstd"][:], ALU.mult))
                    dve.wait_ge(q["counts_made"], 1)
                    ch.add(dve.tensor_copy(r["tot"][:], bank[5][:, 0:TE]))
                    ch.link(dve.tensor_copy(r["acc0"][:], bank[5][:, 0:TE]))
                    now, nxt = "acc0", "acc1"
                    step = 1
                    while step < NT:
                        k = step * EXPERTS
                        ch.add(dve.tensor_copy(r[nxt][:, 0:k], r[now][:, 0:k]))
                        ch.link(dve.tensor_tensor(r[nxt][:, k:TE], r[now][:, k:TE], r[now][:, 0:TE - k], ALU.add))
                        now, nxt, step = nxt, now, 2 * step
                    count = r[now][:, TE - EXPERTS:TE]
                    many = cmp_a[:, 0:EXPERTS * NT].rearrange("p (e k) -> p e k", k=NT)
                    ch.link(dve.tensor_scalar(cmp_b[:, 0:NT], const["tile_no"][:, 0:NT], float(P), None, ALU.mult))
                    ch.link(dve.tensor_tensor(many, count.unsqueeze(2).to_broadcast((P, EXPERTS, NT)),
                                              cmp_b[:, 0:NT].unsqueeze(1).to_broadcast((P, EXPERTS, NT)), ALU.is_gt))
                    ch.link(dve.reduce_sum(e8["tiles"][:], many, AX.X))
                    ch.link(dve.tensor_copy(e8["acc0"][:], e8["tiles"][:]))
                    a, b_ = "acc0", "acc1"
                    step = 1
                    while step < EXPERTS:
                        ch.add(dve.tensor_copy(e8[b_][:, 0:step], e8[a][:, 0:step]))
                        ch.link(dve.tensor_tensor(e8[b_][:, step:], e8[a][:, step:], e8[a][:, 0:EXPERTS - step], ALU.add))
                        a, b_, step = b_, a, 2 * step
                    ch.link(dve.tensor_tensor(e8["first"][:], e8[a][:], e8["tiles"][:], ALU.subtract))
                    ch.link(dve.tensor_scalar(e8["first"][:], e8["first"][:], float(P), None, ALU.mult))
                    ch.link(dve.tensor_tensor(r["slot"][:], r[now][:], r["tot"][:], ALU.subtract))
                    ch.link(dve.tensor_tensor(r["slot"][:], bank[4][:, 0:TE], r["slot"][:], ALU.add))
                    ch.link(dve.tensor_tensor(te("slot"), te("slot"), e8["first"][:].unsqueeze(1).to_broadcast((P, NT, EXPERTS)), ALU.add))
                    ch.link(dve.tensor_tensor(r["slot"][:], r["slot"][:], r["onehot"][:], ALU.mult))
                    ch.link(dve.reduce_sum(t32["slot"][:], te("slot"), AX.X))
                    dve.tensor_copy(slot_i[:], t32["slot"][:]).then_inc(q["slots_ready"], 1)
                    tiles(dve, lambda t: dve.tensor_scalar(ys[:, ds(t * D, D)], xs[:, ds(t * D, D)], mean(t), w["t1"][:, ds(t, 1)],
                                                           ALU.subtract, ALU.mult).then_inc(q["ys_ready"], 1))
                    ended = cmp_a[:, 0:NS * EXPERTS].rearrange("p (k e) -> p k e", e=EXPERTS)
                    ch.link(dve.tensor_tensor(ended, const["tile_no"][:, 0:NS].unsqueeze(2).to_broadcast((P, NS, EXPERTS)),
                                              e8[a][:].unsqueeze(1).to_broadcast((P, NS, EXPERTS)), ALU.is_ge))
                    ch.link(dve.reduce_sum(expert_f[:], ended, AX.X))
                    ch.link(dve.tensor_scalar(expert_f[:], expert_f[:], float(EXPERTS - 1), None, ALU.min))
                    dve.tensor_copy(expert_i[:], expert_f[:]).then_inc(q["expert_ready"], 1)
                    dve.wait_ge(q["expert_ready"], 1)

                    def expert_in(cell):
                        return nc.values_load(cell[0:1, 0:1], engines=DVE_ENGINE, min_val=0, max_val=EXPERTS - 1)

                    def bias1(k, slot):
                        if later(k, 3):
                            dve.wait_ge(q["res_ready"], k - 2)
                        dve.wait_ge(q["e_up_ready"], k + 1)
                        dve.tensor_copy(e_down[slot][:], expert_i[:, ds(k, 1)]).then_inc(q["e_down_ready"], 1)
                        e = expert_in(e_up[slot])
                        dve.wait_ge(q["e_down_ready"], k + 1)
                        dve.wait_ge(q["h_made"], k + 1)
                        dve.tensor_tensor(hp[slot][:], bank[slot][:], b1s[:, ds(e * HID, HID)], ALU.add).then_inc(q["hp_ready"], 1)

                    def bias2(k, slot):
                        e = expert_in(e_down[slot])
                        dve.wait_ge(q["o_made"], k + 1)
                        dve.tensor_tensor(res[:, ds(k * D, D)], bank[7][:, 0:D], b2s[:, ds(e * D, D)],
                                          ALU.add).then_inc(q["res_ready"], 1)
                    skewed(dve, NS, 3, (0, bias1), (2, bias2))

                @block.scalar
                def _(act):
                    act.wait_ge(q["shifted"], 1)
                    act.activation(r["key"][:], r["score"][:], ACT.Exp).then_inc(q["exp_ready"], 1)

                    def turn_x(k, slot):
                        act.wait_ge(q["xt_made"], k + 1)
                        if later(k, 3):
                            act.wait_ge(q["h_made"], k - 2)
                        act.activation(xt[slot][:], bank[6][:, 0:P], ACT.Copy).then_inc(q["xt_ready"], 1)

                    def relu(k, slot):
                        act.wait_ge(q["ht_made"], k + 1)
                        if later(k, 3):
                            act.wait_ge(q["o_made"], k - 2)
                        act.activation(ht[slot][:], bank[3 + slot % 3][:], ACT.Relu).then_inc(q["ht_ready"], 1)
                    skewed(act, NS, 3, (0, turn_x), (2, relu))

                @block.tensor
                def _(pe):
                    pe.wait_ge(q["onehot_ready"], 1)
                    pe.matmul(bank[4][:, 0:TE], const["before"], r["onehot"][:], start=True, stop=True)
                    pe.matmul(bank[5][:, 0:TE], ones[:], r["onehot"][:], start=True, stop=True).then_inc(q["counts_made"], 1)
                    pe.wait_ge(q["expert_ready"], 1)

                    def expert_in(cell):
                        return nc.values_load(cell[0:1, 0:1], engines=PE_ENGINE, min_val=0, max_val=EXPERTS - 1)

                    def turn_x(k, slot):
                        pe.wait_ge(q["xin_ready"], k + 1)
                        if later(k, 1):
                            pe.wait_ge(q["xt_ready"], k)
                        pe.transpose(bank[6][:, 0:P], xin[slot][:], ident[:]).then_inc(q["xt_made"], 1)

                    def up(k, slot):
                        e = expert_in(e_up[slot])
                        pe.wait_ge(q["xt_ready"], k + 1)
                        if later(k, 3):
                            pe.wait_ge(q["hp_ready"], k - 2)
                        pe.matmul(bank[slot][:], xt[slot][:], w1[:, ds(e * HID, HID)], start=True, stop=True).then_inc(q["h_made"], 1)

                    def turn_h(k, slot):
                        pe.wait_ge(q["hp_ready"], k + 1)
                        if later(k, 3):
                            pe.wait_ge(q["ht_ready"], k - 2)
                        for c in range(HC):
                            last = pe.transpose(bank[3 + slot][:, c * P:(c + 1) * P], hp[slot][:, c * P:(c + 1) * P], ident[:])
                        last.then_inc(q["ht_made"], 1)

                    def down(k, slot):
                        e = expert_in(e_down[slot])
                        pe.wait_ge(q["ht_ready"], k + 1)
                        if later(k, 1):
                            pe.wait_ge(q["res_ready"], k)
                        for c in range(HC):
                            last = pe.matmul(bank[7][:, 0:D], ht[slot][:, c * P:(c + 1) * P],
                                             w2[:, ds(e * HC * D + c * D, D)], start=(c == 0), stop=(c == HC - 1))
                        last.then_inc(q["o_made"], 1)
                    skewed(pe, NS, 3, (0, turn_x), (1, up), (2, turn_h), (3, down))
        moe.close()

        full = {n: sb("full_" + n, c) for n, c in [("f1", HID), ("f2", HID), ("h1", HC * HID), ("h2", HC * HID), ("f3", HC * D)]}
        scl = {n: sb("scl_" + n, HC) for n in ["f1", "f2", "h1", "h2"]}
        scl3 = sb("scl3", D)
        W = S
        ob = sb("ob", W)
        raw_t, mv_o, ve_o, rs_o = sb("raw_t", 6 * HALVES), sb("mv_o", 2 * HALVES), sb("ve_o", HALVES), sb("rs_o", HALVES)
        tail = {n: sem("t_" + n) for n in ["proj_read", "tail_own", "var_o", "pow_o", "var_p", "pow_p", "tail_done"]}
        TAIL = 19

        def row(n, h):
            return xs[:, ds((n * HALVES + h) * D, D)]

        def halves_stats(dve, srcs, raw, mv, own, at):
            for h in range(HALVES):
                dve.bn_stats(raw[:, h * 6:(h + 1) * 6], srcs[h]).then_inc(q[own], 1)
            dve.wait_ge(q[own], at + HALVES)
            dve.sem_inc(q["dve_turn"], 1)
            for h in range(HALVES):
                dve.bn_aggr(mv[:, h * 2:(h + 1) * 2], raw[:, h * 6:(h + 1) * 6]).then_inc(q[own], 1)
            dve.wait_ge(q[own], at + 2 * HALVES)

        def var(mv):
            return mv[:].rearrange("p (h k) -> p h k", k=2)[:, :, 1]

        def scale(dve, buf, mv, rs, own, at):
            for h in range(HALVES):
                v = buf[:, h * D:(h + 1) * D]
                dve.tensor_scalar(v, v, mv[:, h * 2:h * 2 + 1], rs[:, h:h + 1], ALU.subtract, ALU.mult).then_inc(q[own], 1)
            dve.wait_ge(q[own], at + HALVES)

        def tail_first(dve, b):
            dve.wait_ge(q["proj_read"], b + 1)
            halves_stats(dve, [ob[:, 0:D], ob[:, D:W]], raw_t, mv_o, "tail_own", b * TAIL)
            dve.tensor_scalar(ve_o[:], var(mv_o), EPS, None, ALU.add).then_inc(q["var_o"], 1)

        def tail_second(dve, b):
            dve.wait_ge(q["pow_o"], b + 1)
            scale(dve, ob, mv_o, rs_o, "tail_own", b * TAIL + 4)
            v = ob[:].rearrange("p (h d) -> p h d", h=HALVES)
            dve.tensor_tensor(v, v, lnog[:].unsqueeze(1).to_broadcast((P, HALVES, D)), ALU.mult).then_inc(q["tail_own"], 1)
            dve.wait_ge(q["tail_own"], b * TAIL + 7)
            dve.tensor_tensor(v, v, lnob[:].unsqueeze(1).to_broadcast((P, HALVES, D)), ALU.add).then_inc(q["tail_own"], 1)
            dve.wait_ge(q["tail_own"], b * TAIL + 8)
            halves_stats(dve, [ob[:, 0:D], ob[:, D:W]], raw_t, mv_o, "tail_own", b * TAIL + 8)
            dve.tensor_scalar(ve_o[:], var(mv_o), EPS, None, ALU.add).then_inc(q["var_p"], 1)

        def tail_third(dve, b):
            dve.wait_ge(q["pow_p"], b + 1)
            scale(dve, ob, mv_o, rs_o, "tail_own", b * TAIL + 12)
            dve.tensor_tensor(xs[:, ds(b * W, W)], xs[:, ds(b * W, W)], ob[:], ALU.add).then_inc(q["tail_own"], 1)
            dve.wait_ge(q["tail_own"], b * TAIL + 15)
            halves_stats(dve, [row(b, 0), row(b, 1)], raw_t, mv_o, "tail_own", b * TAIL + 15)
            dve.tensor_copy(mv_all[:, ds(b * 4, 4)], mv_o[:]).then_inc(q["tail_done"], 1)

        with ExitStack() as ph:
            VW = 96
            UNITS = 18
            SQS = SCALE ** 0.5
            wqh, wql = sb("wqh", HEADS * DH, F32R, ph), sb("wql", HEADS * DH, F32R, ph)
            wkh, wkl = sb("wkh", P, F32R, ph), sb("wkl", P, F32R, ph)
            wvh, wvl = sb("wvh", DH, F32R, ph), sb("wvl", DH, F32R, ph)
            ident_r = sb("ident_r", P, F32R, ph)
            causal_r = sb("causal_r", QG * P, F32R, ph)
            zb = [sb(f"zb{i}", W, F32, ph) for i in range(2)]
            xh = [sb(f"xh{i}", W, F32R, ph) for i in range(2)]
            xl = [sb(f"xl{i}", W, F32R, ph) for i in range(2)]
            xf = sb("xf", W, F32, ph)
            qx = [sb(f"qx{i}", HEADS * W, F32R, ph) for i in range(2)]
            qm = [sb(f"qm{i}", HEADS * W, F32R, ph) for i in range(2)]
            kh = [sb(f"kh{i}", W, F32R, ph) for i in range(2)]
            kl = [sb(f"kl{i}", W, F32R, ph) for i in range(2)]
            vv = [sb(f"vv{i}", HALVES * VW, F32, ph) for i in range(2)]
            mx = sb("mx", HALVES * HEADS, F32, ph)
            mts = sb("mts", P, F32R, ph)
            pt0 = [sb(f"pt0{i}", QG * W, F32, ph) for i in range(2)]
            pt1 = [sb(f"pt1{i}", QG * P, F32, ph) for i in range(2)]
            rec = sb("rec", HALVES * QG, F32, ph)
            on = sb("on", HALVES * HEADS * DH, F32, ph)
            ot = sb("ot", NQ * 4 * P, F32, ph)
            yb = [sb(f"yb{i}", W, F32, ph) for i in range(2)]
            row_i = [sb(f"row_i{i}", HALVES, I32, ph) for i in range(2)]
            raw_f = sb("raw_f", 6 * HALVES, F32, ph)
            mv_y = sb("mv_y", 2 * HALVES, F32, ph)
            mv_x = [sb(f"mv_x{i}", 2 * HALVES, F32, ph) for i in range(2)]
            ve_y, ve_x, rs_y = sb("ve_y", HALVES, F32, ph), sb("ve_x", HALVES, F32, ph), sb("rs_y", HALVES, F32, ph)
            rs_x = [sb(f"rs_x{i}", HALVES, F32, ph) for i in range(2)]
            ring = [psum(f"ring{i}", 1, ph) for i in range(3)]
            ps_s = psum("ps_scores", 3, ph)
            ps_o = psum("ps_out", HALVES, ph)
            names = ["dve_done", "weights_split", "zb_ready", "z_made", "xh_ready", "xf_ready", "x_ready", "ring_made",
                     "ring_read", "kh_ready", "qh_ready", "ot_made", "ot_ready", "mts_ready", "max_loaded", "qm_loaded", "scores_made",
                     "exp_ready", "masked", "pv_made", "rec_ready", "normed", "proj_made", "pool_turn",
                     "row_ready", "gathered0", "gathered1", "feed_own", "var_y", "pow_y", "var_x", "pow_x",
                     "dve_turn"]
            q = {**{n: sem("c_" + n, ph) for n in names}, **tail}
            FEED = 11

            ffn_loads = ((full["f1"][:], f1t), (full["f2"][:], f2t), (full["h1"][:], h1t), (full["h2"][:], h2t), (full["f3"][:], f3t),
                         (scl["f1"][:], f1s), (scl["f2"][:], f2s), (scl["h1"][:], h1s), (scl["h2"][:], h2s),
                         (scl3[:], broadcast(f3s, D)))

            def within(b, k):
                return not isinstance(b, int) or b + k < B

            def sequences(attend):
                def run(eng):
                    for b in range(3):
                        attend(b, b % 2)
                    with eng.Fori(1, B // 2 - 2) as i:
                        attend(i * 2 + 1, 1)
                        attend(i * 2 + 2, 0)
                    for b in range(B - 3, B):
                        attend(b, b % 2)
                return run

            with nc.Block() as block:
                @block.sync
                def _(sp):
                    def load_max(n, slot):
                        sp.wait_ge(q["mts_ready"], n + 1)
                        for h in range(HALVES):
                            sp.dma_start(qm[slot][DH:DH + 1, :].rearrange("o (e h p) -> o e h p", h=HALVES, p=P)[:, :, h, :].bitcast(F32),
                                         mts[h * HEADS:(h + 1) * HEADS, :].bitcast(F32)).then_inc(q["max_loaded"], 16)
                    def copy_high(n, slot):
                        sp.wait_ge(q["qh_ready"], n * 8 + 8)
                        sp.dma_start(qm[slot][0:DH, :].bitcast(F32), qx[slot][0:DH, :].bitcast(F32)).then_inc(q["qm_loaded"], 16)

                    def attend(b, slot):
                        if within(b, 1):
                            copy_high(b + 1, 1 - slot)
                            load_max(b + 1, 1 - slot)
                    copy_high(0, 0)
                    load_max(0, 0)
                    for dst, src in ffn_loads:
                        sp.dma_start(dst, src).then_inc(ffn_loaded, 16)
                    sequences(attend)(sp)
                    sp.wait_ge(q["max_loaded"], 32 * B)
                    sp.wait_ge(q["qm_loaded"], 16 * B)

                @block.gpsimd
                def _(pool):
                    def gather(n, slot):
                        if later(n, 2):
                            pool.wait_ge(q["feed_own"], (n - 1) * FEED - 4)
                        pool.tensor_copy(row_i[slot][:], slot_i[:, ds(n * HALVES, HALVES)]).then_inc(q["row_ready"], 1)
                        pool.wait_ge(q["row_ready"], n + 1)
                        pool.sem_inc(q["pool_turn"], 1)
                        for h in range(HALVES):
                            pool.indirect_dma_start(out=yb[slot][:, h * D:(h + 1) * D], out_offset=None,
                                                    in_offset=bass.IndirectOffsetOnAxis(ap=row_i[slot][:, h:h + 1].bitcast(U32), axis=0),
                                                    in_=sorted_y).then_inc(q[f"gathered{slot}"], 16)

                    def power(out_, in_, ready, n, done):
                        pool.wait_ge(q[ready], n + 1)
                        pool.sem_inc(q["pool_turn"], 1)
                        pool.tensor_tensor(out_[:], in_[:], neg_half[:, 0:HALVES], ALU.pow).then_inc(q[done], 1)

                    def mask(b, g):
                        pool.wait_ge(q["exp_ready"], b * 8 + (2 * g + 1))
                        pool.sem_inc(q["pool_turn"], 1)
                        v = pt0[g % 2][:].rearrange("p (e i) -> p e i", e=QG)[:, :, 0:P]
                        pool.affine_select(out=v, in_=v, compare_op=ALU.is_ge, fill=0.0, base=0, pattern=[[0, QG], [1, P]],
                                           channel_multiplier=-1).then_inc(q["masked"], 1)
                        pool.wait_ge(q["exp_ready"], b * 8 + (2 * g + 2))
                        pool.sem_inc(q["pool_turn"], 1)
                        v = pt1[g % 2][:].rearrange("p (e i) -> p e i", e=QG)
                        pool.affine_select(out=v, in_=v, compare_op=ALU.is_ge, fill=0.0, base=0, pattern=[[0, QG], [1, P]],
                                           channel_multiplier=-1).then_inc(q["masked"], 1)

                    def attend(b, slot):
                        mask(b, 1)
                        if within(b, 2):
                            power(rs_x[slot], ve_x, "var_x", b + 2, "pow_x")
                        if later(b, 1):
                            power(rs_o, ve_o, "var_o", b - 1, "pow_o")
                        if within(b, 3):
                            gather(b + 3, 1 - slot)
                        mask(b, 2)
                        if later(b, 1):
                            power(rs_o, ve_o, "var_p", b - 1, "pow_p")
                        mask(b, 3)
                        if within(b, 1):
                            mask(b + 1, 0)
                        if within(b, 3):
                            power(rs_y, ve_y, "var_y", b + 3, "pow_y")
                    pool.wait_ge(sorted_stored, 48)
                    for n in range(2):
                        gather(n, n)
                    for n in range(2):
                        power(rs_y, ve_y, "var_y", n, "pow_y")
                        power(rs_x[n], ve_x, "var_x", n, "pow_x")
                    gather(2, 0)
                    mask(0, 0)
                    power(rs_y, ve_y, "var_y", 2, "pow_y")
                    sequences(attend)(pool)

                @block.vector
                def _(dve):
                    ch = Chain(dve, q["dve_done"])
                    w = small
                    dve.wait_ge(attn_loaded, 16 * 8)
                    for high, low, full in ((wqh, wql, wq), (wkh, wkl, wk2), (wvh, wvl, wv)):
                        ch.link(dve.tensor_copy(high[:], full[:]))
                        ch.link(dve.tensor_tensor(low[:], full[:], high[:].bitcast(F32), ALU.subtract))
                    ch.link(dve.tensor_copy(ident_r[:], ident[:]))
                    ch.link(dve.tensor_copy(causal_r[:].rearrange("p (e j) -> p e j", e=QG), const["causal"].unsqueeze(1).to_broadcast((P, QG, P))))
                    for i in range(2):
                        ch.link(dve.memset(kl[i][DH:DH + 1, :].bitcast(F32), -1.0))
                        ch.link(dve.memset(vv[i][:], 0.0))
                        ch.link(dve.memset(vv[i][:].rearrange("p (h c) -> p h c", c=VW)[:, :, DH], 1.0))
                    dve.sem_inc(q["weights_split"], 1)

                    def feed_first(n, slot):
                        dve.wait_ge(q[f"gathered{slot}"], (n - slot) * 16 + 32)
                        halves_stats(dve, [yb[slot][:, 0:D], yb[slot][:, D:W]], raw_f, mv_y, "feed_own", n * FEED)
                        dve.tensor_scalar(ve_y[:], var(mv_y), EPS, None, ALU.add).then_inc(q["var_y"], 1)

                    def feed_second(n, slot):
                        dve.wait_ge(q["pow_y"], n + 1)
                        scale(dve, yb[slot], mv_y, rs_y, "feed_own", n * FEED + 4)
                        dve.tensor_tensor(xs[:, ds(n * W, W)], xs[:, ds(n * W, W)], yb[slot][:], ALU.add).then_inc(q["feed_own"], 1)
                        dve.wait_ge(q["feed_own"], n * FEED + 7)
                        halves_stats(dve, [row(n, 0), row(n, 1)], raw_f, mv_x[slot], "feed_own", n * FEED + 7)
                        dve.tensor_scalar(ve_x[:], var(mv_x[slot]), 1.0 + EPS, EPS * EPS, ALU.mult, ALU.add).then_inc(q["var_x"], 1)

                    def normalise(n, slot):
                        dve.wait_ge(q["pow_x"], n + 1)
                        for h in range(HALVES):
                            dve.tensor_scalar(zb[slot][:, h * D:(h + 1) * D], row(n, h), mv_x[slot][:, h * 2:h * 2 + 1],
                                              rs_x[slot][:, h:h + 1], ALU.subtract, ALU.mult).then_inc(q["zb_ready"], 1)

                    def low_x(n, slot):
                        dve.wait_ge(q["xh_ready"], n + 1)
                        dve.tensor_scalar(xf[:], ring[0][:, 0:W], lng[:, 0:1], lnb[:, 0:1], ALU.mult, ALU.add).then_inc(q["xf_ready"], 1)
                        dve.wait_ge(q["xf_ready"], n + 1)
                        dve.tensor_tensor(xl[slot][:], xf[:], xh[slot][:].bitcast(F32), ALU.subtract).then_inc(q["x_ready"], 1)

                    def keys(n, slot):
                        dve.wait_ge(q["kh_ready"], n + 1)
                        dve.scalar_tensor_tensor(out=kl[slot][0:DH, :], in0=ring[0][0:DH, W:2 * W], scalar=SQS,
                                                 in1=kh[slot][0:DH, :].bitcast(F32), op0=ALU.mult, op1=ALU.subtract)
                        dve.tensor_copy(vv[slot][:].rearrange("p (h c) -> p h c", c=VW)[:, :, 0:DH],
                                        ring[0][:, 0:HALVES * DH].rearrange("p (h c) -> p h c", c=DH)).then_inc(q["ring_read"], 1)

                    def low_q(n, slot, u):
                        dve.wait_ge(q["qh_ready"], n * 8 + (2 * u + 2))
                        for par in range(2):
                            src = ring[(1 + u) % 3][par * DH:(par + 1) * DH, :].rearrange("p (k i) -> p k i", k=2)
                            v = qx[slot][:].rearrange("p (k e i) -> p k e i", e=2, i=W)[:, 2 * u:2 * u + 2, par, :]
                            last = dve.scalar_tensor_tensor(out=v[DH:P], in0=src, scalar=SCALE * SQS, in1=v[0:DH].bitcast(F32),
                                                            op0=ALU.mult, op1=ALU.subtract)
                        last.then_inc(q["ring_read"], 1)

                    def maxima(n, m):
                        dve.wait_ge(q["ring_made"], n * UNITS + (6 + m))
                        heads = QG if m < NQ else 2
                        at = m * QG if m < NQ else HEADS + (m - NQ) * 2
                        dve.reduce_max(mx[:, at:at + heads], ring[(5 + m) % 3][:].rearrange("p (e j) -> p e j", e=heads),
                                       AX.X).then_inc(q["ring_read"], 1)

                    def take_max(n):
                        dve.wait_ge(q["ring_made"], n * UNITS + UNITS)
                        if later(n, 1):
                            dve.wait_ge(q["max_loaded"], n * 32)
                        dve.tensor_copy(mts[0:HALVES * HEADS, :], ring[(UNITS - 1) % 3][0:HALVES * HEADS, 0:P]).then_inc(q["mts_ready"], 1)

                    def norm(b, g):
                        dve.wait_ge(q["pv_made"], b * NQ + (g + 1))
                        o = ps_o[:].rearrange("p (h k) -> p h k", h=HALVES)[:, :, 0:QG * VW].rearrange("p h (e c) -> p h e c", c=VW)
                        r3 = rec[:].rearrange("p (h e) -> p h e", h=HALVES)
                        dve.reciprocal(r3, o[:, :, :, DH]).then_inc(q["rec_ready"], 1)
                        dve.wait_ge(q["rec_ready"], b * NQ + (g + 1))
                        dve.tensor_tensor(on[:].rearrange("p (h e c) -> p h e c", h=HALVES, c=DH)[:, :, g * QG:(g + 1) * QG, :],
                                          o[:, :, :, 0:DH], r3.unsqueeze(3).to_broadcast((P, HALVES, QG, DH)),
                                          ALU.mult).then_inc(q["normed"], 1)

                    def attend(b, slot):
                        n, other, prep, further = b + 1, 1 - slot, within(b, 1), within(b, 2)
                        if further:
                            feed_second(b + 2, slot)
                        if prep:
                            low_q(n, other, 2)
                            low_q(n, other, 3)
                        norm(b, 0)
                        if prep:
                            maxima(n, 0)
                            maxima(n, 1)
                        if later(b, 1):
                            tail_first(dve, b - 1)
                        if prep:
                            maxima(n, 2)
                            maxima(n, 3)
                        if later(b, 1):
                            tail_second(dve, b - 1)
                        norm(b, 1)
                        if prep:
                            for m in range(4, 9):
                                maxima(n, m)
                        if further:
                            normalise(b + 2, slot)
                        if prep:
                            maxima(n, 9)
                            maxima(n, 10)
                        norm(b, 2)
                        if prep:
                            maxima(n, 11)
                            take_max(n)
                        if further:
                            low_x(b + 2, slot)
                        if within(b, 3):
                            feed_first(b + 3, other)
                        norm(b, 3)
                        if later(b, 1):
                            tail_third(dve, b - 1)
                        if further:
                            keys(b + 2, slot)
                            low_q(b + 2, slot, 0)
                            low_q(b + 2, slot, 1)
                    feed_first(0, 0)
                    feed_second(0, 0)
                    normalise(0, 0)
                    feed_first(1, 1)
                    low_x(0, 0)
                    keys(0, 0)
                    low_q(0, 0, 0)
                    low_q(0, 0, 1)
                    feed_second(1, 1)
                    low_q(0, 0, 2)
                    low_q(0, 0, 3)
                    normalise(1, 1)
                    for m in range(12):
                        maxima(0, m)
                    take_max(0)
                    low_x(1, 1)
                    keys(1, 1)
                    low_q(1, 1, 0)
                    low_q(1, 1, 1)
                    feed_first(2, 0)
                    sequences(attend)(dve)

                @block.scalar
                def _(act):
                    def high_x(n, slot):
                        act.wait_ge(q["z_made"], n + 1)
                        act.activation(xh[slot][:], ring[0][:, 0:W], ACT.Identity, scale=lng[:, 0:1], bias=lnb[:, 0:1]).then_inc(q["xh_ready"], 1)

                    def high_k(n, slot):
                        act.wait_ge(q["ring_made"], n * UNITS + 1)
                        act.activation(kh[slot][:], ring[0][:, W:2 * W], ACT.Copy, scale=SQS).then_inc(q["kh_ready"], 1)

                    def high_q(n, slot, u):
                        act.wait_ge(q["ring_made"], n * UNITS + (2 + u))
                        for par in range(2):
                            src = ring[(1 + u) % 3][par * DH:(par + 1) * DH, :].rearrange("p (k i) -> p k i", k=2)
                            v = qx[slot][0:DH, :].rearrange("p (k e i) -> p k e i", e=2, i=W)[:, 2 * u:2 * u + 2, par, :]
                            act.activation(v, src, ACT.Copy, scale=SCALE * SQS).then_inc(q["qh_ready"], 1)

                    def exponent(b, g):
                        act.wait_ge(q["scores_made"], b * 8 + (2 * g + 1))
                        if later(b, 1) or g >= 2:
                            act.wait_ge(q["pv_made"], b * NQ + (g - 1))
                        act.activation(pt0[g % 2][:], ps_s[:, 0:2 * 512], ACT.Exp).then_inc(q["exp_ready"], 1)
                        act.wait_ge(q["scores_made"], b * 8 + (2 * g + 2))
                        act.activation(pt1[g % 2][:], ps_s[:, 2 * 512:3 * 512], ACT.Exp).then_inc(q["exp_ready"], 1)

                    def take_heads(b, g):
                        act.wait_ge(q["ot_made"], b * NQ + (g + 1))
                        act.activation(ot[:, g * 512:(g + 1) * 512], ps_o[:, 0:512], ACT.Copy).then_inc(q["ot_ready"], 1)

                    def take_projection(b):
                        act.wait_ge(q["proj_made"], b + 1)
                        if later(b, 1):
                            act.wait_ge(q["tail_own"], b * TAIL - 4)
                        act.activation(ob[:], ps_o[:, 512:512 + W], ACT.Copy).then_inc(q["proj_read"], 1)

                    def attend(b, slot):
                        n, other = b + 1, 1 - slot
                        exponent(b, 1)
                        if within(b, 1):
                            high_q(n, other, 2)
                        if later(b, 1):
                            take_projection(b - 1)
                        if within(b, 1):
                            high_q(n, other, 3)
                        take_heads(b, 0)
                        exponent(b, 2)
                        take_heads(b, 1)
                        exponent(b, 3)
                        take_heads(b, 2)
                        if within(b, 2):
                            high_x(b + 2, slot)
                        if within(b, 1):
                            exponent(n, 0)
                        if within(b, 2):
                            high_k(b + 2, slot)
                            high_q(b + 2, slot, 0)
                        take_heads(b, 3)
                        if within(b, 2):
                            high_q(b + 2, slot, 1)
                    act.wait_ge(attn_loaded, 16 * 8)
                    high_x(0, 0)
                    high_k(0, 0)
                    for u in range(4):
                        high_q(0, 0, u)
                    high_x(1, 1)
                    exponent(0, 0)
                    high_k(1, 1)
                    high_q(1, 1, 0)
                    high_q(1, 1, 1)
                    sequences(attend)(act)
                    take_projection(B - 1)

                @block.tensor
                def _(pe):
                    def three(out_ap, lhs, rhs, start=True):
                        (lh, ll), (rh, rl) = lhs, rhs
                        pe.matmul(out_ap, lh, rl, start=start, stop=False, skip_group_check=True)
                        pe.matmul(out_ap, ll, rh, start=False, stop=False, skip_group_check=True)
                        return pe.matmul(out_ap, lh, rh, start=False, stop=True, skip_group_check=True)

                    def turn_z(n, slot):
                        pe.wait_ge(q["zb_ready"], n * HALVES + HALVES)
                        wait_unit(n, 0)
                        for h in range(HALVES):
                            last = pe.transpose(ring[0][:, h * P:(h + 1) * P], zb[slot][:, h * D:(h + 1) * D], ident[:])
                        last.then_inc(q["z_made"], 1)

                    def keys(n, slot):
                        pe.wait_ge(q["x_ready"], n + 1)
                        three(ring[0][:, W:2 * W], (wkh[:], wkl[:]), (xh[slot][:], xl[slot][:]))
                        for h in range(HALVES):
                            c = slice(h * P, (h + 1) * P)
                            last = three(ring[0][:, h * DH:(h + 1) * DH], (xh[slot][:, c], xl[slot][:, c]), (wvh[:], wvl[:]))
                        last.then_inc(q["ring_made"], 1)

                    def queries(n, slot, u):
                        k = 1 + u
                        wait_unit(n, k)
                        for j in range(2):
                            c = slice((2 * u + j) * P, (2 * u + j + 1) * P)
                            last = three(ring[k % 3][:, j * W:(j + 1) * W], (wqh[:, c], wql[:, c]), (xh[slot][:], xl[slot][:]))
                        last.then_inc(q["ring_made"], 1)

                    def wait_unit(n, k):
                        if k >= 3:
                            pe.wait_ge(q["ring_read"], n * 17 + (k - 2))
                        elif later(n, 1):
                            if k == 2:
                                pe.wait_ge(q["mts_ready"], n)
                            else:
                                pe.wait_ge(q["ring_read"], n * 17 + (k - 1))

                    def maxima(n, slot, m):
                        k = 5 + m
                        wait_unit(n, k)
                        if m == 0:
                            pe.wait_ge(q["ring_read"], n * 17 + 5)
                        bank = ring[k % 3]
                        if m < NQ:
                            for j in range(QG):
                                h = m * QG + j
                                pe.matmul(bank[:, j * P:(j + 1) * P], qx[slot][:, h * W:h * W + P], kh[slot][:, 0:P],
                                          start=(j == 0), stop=False, skip_group_check=True)
                            last = pe.matmul(bank[:], ident_r[:], causal_r[:], start=False, stop=True, skip_group_check=True)
                        else:
                            for j in range(2):
                                h = (m - NQ) * 2 + j
                                pe.matmul(bank[:, j * W:(j + 1) * W], qx[slot][:, h * W + P:(h + 1) * W], kh[slot][:],
                                          start=(j == 0), stop=False, skip_group_check=True)
                            last = pe.matmul(bank[:].rearrange("p (e j) -> p e j", e=2)[:, :, P:W], ident_r[:],
                                             causal_r[:, 0:2 * P].rearrange("p (e j) -> p e j", e=2), start=False, stop=True,
                                             skip_group_check=True)
                        last.then_inc(q["ring_made"], 1)

                    def turn_max(n):
                        pe.wait_ge(q["ring_read"], n * 17 + 17)
                        pe.transpose(ring[(UNITS - 1) % 3][0:HALVES * HEADS, 0:P], mx[:], ident[:]).then_inc(q["ring_made"], 1)

                    def scores(b, slot, g):
                        if g == 0:
                            pe.wait_ge(q["max_loaded"], b * 32 + 32)
                            pe.wait_ge(q["qm_loaded"], b * 16 + 16)
                            if later(b, 1):
                                pe.wait_ge(q["exp_ready"], b * 8)
                        else:
                            pe.wait_ge(q["exp_ready"], b * 8 + 2 * g)
                        for half in range(2):
                            c = slice((QG * g + 2 * half) * W, (QG * g + 2 * half + 2) * W)
                            o = ps_s[:, half * 512:(half + 1) * 512]
                            pe.matmul(o, kh[slot][:, 0:P], qx[slot][:, c], start=True, stop=False)
                            last = pe.matmul(o, kl[slot][0:DH + 1, 0:P], qm[slot][0:DH + 1, c], start=False, stop=True)
                        last.then_inc(q["scores_made"], 1)
                        o = ps_s[:, 2 * 512:3 * 512]

                        def second(t):
                            return t[:, QG * g * W:QG * (g + 1) * W].rearrange("p (e i) -> p e i", i=W)[:, :, P:W]
                        pe.matmul(o, kh[slot][:, P:W], second(qx[slot]), start=True, stop=False)
                        pe.matmul(o, kl[slot][0:DH + 1, P:W], second(qm[slot])[0:DH + 1], start=False, stop=True).then_inc(q["scores_made"], 1)

                    def values(b, slot, g):
                        pe.wait_ge(q["masked"], b * 8 + (2 * g + 2))
                        if g >= 1:
                            pe.wait_ge(q["ot_ready"], b * NQ + g)
                        elif later(b, 1):
                            pe.wait_ge(q["proj_read"], b)
                        for e in range(QG):
                            first, second = ps_o[:, e * VW:(e + 1) * VW], ps_o[:, 512 + e * VW:512 + (e + 1) * VW]
                            keys0, keys1 = vv[slot][:, 0:VW], vv[slot][:, VW:2 * VW]
                            pe.matmul(first, pt0[g % 2][:, e * W:e * W + P], keys0, start=True, stop=True, skip_group_check=True)
                            pe.matmul(second, pt0[g % 2][:, e * W + P:(e + 1) * W], keys0, start=True, stop=False, skip_group_check=True)
                            last = pe.matmul(second, pt1[g % 2][:, e * P:(e + 1) * P], keys1, start=False, stop=True,
                                             skip_group_check=True)
                        last.then_inc(q["pv_made"], 1)

                    def turn_heads(b, g):
                        pe.wait_ge(q["normed"], b * NQ + (g + 1))
                        for h in range(HALVES):
                            for k in range(2):
                                c = h * HEADS * DH + (2 * g + k) * P
                                last = pe.transpose(ps_o[:, (2 * h + k) * P:(2 * h + k + 1) * P], on[:, c:c + P], ident[:])
                        last.then_inc(q["ot_made"], 1)

                    def project(b):
                        pe.wait_ge(q["ot_ready"], b * NQ + NQ)
                        for h in range(HALVES):
                            for k in range(PAIRS):
                                c = (k // 2) * 512 + (2 * h + k % 2) * P
                                last = pe.matmul(ps_o[:, 512 + h * D:512 + (h + 1) * D], ot[:, c:c + P],
                                                 wo[:, k * D:(k + 1) * D], start=(k == 0), stop=(k == PAIRS - 1), skip_group_check=True)
                        last.then_inc(q["proj_made"], 1)

                    def attend(b, slot):
                        n, other, prep, further = b + 1, 1 - slot, within(b, 1), within(b, 2)
                        scores(b, slot, 1)
                        if prep:
                            queries(n, other, 2)
                        if later(b, 1):
                            project(b - 1)
                        if prep:
                            queries(n, other, 3)
                        values(b, slot, 0)
                        if prep:
                            maxima(n, other, 0)
                            maxima(n, other, 1)
                        turn_heads(b, 0)
                        if prep:
                            maxima(n, other, 2)
                            maxima(n, other, 3)
                        scores(b, slot, 2)
                        values(b, slot, 1)
                        if prep:
                            for m in range(4, 7):
                                maxima(n, other, m)
                        turn_heads(b, 1)
                        if prep:
                            for m in range(7, 9):
                                maxima(n, other, m)
                        scores(b, slot, 3)
                        if prep:
                            maxima(n, other, 9)
                            maxima(n, other, 10)
                        values(b, slot, 2)
                        if prep:
                            maxima(n, other, 11)
                        if further:
                            turn_z(b + 2, slot)
                        turn_heads(b, 2)
                        if prep:
                            turn_max(n)
                        values(b, slot, 3)
                        if prep:
                            scores(n, other, 0)
                        if further:
                            keys(b + 2, slot)
                            queries(b + 2, slot, 0)
                        turn_heads(b, 3)
                        if further:
                            queries(b + 2, slot, 1)
                    pe.wait_ge(q["weights_split"], 1)
                    turn_z(0, 0)
                    keys(0, 0)
                    for u in range(4):
                        queries(0, 0, u)
                    for m in range(12):
                        maxima(0, 0, m)
                    turn_max(0)
                    turn_z(1, 1)
                    scores(0, 0, 0)
                    keys(1, 1)
                    queries(1, 1, 0)
                    queries(1, 1, 1)
                    sequences(attend)(pe)
                    project(B - 1)

        with ExitStack() as ph:
            high = {n: sb("high_" + n, c, F32R, ph) for n, c in
                    [("f1", HID), ("f2", HID), ("h1", HC * HID), ("h2", HC * HID)]}
            low = {n: sb("low_" + n, c, F32R, ph) for n, c in
                   [("f1", HID), ("f2", HID), ("h1", HC * HID), ("h2", HC * HID)]}
            zb = [sb(f"fz{i}", GW, F32, ph) for i in range(2)]
            zh = [sb(f"fzh{i}", GW, F32R, ph) for i in range(2)]
            zl = [sb(f"fzl{i}", GW, F32R, ph) for i in range(2)]
            gate = [sb(f"gate{i}", GW, F32, ph) for i in range(HC)]
            hid = [sb(f"hid{i}", GW, F32, ph) for i in range(HC)]
            top = [sb(f"top{i}", GW, F32, ph) for i in range(HC)]
            hh = [[sb(f"hh{i}{c}", GW, F32R, ph) for c in range(HC)] for i in range(2)]
            hl = [[sb(f"hl{i}{c}", GW, F32R, ph) for c in range(HC)] for i in range(2)]
            oa = sb("ffn_out", GW, F32, ph)
            raw_out, mv_out = sb("raw_out", 6 * GT, F32, ph), sb("mv_out", 2 * GT, F32, ph)
            ve_out, rs_out = sb("ve_out", GT, F32, ph), sb("rs_out", GT, F32, ph)
            bank_a = [psum(f"bank_a{i}", 1, ph) for i in range(HC)]
            bank_b = [psum(f"bank_b{i}", 1, ph) for i in range(HC)]
            names = ["dve_turn", "small_high", "big_high", "weights_split", "var_ready", "rstd_ready", "zb_ready", "z_made", "zh_ready", "z_ready",
                     "gate_made", "line_made", "one_made", "two_made", "out_made", "gate_ready", "one_ready", "top_ready",
                     "hid_ready", "high_ready", "split_ready", "out_own", "out_read", "var_out", "rs_ready", "x_ready"]
            q = {**{n: sem("d_" + n, ph) for n in names}, **tail}
            OUT = 12
            with nc.Block() as block:
                @block.sync
                def _(sp):
                    def put(g):
                        sp.wait_ge(q["x_ready"], g + 1)
                        sp.dma_start(out.rearrange("b (h p) d -> p (b h) d", p=P)[:, ds(g * GT, GT), :],
                                     xs[:, ds(g * GW, GW)].rearrange("p (t d) -> p t d", d=D)).then_inc(all_stored, 16)
                    with sp.Fori(0, NG) as g:
                        put(g)
                    sp.wait_ge(all_stored, 16 * NG)

                @block.gpsimd
                def _(pool):
                    pool.wait_ge(q["var_ready"], 1)
                    def root(a, b):
                        pool.tensor_tensor(small["rstd"][:, a:b], small["ve"][:, a:b], neg_half[:, a:b], ALU.pow).then_inc(q["rstd_ready"], 1)
                    root(0, GT)
                    root(GT, NT - GT)
                    for ready, done in (("var_o", "pow_o"), ("var_p", "pow_p")):
                        pool.wait_ge(q[ready], B)
                        pool.tensor_tensor(rs_o[:], ve_o[:], neg_half[:, 0:HALVES], ALU.pow).then_inc(q[done], 1)
                    pool.wait_ge(q["var_ready"], 2)
                    root(NT - GT, NT)
                    with pool.Fori(0, NG) as g:
                        pool.wait_ge(q["var_out"], g + 1)
                        pool.tensor_tensor(rs_out[:], ve_out[:], neg_half[:, 0:GT], ALU.pow).then_inc(q["rs_ready"], 1)

                @block.vector
                def _(dve):
                    w = small
                    mva = mv_all[:].rearrange("p (t k) -> p t k", k=2)
                    dve.tensor_scalar(w["ve"][:, 0:NT - GT], mva[:, 0:NT - GT, 1], EPS, None, ALU.add).then_inc(q["var_ready"], 1)

                    def split_small():
                        dve.wait_ge(ffn_loaded, 16 * 10)
                        for i, n in enumerate(("f1", "f2")):
                            dve.tensor_copy(high[n][:], full[n][:]).then_inc(q["small_high"], 1)
                            dve.wait_ge(q["small_high"], i + 1)
                            dve.tensor_tensor(low[n][:], full[n][:], high[n][:].bitcast(F32), ALU.subtract).then_inc(q["weights_split"], 1)

                    def low_hidden(i, n):
                        dve.wait_ge(q["big_high"], i + 1)
                        dve.tensor_tensor(low[n][:], full[n][:], high[n][:].bitcast(F32), ALU.subtract).then_inc(q["weights_split"], 1)

                    def normalise(g, slot):
                        if not later(g, 2):
                            dve.wait_ge(q["rstd_ready"], g + 1)
                        elif isinstance(g, int) and g == NG - 1:
                            dve.wait_ge(q["rstd_ready"], 3)
                        if later(g, 2):
                            dve.wait_ge(q["z_made"], g - 1)
                        for j in range(GT):
                            dve.tensor_scalar(zb[slot][:, j * D:(j + 1) * D], xs[:, ds((g * GT + j) * D, D)], mv_all[:, ds((g * GT + j) * 2, 1)],
                                              w["rstd"][:, ds(g * GT + j, 1)], ALU.subtract, ALU.mult).then_inc(q["zb_ready"], 1)

                    def low_z(g, slot):
                        dve.wait_ge(q["zh_ready"], g + 1)
                        dve.tensor_tensor(zl[slot][:], bank_b[1][:], zh[slot][:].bitcast(F32), ALU.subtract).then_inc(q["z_ready"], 1)

                    def split(g, layer, c):
                        dve.tensor_copy(hh[layer][c][:], hid[c][:]).then_inc(q["high_ready"], 1)
                        dve.wait_ge(q["high_ready"], g * 2 * HC + (layer * HC + c + 1))
                        dve.tensor_tensor(hl[layer][c][:], hid[c][:], hh[layer][c][:].bitcast(F32), ALU.subtract).then_inc(q["split_ready"], 1)

                    def gated(g):
                        for c in range(HC):
                            dve.wait_ge(q["gate_ready"], g * HC + (c + 1))
                            dve.wait_ge(q["line_made"], g * HC + (c + 1))
                            dve.scalar_tensor_tensor(out=hid[c][:], in0=bank_b[c][:], scalar=scl["f2"][:, c:c + 1], in1=gate[c][:],
                                                     op0=ALU.mult, op1=ALU.mult).then_inc(q["hid_ready"], 1)
                            dve.wait_ge(q["hid_ready"], g * HC + (c + 1))
                            split(g, 0, c)

                    def hidden(g):
                        for c in range(HC):
                            dve.wait_ge(q["one_ready"], g * HC + (c + 1))
                            split(g, 1, c)

                    def take_out(g):
                        dve.wait_ge(q["out_made"], g + 1)
                        if later(g, 1):
                            dve.wait_ge(q["x_ready"], g)
                        dve.tensor_tensor(oa[:].rearrange("p (t d) -> p t d", d=D), bank_b[0][:].rearrange("p (t d) -> p t d", d=D),
                                          scl3[:].unsqueeze(1).to_broadcast((P, GT, D)), ALU.mult).then_inc(q["out_read"], 1)
                        dve.wait_ge(q["out_read"], g + 1)
                        for j in range(GT):
                            dve.bn_stats(raw_out[:, j * 6:(j + 1) * 6], oa[:, j * D:(j + 1) * D]).then_inc(q["out_own"], 1)
                        dve.wait_ge(q["out_own"], g * OUT + 4)
                        dve.sem_inc(q["dve_turn"], 1)
                        for j in range(GT):
                            dve.bn_aggr(mv_out[:, j * 2:(j + 1) * 2], raw_out[:, j * 6:(j + 1) * 6]).then_inc(q["out_own"], 1)
                        dve.wait_ge(q["out_own"], g * OUT + 8)
                        dve.tensor_scalar(ve_out[:], mv_out[:].rearrange("p (t k) -> p t k", k=2)[:, :, 1], EPS, None, ALU.add).then_inc(q["var_out"], 1)

                    def finish(g):
                        dve.wait_ge(q["rs_ready"], g + 1)
                        for j in range(GT):
                            v = oa[:, j * D:(j + 1) * D]
                            dve.tensor_scalar(v, v, mv_out[:, j * 2:j * 2 + 1], rs_out[:, j:j + 1], ALU.subtract, ALU.mult).then_inc(q["out_own"], 1)
                        dve.wait_ge(q["out_own"], g * OUT + 12)
                        dve.tensor_tensor(xs[:, ds(g * GW, GW)], xs[:, ds(g * GW, GW)], oa[:], ALU.add).then_inc(q["x_ready"], 1)

                    def step(g, slot, more=True):
                        first = isinstance(g, int) and g == 0
                        if more:
                            normalise(g + 1, 1 - slot)
                        gated(g)
                        if first:
                            low_hidden(1, "h2")
                        else:
                            take_out(g - 1)
                        if more:
                            low_z(g + 1, 1 - slot)
                        if first:
                            tail_second(dve, B - 1)
                        hidden(g)
                        if first:
                            tail_third(dve, B - 1)
                            dve.wait_ge(q["tail_done"], B)
                            dve.tensor_scalar(w["ve"][:, NT - GT:NT], mva[:, NT - GT:NT, 1], EPS, None, ALU.add).then_inc(q["var_ready"], 1)
                        if not first:
                            finish(g - 1)
                    normalise(0, 0)
                    split_small()
                    tail_first(dve, B - 1)
                    low_z(0, 0)
                    low_hidden(0, "h1")
                    groups(dve, step)
                    take_out(NG - 1)
                    finish(NG - 1)

                @block.scalar
                def _(act):
                    def high_z(g, slot):
                        act.wait_ge(q["z_made"], g + 1)
                        act.activation(zh[slot][:], bank_b[1][:], ACT.Copy).then_inc(q["zh_ready"], 1)

                    def step(g, slot, more=True):
                        for c in range(HC):
                            act.wait_ge(q["gate_made"], g * HC + (c + 1))
                            act.activation(gate[c][:], bank_a[c][:], ACT.Silu, scale=scl["f1"][:, c:c + 1]).then_inc(q["gate_ready"], 1)
                        if more:
                            high_z(g + 1, 1 - slot)
                        for c in range(HC):
                            act.wait_ge(q["one_made"], g * HC + (c + 1))
                            act.activation(hid[c][:], bank_a[c][:], ACT.Gelu, scale=scl["h1"][:, c:c + 1]).then_inc(q["one_ready"], 1)
                        for c in range(HC):
                            act.wait_ge(q["two_made"], g * HC + (c + 1))
                            act.activation(top[c][:], bank_b[c][:], ACT.Gelu, scale=scl["h2"][:, c:c + 1]).then_inc(q["top_ready"], 1)
                    act.wait_ge(ffn_loaded, 16 * 10)
                    act.activation(high["h1"][:], full["h1"][:], ACT.Copy).then_inc(q["big_high"], 1)
                    high_z(0, 0)
                    act.activation(high["h2"][:], full["h2"][:], ACT.Copy).then_inc(q["big_high"], 1)
                    groups(act, step)

                @block.tensor
                def _(pe):
                    def three(out_ap, lhs, rhs, start=True, stop=True):
                        (lh, ll), (rh, rl) = lhs, rhs
                        pe.matmul(out_ap, lh, rl, start=start, stop=False, skip_group_check=True)
                        pe.matmul(out_ap, ll, rh, start=False, stop=False, skip_group_check=True)
                        return pe.matmul(out_ap, lh, rh, start=False, stop=stop, skip_group_check=True)

                    def turn(g, slot):
                        pe.wait_ge(q["zb_ready"], g * GT + GT)
                        if later(g, 1):
                            pe.wait_ge(q["hid_ready"], g * HC - 2)
                        for j in range(GT):
                            last = pe.transpose(bank_b[1][:, j * P:(j + 1) * P], zb[slot][:, j * D:(j + 1) * D], ident[:])
                        last.then_inc(q["z_made"], 1)

                    def gated(g, slot):
                        pe.wait_ge(q["z_ready"], g + 1)
                        for n, banks, made in (("f1", bank_a, "gate_made"), ("f2", bank_b, "line_made")):
                            for c in range(HC):
                                if n == "f2" and later(g, 1):
                                    pe.wait_ge(q["top_ready"], g * HC + (c + 1 - HC))
                                m = slice(c * P, (c + 1) * P)
                                three(banks[c][:], (high[n][:, m], low[n][:, m]), (zh[slot][:], zl[slot][:])).then_inc(q[made], 1)

                    def hidden(g, layer, more):
                        n, banks, made = (("h1", bank_a, "one_made"), ("h2", bank_b, "two_made"))[layer]
                        if layer == 0:
                            pe.wait_ge(q["gate_ready"], g * HC + HC)
                        else:
                            if later(g, 1):
                                pe.wait_ge(q["out_read"], g)
                            if more:
                                pe.wait_ge(q["z_ready"], g + 2)
                        for k in range(HC):
                            pe.wait_ge(q["split_ready"], g * 2 * HC + (layer * HC + k + 1))
                            for c in range(HC):
                                m = slice(k * HID + c * P, k * HID + (c + 1) * P)
                                last = three(banks[c][:], (high[n][:, m], low[n][:, m]), (hh[layer][k][:], hl[layer][k][:]),
                                             start=(k == 0), stop=(k == HC - 1))
                                if k == HC - 1:
                                    last.then_inc(q[made], 1)

                    def outward(g, ready):
                        if ready is not None:
                            pe.wait_ge(q["hid_ready"], ready)
                        pe.wait_ge(q["top_ready"], g * HC + HC)
                        for t in range(GT):
                            for k in range(HC):
                                m = slice(t * P, (t + 1) * P)
                                last = pe.matmul(bank_b[0][:, m], top[k][:, m], full["f3"][:, k * D:(k + 1) * D],
                                                 start=(k == 0), stop=(k == HC - 1), skip_group_check=True)
                        last.then_inc(q["out_made"], 1)

                    def step(g, slot, more=True):
                        first = isinstance(g, int) and g == 0
                        gated(g, slot)
                        if not first:
                            outward(g - 1, g * HC + 1)
                        if more:
                            turn(g + 1, 1 - slot)
                        if first:
                            pe.wait_ge(q["weights_split"], 3)
                        hidden(g, 0, more)
                        if first:
                            pe.wait_ge(q["weights_split"], 4)
                        hidden(g, 1, more)
                    turn(0, 0)
                    pe.wait_ge(q["weights_split"], 2)
                    groups(pe, step)
                    outward(NG - 1, None)


def constants():
    import numpy as np
    r = np.arange(P)
    c = {}
    c["diff"] = (r[:, None] == r[None, :] + 1) * 1.0 - (r[:, None] == r[None, :]) * 1.0
    c["cross"] = ((r[:, None] == 0) & (r[None, :] == P - 1)) * 1.0
    window = min(8, S - 1)
    band = np.zeros((S, S), np.float32)
    for s in range(1, S):
        w = min(s, window)
        for j in range(w):
            band[s - w + j, s] = np.float32(0.1) + np.float32(0.9) * np.float32(j) / np.float32(max(w - 1, 1)) if w > 1 else 0.1
    c["band00"], c["band10"], c["band11"] = band[:P, :P], band[:P, P:], band[P:, P:]
    c["causal"] = np.where(r[None, :] > r[:, None], MASKED, 0.0)
    c["before"] = (r[:, None] < r[None, :]) * 1.0
    e = np.arange(EXPERTS)
    index = np.zeros((P, P))
    index[:, :2 * EXPERTS] = np.concatenate([e + 1, EXPERTS - e])
    c["index_e"] = index
    c["tile_no"] = np.broadcast_to(r[None, :], (P, P))
    return np.concatenate([c[n] for n in CONSTS], axis=1).astype(np.float32)


def kernel(**inputs):
    import numpy as np
    import concourse.bacc as bacc
    from concourse.bass_utils import run_bass_kernel_spmd as run

    a = {n: np.asarray(v) for n, v in inputs.items()}
    wkt, wvt = a["L1_attn_w_kv"][:DH].T, a["L1_attn_w_kv"][DH:].T

    def chunked(w):
        return w.T.reshape(-1, P, w.shape[0]).transpose(1, 0, 2).reshape(P, -1)

    def columns(v):
        return v.reshape(-1, P).T

    laid = [
        a["L0_attn_embeddings"], a["L0_attn_guidance_trajectories"],
        a["L0_ffn_gate_w"].T, a["L0_ffn_gate_b"],
        a["L0_ffn_w1"].transpose(2, 0, 1).reshape(D, -1), a["L0_ffn_b1"].reshape(-1),
        a["L0_ffn_w2"].reshape(EXPERTS, D, HC, P).transpose(3, 0, 2, 1).reshape(P, -1), a["L0_ffn_b2"].reshape(-1),
        a["L1_attn_w_q"].T, np.concatenate([wkt, wkt], axis=1), wvt, chunked(a["L1_attn_w_out"]),
        a["L1_attn_ln_g"].reshape(P, 1), a["L1_attn_ln_b"].reshape(P, 1), a["L1_attn_lno_g"], a["L1_attn_lno_b"],
        a["L1_ffn_w1_w"].T, columns(a["L1_ffn_w1_s"]), a["L1_ffn_w2_w"].T, columns(a["L1_ffn_w2_s"]),
        chunked(a["L1_ffn_h1_w"]), columns(a["L1_ffn_h1_s"]), chunked(a["L1_ffn_h2_w"]), columns(a["L1_ffn_h2_s"]),
        chunked(a["L1_ffn_w3_w"]), a["L1_ffn_w3_s"],
        constants(),
    ]
    nc = bacc.Bacc("TRN2", target_bir_lowering=False, num_devices=1)
    arrays, args = {}, []
    for i, v in enumerate(laid):
        v = np.ascontiguousarray(v)
        arrays[f"in_{i}"] = v
        args.append(nc.dram_tensor(f"in_{i}", v.shape, mybir.dt.from_np(v.dtype), kind="ExternalInput").ap())
    args.append(nc.dram_tensor("out_0", (B, S, D), F32, kind="ExternalOutput").ap())
    program(nc, *args)
    return run(nc, [arrays], core_ids=[0]).results[0]["out_0"]
```
